# Optimizing a Trainium2 kernel written in Bass

```python
import numpy as np
import jax
import jax.numpy as jnp

def _softmax(x, axis=-1):
    return jax.nn.softmax(x, axis=axis)

def _gelu(x):
    return jax.nn.gelu(x, approximate=True)

def _silu(x):
    return jax.nn.silu(x)

def _sigmoid(x):
    return jax.nn.sigmoid(x)

def _layernorm(x, axis=-1, eps=1e-05):
    m = jnp.mean(x, axis=axis, keepdims=True)
    v = jnp.var(x, axis=axis, keepdims=True)
    return (x - m) / jnp.sqrt(v + eps)

def _scatter_add(tgt, idx, src, axis=0):
    return tgt.at[idx].add(src)

def _segment_sum(src, seg, n):
    return jax.ops.segment_sum(src, seg, n)
kernel_name = 'mk_decoder_postln_d1_seqx_r8_626175'

def setup_inputs(seed: int=0):
    np.random.seed(seed)
    _w = jnp.asarray

    def _rec_inputs():
        import jax
        import jax.numpy as jnp
        _rk = jax.random.key(seed)
        x = 7.22e-05 + 1 * jax.random.normal(jax.random.fold_in(_rk, 1), (4, 512, 128), jnp.float32)
        _lenS = 512 - jax.random.randint(jax.random.fold_in(_rk, 7), (4,), 0, max(1, 512 // 4) + 1, jnp.int32)
        _lenS2 = 154 - jax.random.randint(jax.random.fold_in(_rk, 8), (4,), 0, max(1, 154 // 4) + 1, jnp.int32)
        _ctx_1024P = jax.random.normal(jax.random.fold_in(_rk, 11), (4, 16, 128), jnp.float32)
        _ctx_1024c = jax.random.dirichlet(jax.random.fold_in(_rk, 511), 0.3 * jnp.ones((16,), jnp.float32), (4, 154))
        _ctx_1024t = jnp.einsum('bsk,bkd->bsd', _ctx_1024c, _ctx_1024P)
        _ctx_1024t = _ctx_1024t * jax.lax.rsqrt(jnp.mean(jnp.square(_ctx_1024t)) + 1e-12) * 0.953939
        ctx_1024 = 4.13588e-05 + 0.999923 * (_ctx_1024t + 0.3 * jax.random.normal(jax.random.fold_in(_rk, 611), (4, 154, 128), jnp.float32))
        return (x, ctx_1024)
    x, ctx_1024 = _rec_inputs()

    def _L0_attn_setup():
        import jax, jax.numpy as jnp
        import numpy as np
        from functools import partial
        B, S, D, H, DK, DV, DFF = (4, 256, 128, 8, 128, 128, 512)
        EPS = 1e-06

        def rms_norm(x):
            return x * jax.lax.rsqrt(jnp.mean(x * x, axis=-1, keepdims=True) + EPS)

        def l2norm(x):
            return x * jax.lax.rsqrt(jnp.sum(x * x, axis=-1, keepdims=True) + EPS)

        def gated_delta_net(h, Wq, Wk, Wv, Wb, Wa, A_log, dt_bias, Wg, o_norm_w, Wo):
            b, s, _ = h.shape
            q = l2norm(jax.nn.silu(h @ Wq).reshape(b, s, H, DK))
            k = l2norm(jax.nn.silu(h @ Wk).reshape(b, s, H, DK))
            v = jax.nn.silu(h @ Wv).reshape(b, s, H, DV)
            beta = jax.nn.sigmoid(h @ Wb)
            g = -jnp.exp(A_log) * jax.nn.softplus(h @ Wa + dt_bias)
            alpha = jnp.exp(g)
            scale = DK ** (-0.5)
            tm = lambda a: jnp.moveaxis(a, 1, 0)
            qs, ks_, vs, als, bts = (tm(q), tm(k), tm(v), tm(alpha), tm(beta))

            def step(Sst, inp):
                q_t, k_t, v_t, a_t, b_t = inp
                Sst = Sst * a_t[..., None, None]
                kv = jnp.einsum('bhd,bhde->bhe', k_t, Sst)
                delta = (v_t - kv) * b_t[..., None]
                Sst = Sst + jnp.einsum('bhd,bhe->bhde', k_t, delta)
                o_t = jnp.einsum('bhd,bhde->bhe', q_t, Sst) * scale
                return (Sst, o_t)
            S0 = jnp.zeros((b, H, DK, DV), dtype=h.dtype)
            _, o = jax.lax.scan(step, S0, (qs, ks_, vs, als, bts))
            o = jnp.moveaxis(o, 0, 1)
            gate = (h @ Wg).reshape(b, s, H, DV)
            o = rms_norm(o) * o_norm_w * jax.nn.silu(gate)
            return o.reshape(b, s, H * DV) @ Wo
        key = jax.random.key(seed)
        ks = jax.random.split(key, 16)
        w = lambda k, shp: jax.random.normal(k, shp, dtype=jnp.float32) * 0.02
        return {'x': jax.random.normal(ks[0], (B, S, D), dtype=jnp.float32), 'Wq': w(ks[1], (D, H * DK)), 'Wk': w(ks[2], (D, H * DK)), 'Wv': w(ks[3], (D, H * DV)), 'Wb': w(ks[4], (D, H)), 'Wa': w(ks[5], (D, H)), 'A_log': jnp.log(jnp.linspace(1.0, 8.0, H).astype(jnp.float32)), 'dt_bias': jax.random.normal(ks[6], (H,), dtype=jnp.float32) * 0.1, 'Wg': w(ks[7], (D, H * DV)), 'o_norm_w': jnp.ones((DV,), dtype=jnp.float32), 'Wo': w(ks[8], (H * DV, D)), 'W_fc': w(ks[9], (D, DFF)), 'W_proj': w(ks[10], (DFF, D))}
    _L0_attn_all = _L0_attn_setup()
    _L0_attn_in = {k: v for k, v in _L0_attn_all.items() if k in ('Wq', 'Wk', 'Wv', 'Wb', 'Wa', 'A_log', 'dt_bias', 'Wg', 'o_norm_w', 'Wo', 'W_fc', 'W_proj')}
    del _L0_attn_all

    def _L0_xattn_setup():
        import jax, jax.numpy as jnp
        import numpy as np
        B, S, E, H, W = (2, 512, 128, 8, 8)

        def build_window_idx(seq_len):
            rows = []
            for t in range(seq_len):
                rp = [i for i in range(-4, 4) if 0 <= t + i < seq_len]
                while len(rp) < 8:
                    if t + len(rp) < seq_len:
                        rp.append(t + len(rp))
                    else:
                        rp.insert(0, t - (8 - len(rp)))
                rows.append([p % seq_len for p in rp])
            return np.asarray(rows, dtype=np.int32)
        key = jax.random.key(seed)
        ks = jax.random.split(key, 7)
        return {'q': jax.random.normal(ks[0], (B, S, E), jnp.float32), 'k': jax.random.normal(ks[1], (B, S, E), jnp.float32), 'v': jax.random.normal(ks[2], (B, S, E), jnp.float32), 'in_proj_w': jax.random.normal(ks[3], (3 * E, E), jnp.float32) * 0.02, 'in_proj_b': jax.random.normal(ks[4], (3 * E,), jnp.float32) * 0.02, 'out_w': jax.random.normal(ks[5], (E, E), jnp.float32) * 0.02, 'out_b': jax.random.normal(ks[6], (E,), jnp.float32) * 0.02}
    _L0_xattn_all = _L0_xattn_setup()
    _L0_xattn_in = {k: v for k, v in _L0_xattn_all.items() if k in ('in_proj_w', 'in_proj_b', 'out_w', 'out_b')}
    del _L0_xattn_all

    def _L0_ffn_setup():
        import math
        import jax, jax.numpy as jnp
        import numpy as np
        D_MODEL = 128
        D_HIDDEN = 512
        N_EXPERTS = 8
        TOP_K = 2
        CAPACITY_FACTOR = 1.25
        key = jax.random.key(seed)
        ks = jax.random.split(key, 8)
        s = 0.02
        x = jax.random.normal(ks[0], (4, 256, D_MODEL), dtype=jnp.float32)
        router_w = jax.random.normal(ks[1], (D_MODEL, N_EXPERTS), dtype=jnp.float32) * s
        router_b = jnp.zeros((N_EXPERTS,), dtype=jnp.float32)
        w1 = jax.random.normal(ks[2], (N_EXPERTS, D_MODEL, D_HIDDEN), dtype=jnp.float32) * s
        b1 = jnp.zeros((N_EXPERTS, D_HIDDEN), dtype=jnp.float32)
        w2 = jax.random.normal(ks[3], (N_EXPERTS, D_HIDDEN, D_MODEL), dtype=jnp.float32) * s
        b2 = jnp.zeros((N_EXPERTS, D_MODEL), dtype=jnp.float32)
        return {'x': x, 'router_w': router_w, 'router_b': router_b, 'w1': w1, 'b1': b1, 'w2': w2, 'b2': b2}
    _L0_ffn_all = _L0_ffn_setup()
    _L0_ffn_in = {k: v for k, v in _L0_ffn_all.items() if k in ('router_w', 'router_b', 'w1', 'b1', 'w2', 'b2')}
    del _L0_ffn_all
    return {'x': x, 'ctx_1024': ctx_1024, 'L0_attn_Wq': _L0_attn_in['Wq'], 'L0_attn_Wk': _L0_attn_in['Wk'], 'L0_attn_Wv': _L0_attn_in['Wv'], 'L0_attn_Wb': _L0_attn_in['Wb'], 'L0_attn_Wa': _L0_attn_in['Wa'], 'L0_attn_A_log': _L0_attn_in['A_log'], 'L0_attn_dt_bias': _L0_attn_in['dt_bias'], 'L0_attn_Wg': _L0_attn_in['Wg'], 'L0_attn_o_norm_w': _L0_attn_in['o_norm_w'], 'L0_attn_Wo': _L0_attn_in['Wo'], 'L0_attn_W_fc': _L0_attn_in['W_fc'], 'L0_attn_W_proj': _L0_attn_in['W_proj'], 'L0_xattn_in_proj_w': _L0_xattn_in['in_proj_w'], 'L0_xattn_in_proj_b': _L0_xattn_in['in_proj_b'], 'L0_xattn_out_w': _L0_xattn_in['out_w'], 'L0_xattn_out_b': _L0_xattn_in['out_b'], 'L0_ffn_router_w': _L0_ffn_in['router_w'], 'L0_ffn_router_b': _L0_ffn_in['router_b'], 'L0_ffn_w1': _L0_ffn_in['w1'], 'L0_ffn_b1': _L0_ffn_in['b1'], 'L0_ffn_w2': _L0_ffn_in['w2'], 'L0_ffn_b2': _L0_ffn_in['b2']}

def reference(x, ctx_1024, L0_attn_Wq, L0_attn_Wk, L0_attn_Wv, L0_attn_Wb, L0_attn_Wa, L0_attn_A_log, L0_attn_dt_bias, L0_attn_Wg, L0_attn_o_norm_w, L0_attn_Wo, L0_attn_W_fc, L0_attn_W_proj, L0_xattn_in_proj_w, L0_xattn_in_proj_b, L0_xattn_out_w, L0_xattn_out_b, L0_ffn_router_w, L0_ffn_router_b, L0_ffn_w1, L0_ffn_b1, L0_ffn_w2, L0_ffn_b2):
    import jax
    import jax.numpy as jnp

    def _L0_attn_ref(x, Wq, Wk, Wv, Wb, Wa, A_log, dt_bias, Wg, o_norm_w, Wo, W_fc, W_proj):
        import jax, jax.numpy as jnp
        import numpy as np
        from functools import partial
        B, S, D, H, DK, DV, DFF = (4, 256, 128, 8, 128, 128, 512)
        EPS = 1e-06

        def rms_norm(x):
            return x * jax.lax.rsqrt(jnp.mean(x * x, axis=-1, keepdims=True) + EPS)

        def l2norm(x):
            return x * jax.lax.rsqrt(jnp.sum(x * x, axis=-1, keepdims=True) + EPS)

        def gated_delta_net(h, Wq, Wk, Wv, Wb, Wa, A_log, dt_bias, Wg, o_norm_w, Wo):
            b, s, _ = h.shape
            q = l2norm(jax.nn.silu(h @ Wq).reshape(b, s, H, DK))
            k = l2norm(jax.nn.silu(h @ Wk).reshape(b, s, H, DK))
            v = jax.nn.silu(h @ Wv).reshape(b, s, H, DV)
            beta = jax.nn.sigmoid(h @ Wb)
            g = -jnp.exp(A_log) * jax.nn.softplus(h @ Wa + dt_bias)
            alpha = jnp.exp(g)
            scale = DK ** (-0.5)
            tm = lambda a: jnp.moveaxis(a, 1, 0)
            qs, ks_, vs, als, bts = (tm(q), tm(k), tm(v), tm(alpha), tm(beta))

            def step(Sst, inp):
                q_t, k_t, v_t, a_t, b_t = inp
                Sst = Sst * a_t[..., None, None]
                kv = jnp.einsum('bhd,bhde->bhe', k_t, Sst)
                delta = (v_t - kv) * b_t[..., None]
                Sst = Sst + jnp.einsum('bhd,bhe->bhde', k_t, delta)
                o_t = jnp.einsum('bhd,bhde->bhe', q_t, Sst) * scale
                return (Sst, o_t)
            S0 = jnp.zeros((b, H, DK, DV), dtype=h.dtype)
            _, o = jax.lax.scan(step, S0, (qs, ks_, vs, als, bts))
            o = jnp.moveaxis(o, 0, 1)
            gate = (h @ Wg).reshape(b, s, H, DV)
            o = rms_norm(o) * o_norm_w * jax.nn.silu(gate)
            return o.reshape(b, s, H * DV) @ Wo
        ln_scale = 1.0
        h = gated_delta_net(ln_scale * rms_norm(x), Wq, Wk, Wv, Wb, Wa, A_log, dt_bias, Wg, o_norm_w, Wo)
        x = x + h
        m = ln_scale * rms_norm(x)
        y = jnp.square(jax.nn.relu(m @ W_fc)) @ W_proj
        return x + y

    def _L0_xattn_ref(q, k, v, in_proj_w, in_proj_b, out_w, out_b):
        import jax, jax.numpy as jnp
        import numpy as np
        B, S, E, H, W = (2, 512, 128, 8, 8)

        def build_window_idx(seq_len):
            rows = []
            for t in range(seq_len):
                rp = [i for i in range(-4, 4) if 0 <= t + i < seq_len]
                while len(rp) < 8:
                    if t + len(rp) < seq_len:
                        rp.append(t + len(rp))
                    else:
                        rp.insert(0, t - (8 - len(rp)))
                rows.append([p % seq_len for p in rp])
            return np.asarray(rows, dtype=np.int32)
        b, s, e = q.shape
        d = e // H
        scale = 1.0 / np.sqrt(d).astype(np.float32)
        idx = jnp.asarray(build_window_idx(s))
        Wq, Wk, Wv = (in_proj_w[:e], in_proj_w[e:2 * e], in_proj_w[2 * e:])
        bq, bk, bv = (in_proj_b[:e], in_proj_b[e:2 * e], in_proj_b[2 * e:])
        kg = k[:, idx]
        vg = v[:, idx]
        qh = (q @ Wq.T + bq).reshape(b, s, H, d)
        kh = (kg @ Wk.T + bk).reshape(b, s, W, H, d)
        vh = (vg @ Wv.T + bv).reshape(b, s, W, H, d)
        scores = jnp.einsum('bshd,bswhd->bshw', qh * scale, kh)
        attn = jax.nn.softmax(scores, axis=-1)
        o = jnp.einsum('bshw,bswhd->bshd', attn, vh).reshape(b, s, e)
        return o @ out_w.T + out_b

    def _L0_ffn_ref(x, router_w, router_b, w1, b1, w2, b2):
        import math
        import jax, jax.numpy as jnp
        import numpy as np
        D_MODEL = 128
        D_HIDDEN = 512
        N_EXPERTS = 8
        TOP_K = 2
        CAPACITY_FACTOR = 1.25
        B, T, D = x.shape
        N = B * T
        E = N_EXPERTS
        capacity = max(1, math.ceil(N / E * CAPACITY_FACTOR))
        x_flat = x.reshape(N, D)
        logits = x_flat.astype(jnp.float32) @ router_w + router_b
        gates = jax.nn.softmax(logits, axis=-1)
        _, topk_idx = jax.lax.top_k(gates, TOP_K)
        expert_mask = jax.nn.one_hot(topk_idx, E, dtype=jnp.int32).sum(1)
        pos = jnp.cumsum(expert_mask, axis=0) - 1
        expert_mask = expert_mask * (pos < capacity)
        valid = expert_mask > 0
        pos_c = jnp.where(valid, pos, capacity)
        e_idx = jnp.broadcast_to(jnp.arange(E), (N, E))
        dispatched = x_flat[:, None, :] * valid[:, :, None].astype(x.dtype)
        buf = jnp.zeros((E, capacity + 1, D), x.dtype).at[e_idx.ravel(), pos_c.ravel()].add(dispatched.reshape(N * E, D))
        buf = buf[:, :capacity]
        h = jax.nn.gelu(jnp.einsum('ecd,edh->ech', buf, w1) + b1[:, None, :], approximate=False)
        out = jnp.einsum('ech,ehd->ecd', h, w2) + b2[:, None, :]
        pos_g = jnp.minimum(pos_c, capacity - 1)
        gathered = out[e_idx, pos_g]
        weights = (gates * valid).astype(x.dtype)
        y = jnp.einsum('ned,ne->nd', gathered, weights)
        return y.reshape(B, T, D)
    x = _layernorm(x + _L0_attn_ref(x, L0_attn_Wq, L0_attn_Wk, L0_attn_Wv, L0_attn_Wb, L0_attn_Wa, L0_attn_A_log, L0_attn_dt_bias, L0_attn_Wg, L0_attn_o_norm_w, L0_attn_Wo, L0_attn_W_fc, L0_attn_W_proj), axis=-1)
    x = _layernorm(x + _L0_xattn_ref(x, ctx_1024, ctx_1024, L0_xattn_in_proj_w, L0_xattn_in_proj_b, L0_xattn_out_w, L0_xattn_out_b), axis=-1)
    x = _layernorm(x + _L0_ffn_ref(x, L0_ffn_router_w, L0_ffn_router_b, L0_ffn_w1, L0_ffn_b1, L0_ffn_w2, L0_ffn_b2), axis=-1)
    return x

_drawn_inputs = setup_inputs


def setup_inputs(seed=0):
    import zlib

    import numpy as np

    out = dict(_drawn_inputs(seed))
    spreads = {'L0_attn_o_norm_w': (1.0, 0.6),
     'L0_ffn_router_b': (0.0, 0.614),
     'L0_ffn_b1': (0.0, 0.8),
     'L0_ffn_b2': (0.0, 0.454)}
    factors = {'L0_attn_Wq': 3.965,
     'L0_attn_Wk': 3.964,
     'L0_attn_Wv': 3.926,
     'L0_attn_Wb': 8.0,
     'L0_attn_Wa': 8.0,
     'L0_attn_A_log': 8.0,
     'L0_attn_dt_bias': 8.0,
     'L0_attn_Wg': 3.922,
     'L0_attn_Wo': 3.889,
     'L0_attn_W_fc': 4.292,
     'L0_attn_W_proj': 3.968,
     'L0_xattn_in_proj_b': 8.0,
     'L0_ffn_router_w': 3.131,
     'L0_ffn_w1': 5.901,
     'L0_ffn_w2': 5.348}
    for name, (base, spread) in spreads.items():
        noise = np.random.default_rng([zlib.crc32(name.encode()), seed]).standard_normal(out[name].shape)
        drawn = base * np.exp(spread * noise) if base else spread * noise
        out[name] = jnp.asarray(drawn.astype(out[name].dtype))
    for name, factor in factors.items():
        out[name] = (out[name] * factor).astype(out[name].dtype)
    return out
```

```python
from contextlib import ExitStack

import numpy as np

import concourse.bass as bass
from concourse import mybir

F32 = mybir.dt.float32
BF16 = mybir.dt.bfloat16
I32 = mybir.dt.int32
U32 = mybir.dt.uint32
ALU = mybir.AluOpType
ACT = mybir.ActivationFunctionType
AX = mybir.AxisListType

P = 128
B, S, D, H = 4, 512, 128, 8
CH = S // P
HG = 4
GR = H // HG
NU = CH * GR
NP = CH * H
BLK = 32
NBLK = P // BLK
DFF = 512
FC = DFF // P
CTX = 154
KEYS = list(range(11)) + [CTX - 1]
NK = len(KEYS)
XH = 8
XD = D // XH
HK = XH * NK
E = 8
CAP = 320
SLOTS = E * CAP
HID = 512
HC = HID // P
NT = B * CH
SLOT_TILES = [(0, 128), (128, 128), (256, 64)]
NEG = -30000.0
G_FLOOR = -200.0
LOG1P_TERMS = 8
PH1, PH1_Z = 20, 3
INV = 2 * (BLK - 1) + 2
POST = 25

C_ID, C_LE, C_GT, C_NEG = 0, P, 2 * P, 3 * P
C_HM = 4 * P
C_IOTA = C_HM + 2 * XH
C_CNT = C_IOTA + E
C_END = C_CNT + CH * HK


def shape_constants():
    t = np.zeros((P, C_END), np.float32)
    r = np.arange(P)
    t[:, C_ID:C_ID + P] = np.eye(P)
    t[:, C_LE:C_LE + P] = r[:, None] <= r[None, :]
    t[:, C_GT:C_GT + P] = r[:, None] > r[None, :]
    t[:, C_NEG:C_NEG + P] = np.where(r[:, None] > r[None, :], NEG, 0.0)
    hm = (r[:, None] // XD) == np.arange(XH)[None, :]
    t[:, C_HM:C_HM + XH] = hm / np.sqrt(XD)
    t[:, C_HM + XH:C_HM + 2 * XH] = hm
    t[:, C_IOTA:C_IOTA + E] = np.arange(E)
    for tok in range(S):
        rows = [i for i in range(-4, 4) if 0 <= tok + i < S]
        while len(rows) < 8:
            if tok + len(rows) < S:
                rows.append(tok + len(rows))
            else:
                rows.insert(0, tok - (8 - len(rows)))
        hit = [min(p % S, CTX - 1) for p in rows]
        count = [hit.count(k) for k in KEYS]
        row = [np.log(n) if n else -1e30 for n in count]
        c = C_CNT + (tok // P) * HK
        t[tok % P, c:c + HK] = row * XH
    return t


def decoder_kernel(nc, x, ctx_in, Wq, Wk, Wv, Wb, Wa, A_log, dt_bias, Wg, o_norm_w, Wo, W_fc, W_proj,
                   in_w, in_b, out_w, out_b, router_w, router_b, w1, b1, w2, b2, table,
                   n_dram, t_dram, tt_dram, x2_dram, slots_dram, moe_dram, out):
    with ExitStack() as ctx:
        def sb(name, shape, dt=F32):
            return ctx.enter_context(nc.sbuf_tensor(name, shape, dt))

        def sem(name):
            return ctx.enter_context(nc.semaphore(name))

        const = sb("const", [P, C_END])
        ident, le, gt = const[:, C_ID:C_ID + P], const[:, C_LE:C_LE + P], const[:, C_GT:C_GT + P]
        iota8 = const[:, C_IOTA:C_IOTA + E]
        ident_h, neg_h = sb("ident_h", [P, P], BF16), sb("neg_h", [P, P], BF16)
        ones = sb("ones", [P, P])
        zeros = sb("zeros", [P, 512])
        mhalf = sb("mhalf", [P, 16])
        w_qkvg = sb("w_qkvg", [P, 4, H * P])
        w_ba = sb("w_ba", [P, 2 * H])
        dtb = sb("dtb", [P, H])
        neg_a = sb("neg_a", [P, H])
        w_o = sb("w_o", [P, H, P])
        onw = sb("onw", [P, 1])
        w_fc = sb("w_fc", [P, DFF])
        w_pr = sb("w_pr", [P, FC, P])
        outb = sb("outb", [1, P])
        w_r = sb("w_r", [P, E])
        rb = sb("rb", [1, E])
        xattn_m = sb("xattn_m", [P, B * HK])
        xattn_b = sb("xattn_b", [1, B * HK])
        xattn_vo = sb("xattn_vo", [HK, B * P])

        xin = sb("xin", [P, CH, P])
        xres = sb("xres", [P, CH, P])
        hT = sb("hT", [P, CH * P])
        x1 = sb("x1", [P, CH, P])
        xx = sb("xx", [P, CH, P])
        kn = sb("kn", [P, NU, HG * P])
        kT = sb("kT", [P, NU, HG * P])
        att = sb("att", [P, NU, HG * P])
        Nm = sb("Nm", [P, NP, P])
        Tm = sb("Tm", [P, NP, 2 * BLK])
        TT = sb("TT", [P, NP, P])
        qT = sb("qT", [P, NU, HG * P])
        vv = sb("vv", [P, NU, HG * P])
        St = sb("St", [P, GR, HG * P])
        gates = sb("gates", [P, 16, NP])
        eg = sb("eg", [P, 3, NP])
        neg_eg = sb("neg_eg", [P, NP])
        ekb = sb("ekb", [P, NP])
        beta = sb("beta", [P, NP])
        g_all = sb("g_all", [P, NP])
        kss = sb("kss", [P, NP])
        rk = sb("rk", [P, NP])
        cq = sb("cq", [P, NP])
        oss = sb("oss", [P, NP])
        of = sb("of", [P, NP])
        st4 = sb("st4", [P, 8, CH])
        bn = sb("bn", [P, CH, 6])
        mv = sb("mv", [P, CH, 2])
        blk_t = sb("blk_t", [P, BLK, BLK])
        prod = sb("prod", [P, 17 * 16])
        p_lo = sb("p_lo", [P, NP, BLK])
        work = sb("work", [P, 3, 2, HG * P])
        gate_sb = sb("gate_sb", [P, 2, HG * P])
        k_raw = work[:, 0]
        gm = work[:, 1]
        qsq = work[:, 2]
        u_sb = work[:, 0]
        o_sb = work[:, 1]
        ogT = work[:, 2]
        h_sb = work[:, 1, 0]
        blk_n = St[:, :, :].rearrange("p a b -> p (a b)").rearrange("p (i j) -> p i j", i=BLK)
        blk_tt = gate_sb[:, :, :].rearrange("p a b -> p (a b)").rearrange("p (i j) -> p i j", i=BLK)
        fT = work[:, 0:2].rearrange("p a b n -> p (a b) n")
        mT = work[:, 2, 0]
        a1 = sb("a1", [P, CH, P])
        aT = work[:, 2, 1]
        soft = work[:, 0, 0]
        pT = work[:, 0, 1]
        m_sb = work[:, 1, 0].rearrange("p (c n) -> p c n", c=CH)
        x2 = work[:, 1, 1].rearrange("p (c n) -> p c n", c=CH)
        x2T = work[:, 2, 0]
        rt = sb("rt", [P, 14, CH * E])
        top8 = sb("top8", [P, CH, 8])
        top8i = sb("top8i", [P, CH, 8], U32)
        base = sb("base", [P, E])
        scat_i = sb("scat_i", [P, 2, CH], I32)
        slot_all = sb("slot_all", [P, NT // CH, 2 * CH], I32)
        wgt_all = sb("wgt_all", [P, NT // CH, 2 * CH])
        moe_w1 = kn[:, 0:2]
        moe_w2 = kn[:, 2:4].rearrange("p a (c n) -> p a c n", c=HC)
        moe_b1 = sb("moe_b1", [P, 2, HC])
        moe_b2 = sb("moe_b2", [1, 2, P])
        xe = kT[:, 0:2]
        xeT = kT[:, 2:4]
        hidT = att[:, 0:8].rearrange("p (a c) n -> p a c n", a=2)
        oe = kT[:, 4:6]
        rows = qT[:, 0:8].rearrange("p a (c n) -> p a c n", c=CH)
        x2f = vv[:, 0:2].rearrange("p a (c n) -> p a c n", c=CH)
        yf = vv[:, 2:4].rearrange("p a (c n) -> p a c n", c=CH)
        slot_s = sb("slot_s", [P, 2, 2 * CH], I32)
        wgt_s = sb("wgt_s", [P, 2, 2 * CH])
        ctx48 = vv[0:B * NK, 0, 0:P]
        bias_rows = vv[0:E * HC + 3, 1, 0:P]
        inw = vv[:, 2, 0:3 * P].rearrange("p (s d) -> p s d", s=3)
        outw = vv[:, 3, 0:P]
        bias_T = sb("bias_T", [P, E * HC + 3])
        b1T, inb = bias_T[:, 0:E * HC], bias_T[:, E * HC:]

        ps = [ctx.enter_context(nc.psum_tensor(f"ps{i}", [P, 512], F32)) for i in range(8)]

        names = """ld_const ld_wk ld_w1 ld_x ld_misc ld_xattn zeroed consts_ok setup_tr setup_cp setup_kv setup_blk setup_m setup_done
        base_ok x_kept h_ready hT_ps hT_ok gates_ps g_ready u_exp eg_ps eg_ok egs_ok o_step k_ps k_act k_sq rk_ok kn_ok kT_ps kT_ok
        gm_ok e_ps dt_exp dt_ok kk_ps n_ok n_stored n_back t_ok t_stored tt_back q_ps q_ok q_sq sq_ps cq_ok v_ps v_ok qk_ps at_ok
        kd_ok l1_ps l1_ok l2_ps l2_ok l3_ps l3_ok l4_ps l4_ok ks_ps r_ok tr_ps u_ok qs_ps qc_ok au_ps o_ok f_ok og_ok ogT_ps ogT_ok
        g_ps gate_ok ktu_ps s_ok hp_ps x1_ok xx_ok ssx_ok r1_ok m_ok mT_ps mT_ok fc_ps fr_ok f2_ok y_ps z_ok v1_ok rs1_ok a_ok aT_ps
        aT_ok sc_ps sm_ok sexp_ok p_ok pT_ps pT_ok xo_ps v2_ok rs2_ok x2_ok x2_st x2T_ps x2T_ok lg_ps lsub_ok lexp_ok mask_ok
        cum_ps slots_ok scattered ssh_ok rh_ok
        e_w_ld0 e_w_ld1 e_x_ld0 e_x_ld1 e_b_ok e_xT_ps e_xT_ok e_h_ps e_h_ok e_o_ps e_o_ok e_o_st
        f_idx f_rows0 f_rows1 f_x2_0 f_x2_1 f_v f_rs f_y f_out0 f_out1""".split()
        sm = {n: sem(n) for n in names}
        dchain, pchain = {}, {}
        for ph in ("set", "ph1", "inv", "post", "fin"):
            dchain[ph] = sem(f"dve_step_{ph}")

        class Steps:
            def __init__(self, eng, s, b, per):
                self.eng, self.s, self.b, self.per, self.k = eng, s, b, per, 0

            def then(self, ins, plain=False):
                self.k += 1
                ins.then_inc(self.s, 1)
                if plain:
                    wait_apart(self.eng, self.s, self.b * self.per + self.k)
                else:
                    self.eng.wait_ge(self.s, self.b * self.per + self.k)

            def close(self):
                assert self.k == self.per, (self.k, self.per)

        def after(name, b, per, k):
            return sm[name], b * per + k + 1

        def wait_apart(eng, s, value):
            if not isinstance(value, int):
                value = eng.to_reg(value)
                eng.wait_ge(sm["ld_const"], 16)
            eng.wait_ge(s, value)

        def bc(ap, shape):
            return ap.to_broadcast(shape)

        def heads(ap):
            return ap.rearrange("p (h n) -> p h n", h=HG)

        block = ctx.enter_context(nc.Block())

        @block.sync
        def _(sp):
            sp.dma_start(const[:], table).then_inc(sm["ld_const"], 16)
            sp.dma_start(xin[:], x[0].rearrange("(c p) d -> p c d", p=P)).then_inc(sm["ld_x"], 16)
            sp.dma_start(w_ba[:, 0:H], Wb).then_inc(sm["ld_misc"], 16)
            sp.dma_start(w_ba[:, H:2 * H], Wa).then_inc(sm["ld_misc"], 16)
            sp.dma_start(dtb[:], dt_bias.partition_broadcast(P)).then_inc(sm["ld_misc"], 16)
            sp.dma_start(neg_a[:], A_log.partition_broadcast(P)).then_inc(sm["ld_misc"], 16)
            sp.dma_start(w_qkvg[:, 1, :], Wk).then_inc(sm["ld_wk"], 16)
            for i, w in ((0, Wq), (2, Wv), (3, Wg)):
                sp.dma_start(w_qkvg[:, i, :], w).then_inc(sm["ld_w1"], 16)
            sp.dma_start(w_o[:], Wo.rearrange("(h p) n -> p h n", p=P)).then_inc(sm["ld_w1"], 16)
            sp.dma_start(onw[:], o_norm_w.rearrange("(p o) -> p o", o=1)).then_inc(sm["ld_w1"], 16)
            sp.dma_start(w_fc[:], W_fc).then_inc(sm["ld_w1"], 16)
            sp.dma_start(w_pr[:], W_proj.rearrange("(f p) n -> p f n", p=P)).then_inc(sm["ld_w1"], 16)
            sp.wait_ge(sm["zeroed"], 1)
            zrows = slots_dram.rearrange("(k p r) d -> k p (r d)", p=P, r=4)
            for k in range(SLOTS // (4 * P)):
                sp.dma_start(zrows[k], zeros[:]).then_inc(sm["e_w_ld0"], 16)

            def exchange(b):
                sp.wait_ge(*after("n_ok", b, NU, NU - 1))
                for r in range(NBLK):
                    sp.dma_start(n_dram[:, r].rearrange("q i j -> i q j"),
                                 Nm[BLK * r:BLK * r + BLK, :, BLK * r:BLK * r + BLK]).then_inc(sm["n_stored"], 16)
                sp.wait_ge(sm["n_stored"], b * 64 + 64)
                sp.dma_start(blk_n, n_dram.rearrange("q r i j -> (q r) i j")).then_inc(sm["n_back"], 16)
                sp.wait_ge(*after("t_ok", b, 1, 0))
                sp.dma_start(t_dram.rearrange("q r i j -> (q r) i j"), blk_t[:]).then_inc(sm["t_stored"], 16)
                sp.dma_start(tt_dram.rearrange("q r i j -> (q r) i j"), blk_tt).then_inc(sm["t_stored"], 16)
                sp.wait_ge(sm["t_stored"], b * 32 + 32)
                if isinstance(b, int):
                    sp.wait_ge(sm["zeroed"], 3)
                for r in range(NBLK):
                    sp.dma_start(Tm[BLK * r:BLK * r + BLK, :, BLK * (r % 2):BLK * (r % 2) + BLK],
                                 t_dram[:, r].rearrange("q i j -> i q j")).then_inc(sm["tt_back"], 16)
                    sp.dma_start(TT[BLK * r:BLK * r + BLK, :, BLK * r:BLK * r + BLK],
                                 tt_dram[:, r].rearrange("q i j -> i q j")).then_inc(sm["tt_back"], 16)

            def next_x(b):
                sp.wait_ge(sm["x_kept"], b)
                sp.wait_ge(sm["h_ready"], b)
                sp.dma_start(xin[:], x[b].rearrange("(c p) d -> p c d", p=P)).then_inc(sm["ld_x"], 16)

            def store_x2(b):
                sp.wait_ge(*after("x2_ok", b, CH, CH - 1))
                sp.dma_start(x2_dram[b].rearrange("(c p) d -> p c d", p=P), x2).then_inc(sm["x2_st"], 16)

            exchange(0)
            with sp.Fori(1, B) as b:
                next_x(b)
                exchange(b)
                store_x2(b - 1)
            store_x2(B - 1)

            def load_weights(ep, a, first):
                e = ep * 2 + a
                if not first:
                    sp.wait_ge(sm["e_o_ps"], ep * 2 + a - 1)
                s = sm[f"e_w_ld{a}"]
                sp.dma_start(moe_w1[:, a], w1[e]).then_inc(s, 16)
                sp.dma_start(moe_w2[:, a], w2[e].rearrange("(c p) n -> p c n", p=P)).then_inc(s, 16)
                sp.dma_start(moe_b2[:, a], b2[bass.ds(e, 1)]).then_inc(s, 16)

            def load_rows(ep, a):
                e = ep * 2 + a
                s = sm[f"e_x_ld{a}"]
                for i, (r0, n) in enumerate(SLOT_TILES):
                    sp.dma_start(xe[0:n, a, i * P:(i + 1) * P], slots_dram[bass.ds(e * CAP + r0, n)]).then_inc(s, 16)

            def store_rows(ep, a):
                e = ep * 2 + a
                sp.wait_ge(sm["e_o_ok"], e + 1)
                for i, (r0, n) in enumerate(SLOT_TILES):
                    sp.dma_start(moe_dram[bass.ds(e * CAP + r0, n)], oe[0:n, a, i * P:(i + 1) * P]).then_inc(sm["e_o_st"], 16)

            sp.wait_ge(sm["s_ok"], B * (NU - 2))
            sp.wait_ge(sm["o_ok"], B * NU)
            sp.wait_ge(sm["hp_ps"], B * NU)
            for a in range(2):
                load_weights(0, a, True)
            sp.wait_ge(sm["scattered"], B * 2 * CH * 16)
            for a in range(2):
                load_rows(0, a)
            for a in range(2):
                store_rows(0, a)
            with sp.Fori(1, E // 2) as ep:
                for a in range(2):
                    load_weights(ep, a, False)
                    sp.wait_ge(sm["e_xT_ps"], ep * 2 + a - 1)
                    load_rows(ep, a)
                for a in range(2):
                    store_rows(ep, a)
            sp.wait_ge(sm["x2_st"], B * 16)
            for i in range(B):
                a = i % 2
                if i >= 2:
                    sp.wait_ge(sm["f_y"], i - 1)
                sp.dma_start(x2f[:, a], x2_dram[i].rearrange("(c p) d -> p c d", p=P)).then_inc(sm[f"f_x2_{a}"], 16)
                if i >= 1:
                    sp.wait_ge(sm["f_y"], i)
                    sp.dma_start(out[i - 1].rearrange("(c p) d -> p c d", p=P), yf[:, (i - 1) % 2]).then_inc(sm[f"f_out{(i - 1) % 2}"], 16)
            sp.wait_ge(sm["f_y"], B)
            sp.dma_start(out[B - 1].rearrange("(c p) d -> p c d", p=P), yf[:, (B - 1) % 2]).then_inc(sm[f"f_out{(B - 1) % 2}"], 16)
            sp.wait_ge(sm["f_out0"], B * 8)
            sp.wait_ge(sm["f_out1"], B * 8)

        @block.gpsimd
        def _(pool):
            pool.memset(ones[:], 1.0).then_inc(sm["consts_ok"], 1)
            pool.memset(mhalf[:], -0.5).then_inc(sm["consts_ok"], 1)
            pool.memset(zeros[:], 0.0).then_inc(sm["zeroed"], 1)
            pool.memset(Tm[:], 0.0).then_inc(sm["zeroed"], 1)
            pool.memset(TT[:], 0.0).then_inc(sm["zeroed"], 1)
            pool.memset(base[:], 0.0).then_inc(sm["base_ok"], 1)

            def power(out_ap, in_ap, done, n):
                pool.tensor_tensor(out_ap, in_ap, mhalf[:, 0:n], ALU.pow).then_inc(done, 1)

            def phase1(b):
                wait_apart(pool, sm["ld_x"], b * 16 + 16)
                if not isinstance(b, int) or b > 0:
                    pool.wait_ge(sm["xx_ok"], b)
                    pool.wait_ge(sm["x1_ok"], b)
                pool.tensor_copy(xres[:], xin[:]).then_inc(sm["x_kept"], 1)
                pool.wait_ge(sm["ssh_ok"], b + 1)
                power(st4[:, 1], st4[:, 0], sm["rh_ok"], CH)
                for n in range(NU):
                    pool.wait_ge(*after("k_sq", b, NU, n))
                    power(rk[:, n * HG:(n + 1) * HG], kss[:, n * HG:(n + 1) * HG], sm["rk_ok"], HG)
                pool.wait_ge(sm["g_ready"], b + 1)
                for n in range(NU):
                    if n >= 2:
                        pool.wait_ge(*after("e_ps", b, NU, n - 2))
                    pool.tensor_tensor(heads(gm[:, n % 2]), bc(gt.unsqueeze(1), [P, HG, P]),
                                       bc(g_all[:, n * HG:(n + 1) * HG].unsqueeze(2), [P, HG, P]),
                                       ALU.mult).then_inc(sm["gm_ok"], 1)
                    if n >= 1:
                        beta_mult(b, n - 1)
                beta_mult(b, NU - 1)
                pool.wait_ge(*after("egs_ok", b, 3, 2))
                pool.wait_ge(*after("kT_ps", b, NU, NU - 1))
                for n in range(NU - GR):
                    pool.tensor_tensor(heads(kn[:, n]), heads(kn[:, n]),
                                       bc(ekb[:, n * HG:(n + 1) * HG].unsqueeze(2), [P, HG, P]),
                                       ALU.mult).then_inc(sm["kd_ok"], 1)
                for n in range(NU):
                    pool.wait_ge(*after("q_ok", b, NU, n))
                    if n >= 2:
                        pool.wait_ge(*after("sq_ps", b, NU, n - 2))
                    pool.tensor_tensor(qsq[:, n % 2], qT[:, n], qT[:, n], ALU.mult).then_inc(sm["q_sq"], 1)

            def beta_mult(b, n):
                if n == 0:
                    pool.wait_ge(*after("egs_ok", b, 3, 0))
                pool.wait_ge(*after("dt_exp", b, NU, n))
                pool.tensor_tensor(heads(att[:, n]), heads(att[:, n]),
                                   bc(beta[:, n * HG:(n + 1) * HG].unsqueeze(2), [P, HG, P]),
                                   ALU.mult).then_inc(sm["dt_ok"], 1)

            def phase2b(b):
                for n in range(NU):
                    pool.wait_ge(*after("o_ok", b, NU, n))
                    power(of[:, n * HG:(n + 1) * HG], oss[:, n * HG:(n + 1) * HG], sm["f_ok"], HG)
                pool.wait_ge(sm["x1_ok"], b + 1)
                pool.tensor_tensor(xx[:], xres[:], x1[:], ALU.add).then_inc(sm["xx_ok"], 1)

            def post(b):
                pool.wait_ge(sm["ssx_ok"], b + 1)
                power(st4[:, 3], st4[:, 2], sm["r1_ok"], CH)
                pool.wait_ge(sm["v1_ok"], b + 1)
                power(st4[:, 5], st4[:, 4], sm["rs1_ok"], CH)
                pool.wait_ge(sm["v2_ok"], b + 1)
                power(st4[:, 7], st4[:, 6], sm["rs2_ok"], CH)
                wait_apart(pool, sm["slots_ok"], b + 1)
                for k in range(2):
                    for c in range(CH):
                        pool.indirect_dma_start(
                            slots_dram, bass.IndirectOffsetOnAxis(ap=scat_i[:, k, c:c + 1], axis=0),
                            x2[:, c, :], None, bounds_check=SLOTS - 1, oob_is_err=False,
                        ).then_inc(sm["scattered"], 16)

            phase1(0)
            phase2b(0)
            with pool.Fori(1, B) as b:
                phase1(b)
                pool.wait_ge(sm["e_w_ld0"], 16 * (SLOTS // (4 * P)))
                post(b - 1)
                phase2b(b)
            post(B - 1)

            pool.wait_ge(sm["e_o_st"], E * len(SLOT_TILES) * 16)
            def gather(i):
                a = i % 2
                if i >= 2:
                    pool.wait_ge(sm["f_y"], i - 1)
                for j in range(2 * CH):
                    pool.indirect_dma_start(
                        rows[:, a * 2 + j // CH, j % CH, :], None, moe_dram,
                        bass.IndirectOffsetOnAxis(ap=slot_all[:, i, j:j + 1], axis=0),
                    ).then_inc(sm[f"f_rows{a}"], 16)

            gather(0)
            gather(1)
            for i in range(B):
                pool.wait_ge(sm["f_v"], i + 1)
                power(st4[:, 1], st4[:, 0], sm["f_rs"], CH)
                if i + 2 < B:
                    gather(i + 2)

        @block.tensor
        def _(pe):
            mm = nc.tensor.matmul

            def transpose(out_ap, in_ap, n=P):
                return nc.tensor.transpose(out_ap, in_ap, ident[0:n, 0:n])

            def setup():
                pe.wait_ge(sm["ld_const"], 16)
                pe.wait_ge(sm["ld_xattn"], 16 * (B * 2 + 7))
                transpose(ps[4][:, 0:B * NK], ctx48, B * NK)
                transpose(ps[3][:, 0:E * HC + 3], bias_rows, E * HC + 3)
                transpose(ps[5][:, 0:P], inw[:, 1, :])
                transpose(ps[6][:, 0:P], inw[:, 2, :])
                transpose(ps[7][:, 0:P], outw).then_inc(sm["setup_tr"], 1)
                pe.wait_ge(sm["setup_cp"], 5)
                ctxT, wkT, wvT, woT = (kT[:, i, 0:P] for i in range(4))
                mm(ps[4][:, 0:B * NK], wkT, ctxT[:, 0:B * NK], start=True, stop=True)
                mm(ps[5][:, 0:B * NK], wvT, ctxT[:, 0:B * NK], start=True, stop=True).then_inc(sm["setup_kv"], 1)
                pe.wait_ge(sm["setup_blk"], 2 * B)
                kblk, vblk = kT[:, 4, 0:B * HK], kT[:, 5, 0:B * HK]
                mm(ps[6][:, 0:B * HK], inw[:, 0, :], kblk, start=True, stop=True)
                mm(ps[7][0:1, 0:B * HK], inb[:, 0:1], kblk, start=True, stop=True)
                for b in range(B):
                    last = mm(ps[4][0:HK, b * P:(b + 1) * P], vblk[:, b * HK:(b + 1) * HK], woT, start=True, stop=True)
                last.then_inc(sm["setup_m"], 1)

            def k_proj(b, n):
                c, g = n // GR, n % GR
                if n >= 2:
                    pe.wait_ge(*after("k_act", b, NU, n - 2))
                mm(ps[2 + n % 2][:], hT[:, c * P:(c + 1) * P], w_qkvg[:, 1, g * 512:(g + 1) * 512],
                   start=True, stop=True).then_inc(sm["k_ps"], 1)

            def k_transpose(b, n):
                pe.wait_ge(*after("kn_ok", b, NU, n))
                if n >= 2:
                    pe.wait_ge(*after("kT_ok", b, NU, n - 2))
                for h in range(HG):
                    last = transpose(ps[4 + n % 2][:, h * P:(h + 1) * P], kn[:, n, h * P:(h + 1) * P])
                last.then_inc(sm["kT_ps"], 1)

            def phase1(b):
                first = isinstance(b, int) and b == 0
                if first:
                    pe.wait_ge(sm["ld_const"], 16)
                else:
                    pe.wait_ge(sm["x1_ok"], b)
                pe.wait_ge(sm["h_ready"], b + 1)
                for c in range(CH):
                    last = transpose(ps[0][:, c * P:(c + 1) * P], h_sb[:, c * P:(c + 1) * P])
                last.then_inc(sm["hT_ps"], 1)
                pe.wait_ge(sm["hT_ok"], b + 1)
                if first:
                    pe.wait_ge(sm["ld_misc"], 64)
                for c in range(CH):
                    last = mm(ps[1][:, c * 16:(c + 1) * 16], hT[:, c * P:(c + 1) * P], w_ba[:], start=True, stop=True)
                last.then_inc(sm["gates_ps"], 1)
                if first:
                    pe.wait_ge(sm["ld_wk"], 16)
                for n in range(NU + 2):
                    if n < NU:
                        k_proj(b, n)
                    if n >= 2:
                        k_transpose(b, n - 2)
                pe.wait_ge(sm["g_ready"], b + 1)
                if first:
                    pe.wait_ge(sm["consts_ok"], 4)
                for i, tri in enumerate((le, ones[:], gt)):
                    last = mm(ps[1][:, 64 + i * NP:64 + (i + 1) * NP], tri, g_all[:], start=True, stop=True)
                last.then_inc(sm["eg_ps"], 1)
                for n in range(NU + 1):
                    if n < NU:
                        e = ps[6 + n % 2]
                        if n >= 2:
                            pe.wait_ge(*after("dt_exp", b, NU, n - 2))
                        pe.wait_ge(*after("gm_ok", b, NU, n))
                        for h in range(HG):
                            mm(e[:, h * P:(h + 1) * P], ident_h[:], neg_h[:], start=True, stop=False, skip_group_check=True)
                            last = mm(e[:, h * P:(h + 1) * P], gm[:, n % 2, h * P:(h + 1) * P], le,
                                      start=False, stop=True, skip_group_check=True)
                        last.then_inc(sm["e_ps"], 1)
                    if n >= 1:
                        kk_gram(b, n - 1)

            def kk_gram(b, n):
                pe.wait_ge(*after("kT_ok", b, NU, n))
                if n >= 2:
                    pe.wait_ge(*after("n_ok", b, NU, n - 2))
                if n == 1:
                    pe.wait_ge(sm["eg_ok"], b + 1)
                for h in range(HG):
                    kh = kT[:, n, h * P:(h + 1) * P]
                    last = mm(ps[n % 2][:, h * P:(h + 1) * P], kh, kh, start=True, stop=True)
                last.then_inc(sm["kk_ps"], 1)

            def phase2a(b):
                if isinstance(b, int) and b == 0:
                    pe.wait_ge(sm["ld_w1"], 16 * 7)
                pe.wait_ge(*after("k_act", b, NU, NU - 1))
                pe.wait_ge(*after("n_ok", b, NU, NU - 1))
                for n in range(NU + 1):
                    if n < NU:
                        c, g = n // GR, n % GR
                        if n >= 1:
                            pe.wait_ge(*after("q_ok", b, NU, n - 1))
                        for h in range(HG):
                            hh = (g * HG + h) * P
                            last = mm(ps[2][:, h * P:(h + 1) * P], w_qkvg[:, 0, hh:hh + P], hT[:, c * P:(c + 1) * P],
                                      start=True, stop=True)
                        last.then_inc(sm["q_ps"], 1)
                        if n >= 1:
                            pe.wait_ge(*after("v_ok", b, NU, n - 1))
                        mm(ps[3][:], hT[:, c * P:(c + 1) * P], w_qkvg[:, 2, g * 512:(g + 1) * 512],
                           start=True, stop=True).then_inc(sm["v_ps"], 1)
                    if n >= 1:
                        m = n - 1
                        pe.wait_ge(*after("q_ok", b, NU, m))
                        if m >= 2:
                            pe.wait_ge(*after("at_ok", b, NU, m - 2))
                        elif m == 0:
                            pe.wait_ge(*after("kT_ok", b, NU, NU - 1))
                        for h in range(HG):
                            last = mm(ps[4 + m % 2][:, h * P:(h + 1) * P], kT[:, m, h * P:(h + 1) * P],
                                      qT[:, m, h * P:(h + 1) * P], start=True, stop=True)
                        last.then_inc(sm["qk_ps"], 1)
                        pe.wait_ge(*after("q_sq", b, NU, m))
                        for h in range(HG):
                            last = mm(ps[1][:, m * HG + h:m * HG + h + 1], qsq[:, m % 2, h * P:(h + 1) * P],
                                      ones[:, 0:1], start=True, stop=True)
                        last.then_inc(sm["sq_ps"], 1)

            def t_levels(b):
                wait_apart(pe, sm["tt_back"], b * 128 + 128)
                pe.wait_ge(*after("v_ok", b, NU, NU - 1))
                pe.wait_ge(*after("at_ok", b, NU, NU - 1))
                if not isinstance(b, int) or b > 0:
                    pe.wait_ge(sm["slots_ok"], b)
                pe.wait_ge(sm["cq_ok"], b + 1)
                pe.wait_ge(*after("dt_exp", b, NU, NU - 1))
                for half in range(2):
                    for q in range(16 * half, 16 * half + 16):
                        col = (q % 16) * BLK
                        for lo in (0, 64):
                            hi = lo + BLK
                            last = mm(ps[2 + half][hi:hi + BLK, col:col + BLK], Nm[lo:lo + BLK, q, hi:hi + BLK],
                                      Tm[lo:lo + BLK, q, 0:BLK], start=True, stop=True, skip_group_check=True)
                    last.then_inc(sm["l1_ps"], 1)
                for half in range(2):
                    wait_apart(pe, *after("l1_ok", b, 4, 2 * half + 1))
                    for q in range(16 * half, 16 * half + 16):
                        col = (q % 16) * BLK
                        mm(ps[4 + half][BLK:2 * BLK, col:col + BLK], TT[BLK:2 * BLK, q, BLK:2 * BLK],
                           p_lo[BLK:2 * BLK, q, :], start=True, stop=True, skip_group_check=True)
                        for lo in (0, 64):
                            hi = lo + BLK
                            last = mm(ps[6 + half][lo:lo + BLK, col:col + BLK], p_lo[hi:hi + BLK, q, :],
                                      TT[hi:hi + BLK, q, hi:hi + BLK], start=True, stop=True, skip_group_check=True)
                    last.then_inc(sm["l2_ps"], 1)
                banks = [2, 3, 4, 5]
                wait_apart(pe, *after("l2_ok", b, 6, 5))
                for i in range(4):
                    for q in range(8 * i, 8 * i + 8):
                        col = (q % 8) * 64
                        last = mm(ps[banks[i]][64:P, col:col + 64], Nm[0:64, q, 64:P], Tm[0:64, q, :],
                                  start=True, stop=True, skip_group_check=True)
                    last.then_inc(sm["l3_ps"], 1)
                for i in range(4):
                    wait_apart(pe, *after("l3_ok", b, 4, i))
                    p64 = p_lo[64:P].rearrange("p q n -> p (q n)").rearrange("p (q n) -> p q n", n=64)
                    if i >= 2:
                        wait_apart(pe, *after("l4_ok", b, 4, i - 2))
                    for q in range(8 * i, 8 * i + 8):
                        col = (q % 8) * 64
                        last = mm(ps[6 + i % 2][0:64, col:col + 64], p64[:, q % 16, :], TT[64:P, q, 64:P],
                                  start=True, stop=True, skip_group_check=True)
                    last.then_inc(sm["l4_ps"], 1)

            def ks(b, n):
                g = n % GR
                if n == 2:
                    pe.wait_ge(*after("l3_ok", b, 4, 3))
                if n >= 4:
                    pe.wait_ge(*after("r_ok", b, NU - 2, n - 4))
                pe.wait_ge(*after("s_ok", b, NU - 2, n - 2))
                for h in range(HG):
                    last = mm(ps[1 + n % 2][:, h * P:(h + 1) * P], kT[:, n, h * P:(h + 1) * P],
                              St[:, g, h * P:(h + 1) * P], start=True, stop=True)
                last.then_inc(sm["ks_ps"], 1)

            def phase2b(b):
                pe.wait_ge(*after("l4_ok", b, 4, 3))
                if not isinstance(b, int) or b > 0:
                    pe.wait_ge(sm["xx_ok"], b)
                for n in range(NU + 1):
                    c, g = n // GR, n % GR
                    if n < NU:
                        if GR <= n + 1 < NU:
                            ks(b, n + 1)
                        if n >= 2:
                            pe.wait_ge(*after("r_ok", b, NU - 2, n - 2))
                        if n >= 1:
                            pe.wait_ge(*after("u_ok", b, NU, n - 1))
                        for h in range(HG):
                            last = mm(ps[3][:, h * P:(h + 1) * P], TT[:, c * H + g * HG + h, :],
                                      vv[:, n, h * P:(h + 1) * P], start=True, stop=True)
                        last.then_inc(sm["tr_ps"], 1)
                        if n >= 1:
                            pe.wait_ge(*after("o_ok", b, NU, n - 1))
                        if c > 0:
                            for h in range(HG):
                                last = mm(ps[4][:, h * P:(h + 1) * P], qT[:, n, h * P:(h + 1) * P],
                                          St[:, g, h * P:(h + 1) * P], start=True, stop=True)
                            last.then_inc(sm["qs_ps"], 1)
                        if n >= 1:
                            if n >= 2:
                                pe.wait_ge(*after("ogT_ok", b, NU, n - 2))
                            pe.wait_ge(*after("og_ok", b, NU, n - 1))
                            for h in range(HG):
                                last = transpose(ps[7][:, h * P:(h + 1) * P], o_sb[:, (n - 1) % 2, h * P:(h + 1) * P])
                            last.then_inc(sm["ogT_ps"], 1)
                        pe.wait_ge(*after("u_ok", b, NU, n))
                        for h in range(HG):
                            last = mm(ps[5][:, h * P:(h + 1) * P], att[:, n, h * P:(h + 1) * P],
                                      u_sb[:, n % 2, h * P:(h + 1) * P], start=True, stop=True)
                        last.then_inc(sm["au_ps"], 1)
                        if 1 <= n <= NU - 2:
                            pe.wait_ge(*after("s_ok", b, NU - 2, n - 1))
                        elif n == NU - 1:
                            pe.wait_ge(*after("gate_ok", b, NU, n - 1))
                        mm(ps[6][:], hT[:, c * P:(c + 1) * P], w_qkvg[:, 3, g * 512:(g + 1) * 512],
                           start=True, stop=True).then_inc(sm["g_ps"], 1)
                        if n < NU - 2:
                            pe.wait_ge(*after("gate_ok", b, NU, n))
                            pe.wait_ge(*after("kd_ok", b, NU - 2, n))
                            for h in range(HG):
                                last = mm(ps[6][:, h * P:(h + 1) * P], kn[:, n, h * P:(h + 1) * P],
                                          u_sb[:, n % 2, h * P:(h + 1) * P], start=True, stop=True)
                            last.then_inc(sm["ktu_ps"], 1)
                    else:
                        pe.wait_ge(*after("ogT_ok", b, NU, n - 2))
                        pe.wait_ge(*after("og_ok", b, NU, n - 1))
                        for h in range(HG):
                            last = transpose(ps[7][:, h * P:(h + 1) * P], o_sb[:, (n - 1) % 2, h * P:(h + 1) * P])
                        last.then_inc(sm["ogT_ps"], 1)
                    if n >= 1:
                        m = n - 1
                        pe.wait_ge(*after("ogT_ok", b, NU, m))
                        cm, gmm = m // GR, m % GR
                        for h in range(HG):
                            hh = gmm * HG + h
                            last = mm(ps[0][:, cm * P:(cm + 1) * P], ogT[:, m % 2, h * P:(h + 1) * P], w_o[:, hh, :],
                                      start=(hh == 0), stop=(hh == H - 1), skip_group_check=True)
                        last.then_inc(sm["hp_ps"], 1)

            def post(b, nxt):
                if nxt:
                    pe.wait_ge(*after("dt_exp", b + 1, NU, NU - 1))
                else:
                    pe.wait_ge(*after("gate_ok", b, NU, NU - 1))
                pe.wait_ge(sm["m_ok"], b + 1)
                for c in range(CH):
                    last = transpose(ps[6][:, c * P:(c + 1) * P], m_sb[:, c, :])
                last.then_inc(sm["mT_ps"], 1)
                pe.wait_ge(sm["mT_ok"], b + 1)
                for f in range(FC):
                    if f >= 2:
                        pe.wait_ge(*after("fr_ok", b, FC, f - 2))
                    mm(ps[6 + (f + 1) % 2][:], w_fc[:, f * P:(f + 1) * P], mT, start=True, stop=True).then_inc(sm["fc_ps"], 1)
                pe.wait_ge(*after("f2_ok", b, FC, FC - 1))
                for c in range(CH):
                    for f in range(FC):
                        last = mm(ps[0][:, c * P:(c + 1) * P], fT[:, f, c * P:(c + 1) * P], w_pr[:, f, :],
                                  start=(f == 0), stop=(f == FC - 1), skip_group_check=True)
                last.then_inc(sm["y_ps"], 1)
                pe.wait_ge(*after("a_ok", b, CH, CH - 1))
                for c in range(CH):
                    last = transpose(ps[6][:, c * P:(c + 1) * P], a1[:, c, :])
                last.then_inc(sm["aT_ps"], 1)
                pe.wait_ge(sm["aT_ok"], b + 1)
                off = b * HK
                for c in range(CH):
                    mm(ps[7][:, c * HK:(c + 1) * HK], aT[:, c * P:(c + 1) * P], xattn_m[:, bass.ds(off, HK)],
                       start=True, stop=False, skip_group_check=True)
                    last = mm(ps[7][:, c * HK:(c + 1) * HK], ones[0:1, :], xattn_b[:, bass.ds(off, HK)],
                              start=False, stop=True, skip_group_check=True)
                last.then_inc(sm["sc_ps"], 1)
                pe.wait_ge(sm["p_ok"], b + 1)
                for c in range(CH):
                    last = transpose(ps[6][0:HK, c * P:(c + 1) * P], soft[:, c * HK:(c + 1) * HK])
                last.then_inc(sm["pT_ps"], 1)
                pe.wait_ge(sm["pT_ok"], b + 1)
                for c in range(CH):
                    mm(ps[7][:, c * P:(c + 1) * P], pT[0:HK, c * P:(c + 1) * P], xattn_vo[:, bass.ds(b * P, P)],
                       start=True, stop=False, skip_group_check=True)
                    last = mm(ps[7][:, c * P:(c + 1) * P], ones[0:1, :], outb[:], start=False, stop=True,
                              skip_group_check=True)
                last.then_inc(sm["xo_ps"], 1)
                pe.wait_ge(*after("x2_ok", b, CH, CH - 1))
                for c in range(CH):
                    last = transpose(ps[6][:, c * P:(c + 1) * P], x2[:, c, :])
                last.then_inc(sm["x2T_ps"], 1)
                pe.wait_ge(sm["x2T_ok"], b + 1)
                for c in range(CH):
                    mm(ps[7][:, c * E:(c + 1) * E], x2T[:, c * P:(c + 1) * P], w_r[:], start=True, stop=False,
                       skip_group_check=True)
                    last = mm(ps[7][:, c * E:(c + 1) * E], ones[0:1, :], rb[:], start=False, stop=True,
                              skip_group_check=True)
                last.then_inc(sm["lg_ps"], 1)
                pe.wait_ge(sm["mask_ok"], b + 1)
                mask = rt[:, 7]
                mm(ps[6][:, 0:CH * E], le, mask, start=True, stop=False, skip_group_check=True)
                for s in range(1, CH):
                    mm(ps[6][:, s * E:CH * E], ones[:], mask[:, 0:(CH - s) * E], start=False, stop=(s == CH - 1),
                       skip_group_check=True)
                mm(ps[6][:, CH * E:2 * CH * E], ones[:], mask, start=True, stop=True,
                   skip_group_check=True).then_inc(sm["cum_ps"], 1)

            setup()
            phase1(0)
            phase2a(0)
            t_levels(0)
            phase2b(0)
            with pe.Fori(1, B) as b:
                phase1(b)
                phase2a(b)
                post(b - 1, True)
                t_levels(b)
                phase2b(b)
            post(B - 1, False)

            def expert(ep, a):
                e = ep * 2 + a
                first = isinstance(ep, int)
                pe.wait_ge(sm[f"e_x_ld{a}"], ep * 48 + 48)
                if first and a == 0:
                    pe.wait_ge(sm["slots_ok"], B)
                if not first or a > 0:
                    pe.wait_ge(sm["e_xT_ok"], e)
                for i, (r0, n) in enumerate(SLOT_TILES):
                    last = transpose(ps[0][:, r0:r0 + n], xe[0:n, a, i * P:(i + 1) * P], n)
                last.then_inc(sm["e_xT_ps"], 1)
                pe.wait_ge(sm["e_xT_ok"], e + 1)
                pe.wait_ge(sm[f"e_w_ld{a}"], ep * 48 + (48 + (16 * (SLOTS // (4 * P)) if a == 0 else 0)))
                for f in range(HC):
                    if not first or a > 0:
                        pe.wait_ge(*after("e_h_ok", e - 1, HC, f))
                    mm(ps[1 + f][:, 0:CAP], moe_w1[:, a, f * P:(f + 1) * P], xeT[:, a, 0:CAP],
                       start=True, stop=True).then_inc(sm["e_h_ps"], 1)
                pe.wait_ge(*after("e_h_ok", e, HC, HC - 1))
                if not first or a > 0:
                    pe.wait_ge(sm["e_o_ok"], e)
                for i, (r0, n) in enumerate(SLOT_TILES):
                    for f in range(HC):
                        mm(ps[5][0:n, i * P:(i + 1) * P], hidT[:, a, f, r0:r0 + n], moe_w2[:, a, f, :],
                           start=(f == 0), stop=False, skip_group_check=True)
                    last = mm(ps[5][0:n, i * P:(i + 1) * P], ones[0:1, 0:n], moe_b2[:, a, :], start=False, stop=True,
                              skip_group_check=True)
                last.then_inc(sm["e_o_ps"], 1)

            expert(0, 0)
            expert(0, 1)
            with pe.Fori(1, E // 2) as ep:
                expert(ep, 0)
                expert(ep, 1)

        @block.scalar
        def _(act):
            A = nc.scalar.activation

            def copy(out_ap, in_ap, done):
                A(out_ap, in_ap, ACT.Copy).then_inc(done, 1)

            for b in range(B):
                act.dma_start(ctx48[b * NK:b * NK + NK - 1, :], ctx_in[b, 0:NK - 1, :]).then_inc(sm["ld_xattn"], 16)
                act.dma_start(ctx48[b * NK + NK - 1:(b + 1) * NK, :], ctx_in[b, CTX - 1:CTX, :]).then_inc(sm["ld_xattn"], 16)
            act.dma_start(inw, in_w.rearrange("(s e) d -> e s d", e=P)).then_inc(sm["ld_xattn"], 16)
            act.dma_start(bias_rows[E * HC:, :], in_b.rearrange("(s e) -> s e", e=P)).then_inc(sm["ld_xattn"], 16)
            act.dma_start(bias_rows[0:E * HC, :], b1.rearrange("e (c p) -> (e c) p", p=P)).then_inc(sm["ld_xattn"], 16)
            act.dma_start(outw, out_w).then_inc(sm["ld_xattn"], 16)
            act.dma_start(outb[:], out_b.rearrange("(o n) -> o n", o=1)).then_inc(sm["ld_xattn"], 16)
            act.dma_start(w_r[:], router_w).then_inc(sm["ld_xattn"], 16)
            act.dma_start(rb[:], router_b.rearrange("(o n) -> o n", o=1)).then_inc(sm["ld_xattn"], 16)

            def setup():
                act.wait_ge(sm["setup_tr"], 1)
                for i, n in enumerate((B * NK, P, P, P)):
                    copy(kT[:, i, 0:n], ps[4 + i][:, 0:n], sm["setup_cp"])
                copy(bias_T[:], ps[3][:, 0:E * HC + 3], sm["setup_cp"])
                act.wait_ge(sm["setup_m"], 1)
                copy(xattn_m[:], ps[6][:, 0:B * HK], sm["setup_done"])
                copy(xattn_b[:], ps[7][0:1, 0:B * HK], sm["setup_done"])
                copy(xattn_vo[:], ps[4][0:HK, :], sm["setup_done"])

            def phase1(b):
                act.wait_ge(sm["hT_ps"], b + 1)
                copy(hT[:], ps[0][:], sm["hT_ok"])
                act.wait_ge(dchain["ph1"], b * PH1 + 1)
                A(gates[:, 1].rearrange("p (c h) -> p c h", c=CH),
                  ps[1][:, 0:64].rearrange("p (c n) -> p c n", c=CH)[:, :, 0:H], ACT.Exp, scale=-1.0).then_inc(sm["u_exp"], 1)
                act.wait_ge(dchain["ph1"], b * PH1 + PH1_Z)
                A(gates[:, 4], gates[:, 3], ACT.Exp).then_inc(sm["u_exp"], 1)
                for n in range(NU):
                    act.wait_ge(*after("k_ps", b, NU, n))
                    if n >= 2:
                        act.wait_ge(*after("kn_ok", b, NU, n - 2))
                    A(k_raw[:, n % 2], ps[2 + n % 2][:], ACT.Silu).then_inc(sm["k_act"], 1)
                    if n >= 2:
                        kT_copy(b, n - 2)
                kT_copy(b, NU - 2)
                kT_copy(b, NU - 1)
                act.wait_ge(sm["eg_ps"], b + 1)
                A(eg[:, :, :].rearrange("p a n -> p (a n)"), ps[1][:, 64:64 + 3 * NP], ACT.Exp).then_inc(sm["eg_ok"], 1)
                for n in range(NU):
                    act.wait_ge(*after("e_ps", b, NU, n))
                    A(att[:, n], ps[6 + n % 2][:], ACT.Exp).then_inc(sm["dt_exp"], 1)

            def kT_copy(b, n):
                act.wait_ge(*after("kT_ps", b, NU, n))
                copy(kT[:, n], ps[4 + n % 2][:], sm["kT_ok"])

            def phase2a(b):
                for n in range(NU):
                    act.wait_ge(*after("q_ps", b, NU, n))
                    A(qT[:, n], ps[2][:], ACT.Silu).then_inc(sm["q_ok"], 1)
                    act.wait_ge(*after("v_ps", b, NU, n))
                    A(vv[:, n], ps[3][:], ACT.Silu).then_inc(sm["v_ok"], 1)

            def t_levels(b):
                for half in range(2):
                    act.wait_ge(*after("l1_ps", b, 2, half))
                    for hi in (32, 96):
                        copy(p_lo[hi:hi + BLK, 16 * half:16 * half + 16, :],
                             ps[2 + half][hi:hi + BLK, :].rearrange("p (q n) -> p q n", n=BLK), sm["l1_ok"])
                for half in range(2):
                    act.wait_ge(*after("l2_ps", b, 2, half))
                    qs = slice(16 * half, 16 * half + 16)
                    A(Tm[BLK:2 * BLK, qs, 0:BLK], ps[4 + half][BLK:2 * BLK, :].rearrange("p (q n) -> p q n", n=BLK),
                      ACT.Copy, scale=-1.0).then_inc(sm["l2_ok"], 1)
                    for lo in (0, 64):
                        hi = lo + BLK
                        A(TT[lo:lo + BLK, qs, hi:hi + BLK], ps[6 + half][lo:lo + BLK, :].rearrange("p (q n) -> p q n", n=BLK),
                          ACT.Copy, scale=-1.0).then_inc(sm["l2_ok"], 1)
                p64 = p_lo[64:P].rearrange("p q n -> p (q n)").rearrange("p (q n) -> p q n", n=64)
                for i in range(4):
                    act.wait_ge(*after("l3_ps", b, 4, i))
                    if i >= 2:
                        act.wait_ge(*after("l4_ps", b, 4, i - 2))
                    copy(p64[:, 8 * (i % 2):8 * (i % 2) + 8, :], ps[2 + i][64:P, :].rearrange("p (q n) -> p q n", n=64), sm["l3_ok"])
                    if i >= 1:
                        l4_copy(b, i - 1)
                l4_copy(b, 3)

            def l4_copy(b, i):
                act.wait_ge(*after("l4_ps", b, 4, i))
                A(TT[0:64, 8 * i:8 * i + 8, 64:P], ps[6 + i % 2][0:64, :].rearrange("p (q n) -> p q n", n=64),
                  ACT.Copy, scale=-1.0).then_inc(sm["l4_ok"], 1)

            def phase2b(b):
                for n in range(NU + 1):
                    if n < NU:
                        act.wait_ge(*after("tr_ps", b, NU, n))
                        if n >= 2:
                            act.wait_ge(*after("au_ps", b, NU, n - 2))
                        copy(u_sb[:, n % 2], ps[3][:], sm["u_ok"])
                        if n >= GR:
                            act.wait_ge(*after("qs_ps", b, NU - 2, n - 2))
                            act.wait_ge(*after("ogT_ps", b, NU, n - 2))
                            copy(o_sb[:, n % 2], ps[4][:], sm["qc_ok"])
                    if n >= 1:
                        act.wait_ge(*after("ogT_ps", b, NU, n - 1))
                        if n >= 3:
                            act.wait_ge(*after("hp_ps", b, NU, n - 3))
                        copy(ogT[:, (n - 1) % 2], ps[7][:], sm["ogT_ok"])
                    if n < NU:
                        act.wait_ge(*after("g_ps", b, NU, n))
                        if n >= 2:
                            act.wait_ge(*after("og_ok", b, NU, n - 2))
                        A(gate_sb[:, n % 2], ps[6][:], ACT.Silu).then_inc(sm["gate_ok"], 1)

            def post(b):
                act.wait_ge(sm["mT_ps"], b + 1)
                copy(mT, ps[6][:], sm["mT_ok"])
                for f in range(FC):
                    act.wait_ge(*after("fc_ps", b, FC, f))
                    A(fT[:, f], ps[6 + (f + 1) % 2][:], ACT.Relu).then_inc(sm["fr_ok"], 1)
                act.wait_ge(sm["aT_ps"], b + 1)
                copy(aT, ps[6][:], sm["aT_ok"])
                act.wait_ge(sm["sm_ok"], b + 1)
                A(soft[:, 0:CH * HK], soft[:, 0:CH * HK], ACT.Exp).then_inc(sm["sexp_ok"], 1)
                act.wait_ge(sm["pT_ps"], b + 1)
                copy(pT[0:HK, :], ps[6][0:HK, :], sm["pT_ok"])
                act.wait_ge(sm["x2T_ps"], b + 1)
                copy(x2T, ps[6][:], sm["x2T_ok"])
                act.wait_ge(sm["lsub_ok"], b + 1)
                A(rt[:, 1], rt[:, 0], ACT.Exp).then_inc(sm["lexp_ok"], 1)

            setup()
            act.wait_ge(sm["ld_misc"], 64)
            A(neg_a[:], neg_a[:], ACT.Exp).then_inc(sm["u_exp"], 1)
            phase1(0)
            phase2a(0)
            t_levels(0)
            phase2b(0)
            with act.Fori(1, B) as b:
                phase1(b)
                phase2a(b)
                post(b - 1)
                t_levels(b)
                phase2b(b)
            post(B - 1)

            def expert(ep, a):
                e = ep * 2 + a
                act.wait_ge(sm["e_xT_ps"], e + 1)
                if not isinstance(ep, int):
                    act.wait_ge(*after("e_h_ps", e - 2, HC, HC - 1))
                copy(xeT[:, a, 0:CAP], ps[0][:, 0:CAP], sm["e_xT_ok"])
                if not isinstance(ep, int):
                    act.wait_ge(sm["e_o_ps"], e - 1)
                A(moe_b1[:, a], b1T[:, bass.ds(e * HC, HC)], ACT.Copy).then_inc(sm["e_b_ok"], 1)
                act.wait_ge(sm["e_b_ok"], e + 1)
                for f in range(HC):
                    act.wait_ge(*after("e_h_ps", e, HC, f))
                    A(hidT[:, a, f, 0:CAP], ps[1 + f][:, 0:CAP], ACT.Gelu, bias=moe_b1[:, a, f:f + 1]).then_inc(sm["e_h_ok"], 1)

            expert(0, 0)
            expert(0, 1)
            with act.Fori(1, E // 2) as ep:
                expert(ep, 0)
                expert(ep, 1)

        @block.vector
        def _(dve):
            tt, ts, stt = dve.tensor_tensor, dve.tensor_scalar, dve.scalar_tensor_tensor
            o_step = sm["o_step"]

            def setup():
                st = Steps(dve, dchain["set"], 0, 2)
                dve.wait_ge(sm["ld_const"], 16)
                dve.tensor_copy(ident_h[:], ident).then_inc(sm["consts_ok"], 1)
                dve.tensor_copy(neg_h[:], const[:, C_NEG:C_NEG + P]).then_inc(sm["consts_ok"], 1)
                dve.wait_ge(sm["setup_kv"], 1)
                dve.wait_ge(sm["ld_xattn"], 16 * (B * 2 + 7))
                k48, v48 = kT[:, 6, 0:B * NK], kT[:, 7, 0:B * NK]
                st.then(ts(k48, ps[4][:, 0:B * NK], inb[:, 1:2], None, ALU.add))
                st.then(ts(v48, ps[5][:, 0:B * NK], inb[:, 2:3], None, ALU.add))
                st.close()
                for i, src in enumerate((k48, v48)):
                    hm = const[:, C_HM + i * XH:C_HM + (i + 1) * XH]
                    for b in range(B):
                        tt(kT[:, 4 + i, b * HK:(b + 1) * HK].rearrange("p (h k) -> p h k", h=XH),
                           bc(src[:, b * NK:(b + 1) * NK].unsqueeze(1), [P, XH, NK]), bc(hm.unsqueeze(2), [P, XH, NK]),
                           ALU.mult).then_inc(sm["setup_blk"], 1)
                dve.wait_ge(sm["ld_w1"], 16 * 7)
                ts(w_o[:], w_o[:], onw[:, 0:1], None, ALU.mult).then_inc(sm["setup_done"], 1)

            def rows_scale(dst, src, r, done):
                for c in range(CH):
                    last = ts(dst[:, c, :], src[:, c, :], r[:, c:c + 1], None, ALU.mult)
                last.then_inc(done, 1)

            def phase1(b):
                st = Steps(dve, dchain["ph1"], b, PH1)
                dve.wait_ge(sm["ld_x"], b * 16 + 16)
                for c in range(CH):
                    last = dve.tensor_tensor_reduce(h_sb[:, c * P:(c + 1) * P], xin[:, c, :], xin[:, c, :], 1.0 / D, 1e-6, ALU.mult, ALU.add,
                                                    st4[:, 0, c:c + 1])
                last.then_inc(sm["ssh_ok"], 1)
                dve.wait_ge(sm["rh_ok"], b + 1)
                rows_scale(h_sb.rearrange("p (c n) -> p c n", c=CH), xin, st4[:, 1], sm["h_ready"])
                gg = lambda i: gates[:, i]
                dve.wait_ge(sm["gates_ps"], b + 1)
                if isinstance(b, int):
                    dve.wait_ge(sm["ld_misc"], 64)
                st.then(tt(gg(0).rearrange("p (c h) -> p c h", c=CH),
                           ps[1][:, 0:64].rearrange("p (c n) -> p c n", c=CH)[:, :, H:2 * H],
                           bc(dtb[:, :].unsqueeze(1), [P, CH, H]), ALU.add))
                st.then(ts(gg(2), gg(0), -1.0, None, ALU.mult))
                st.then(tt(gg(3), gg(0), gg(2), ALU.min))
                dve.wait_ge(sm["u_exp"], b * 2 + 3)
                st.then(ts(gg(5), gg(4), 2.0, None, ALU.add))
                st.then(dve.reciprocal(gg(6), gg(5)))
                st.then(tt(gg(7), gg(4), gg(6), ALU.mult))
                st.then(tt(gg(8), gg(7), gg(7), ALU.mult))
                st.then(ts(gg(9), gg(8), 1.0 / (2 * LOG1P_TERMS + 1), None, ALU.mult))
                for k in range(LOG1P_TERMS - 1, 0, -1):
                    st.then(stt(gg(9), gg(9), 1.0 / (2 * k + 1), gg(8), ALU.add, ALU.mult))
                st.then(stt(gg(10), gg(9), 1.0, gg(7), ALU.add, ALU.mult))
                st.then(ts(gg(11), gg(0), 0.0, None, ALU.max))
                st.then(stt(gg(12), gg(10), 2.0, gg(11), ALU.mult, ALU.add))
                st.then(stt(gg(13).rearrange("p (c h) -> p c h", c=CH), gg(12).rearrange("p (c h) -> p c h", c=CH), -1.0,
                            bc(neg_a[:, :].unsqueeze(1), [P, CH, H]), ALU.mult, ALU.mult))
                ts(g_all[:], gg(13), G_FLOOR, None, ALU.max).then_inc(sm["g_ready"], 1)
                st.then(ts(gg(14), gg(1), 1.0, None, ALU.add))
                dve.reciprocal(beta[:], gg(14)).then_inc(sm["egs_ok"], 1)
                st.close()
                for n in range(NU + 1):
                    if n < NU:
                        dve.wait_ge(*after("k_act", b, NU, n))
                        for h in range(HG):
                            kh = k_raw[:, n % 2, h * P:(h + 1) * P]
                            last = dve.tensor_tensor_reduce(kn[:, n, h * P:(h + 1) * P], kh, kh, 1.0, 1e-6, ALU.mult, ALU.add,
                                                            kss[:, n * HG + h:n * HG + h + 1])
                        last.then_inc(sm["k_sq"], 1)
                    if n >= 1:
                        m = n - 1
                        dve.wait_ge(*after("rk_ok", b, NU, m))
                        tt(heads(kn[:, m]), heads(k_raw[:, m % 2]),
                           bc(rk[:, m * HG:(m + 1) * HG].unsqueeze(2), [P, HG, P]), ALU.mult).then_inc(sm["kn_ok"], 1)
                dve.wait_ge(sm["eg_ok"], b + 1)
                dve.wait_ge(*after("egs_ok", b, 3, 0))
                ts(neg_eg[:], eg[:, 0], -1.0, None, ALU.mult).then_inc(sm["egs_ok"], 1)
                tt(ekb[:], eg[:, 2], beta[:], ALU.mult).then_inc(sm["egs_ok"], 1)
                for n in range(NU):
                    dve.wait_ge(*after("dt_ok", b, NU, n))
                    dve.wait_ge(*after("kk_ps", b, NU, n))
                    tt(Nm[:, n * HG:(n + 1) * HG, :], heads(ps[n % 2][:]), heads(att[:, n]), ALU.mult).then_inc(sm["n_ok"], 1)

            def eliminate(st, j):
                ni, ncol = BLK - 1 - j, j + 1
                pr = prod[:, 0:ni * ncol].rearrange("p (i c) -> p i c", i=ni)
                st.then(tt(pr, bc(blk_n[:, j, j + 1:].unsqueeze(2), [P, ni, ncol]),
                           bc(blk_t[:, j, 0:ncol].unsqueeze(1), [P, ni, ncol]), ALU.mult))
                st.then(tt(blk_t[:, j + 1:, 0:ncol], blk_t[:, j + 1:, 0:ncol], pr, ALU.subtract))

            def phase2a(b):
                st = Steps(dve, dchain["inv"], b, INV)
                if not isinstance(b, int):
                    dve.wait_ge(sm["t_stored"], b * 32)
                flat = blk_t[:, :, :].rearrange("p i c -> p (i c)")
                st.then(dve.memset(flat, 0.0))
                st.then(dve.memset(flat[:, 0:BLK * BLK:BLK + 1], 1.0))
                for n in range(NU):
                    dve.wait_ge(*after("qk_ps", b, NU, n))
                    tt(att[:, n], ps[4 + n % 2][:], att[:, n], ALU.mult).then_inc(sm["at_ok"], 1)
                    if n == 2:
                        dve.wait_ge(sm["n_back"], b * 16 + 16)
                    if n >= 2:
                        for j in range(5 * (n - 2) + (n - 2 > 0), min(BLK - 1, 5 * (n - 1) + 1)):
                            eliminate(st, j)
                st.close()
                dve.tensor_copy(blk_tt, blk_t[:, :, :].rearrange("p i c -> p c i")).then_inc(sm["t_ok"], 1)
                dve.wait_ge(*after("sq_ps", b, NU, NU - 1))
                ts(cq[:], ps[1][:, 0:NP], 1e-6, 1e-6 * P, ALU.add, ALU.mult).then_inc(sm["cq_ok"], 1)

            def rhs(b, n):
                dve.wait_ge(*after("ks_ps", b, NU - 2, n - 2))
                for h in range(HG):
                    col = slice(h * P, (h + 1) * P)
                    last = stt(vv[:, n, col], ps[1 + n % 2][:, col], neg_eg[:, n * HG + h:n * HG + h + 1], vv[:, n, col],
                               ALU.mult, ALU.add)
                last.then_inc(sm["r_ok"], 1)

            def gate_out(b, n):
                dve.wait_ge(*after("f_ok", b, NU, n))
                dve.wait_ge(*after("gate_ok", b, NU, n))
                for h in range(HG):
                    col = slice(h * P, (h + 1) * P)
                    last = stt(o_sb[:, n % 2, col], o_sb[:, n % 2, col], of[:, n * HG + h:n * HG + h + 1],
                               gate_sb[:, n % 2, col], ALU.mult, ALU.mult)
                last.then_inc(sm["og_ok"], 1)

            def phase2b(b):
                dve.wait_ge(*after("egs_ok", b, 3, 2))
                if not isinstance(b, int):
                    dve.wait_ge(sm["x2_st"], b * 16)
                    dve.wait_ge(sm["scattered"], b * 2 * CH * 16)
                for n in range(NU + 1):
                    c, g = n // GR, n % GR
                    if GR <= n + 1 < NU:
                        rhs(b, n + 1)
                    if n >= 1:
                        gate_out(b, n - 1)
                    if n < NU:
                        dve.wait_ge(*after("au_ps", b, NU, n))
                        if n >= 2:
                            dve.wait_ge(*after("ogT_ps", b, NU, n - 2))
                        if c == 0:
                            dve.tensor_copy(o_sb[:, n % 2], ps[5][:]).then_inc(o_step, 1)
                        else:
                            dve.wait_ge(*after("qc_ok", b, NU - 2, n - 2))
                            for h in range(HG):
                                col = slice(h * P, (h + 1) * P)
                                last = stt(o_sb[:, n % 2, col], o_sb[:, n % 2, col], eg[:, 0, n * HG + h:n * HG + h + 1],
                                           ps[5][:, col], ALU.mult, ALU.add)
                            last.then_inc(o_step, 1)
                        if n < NU - 2:
                            dve.wait_ge(*after("ktu_ps", b, NU - 2, n))
                            if c == 0:
                                dve.tensor_copy(St[:, g], ps[6][:]).then_inc(sm["s_ok"], 1)
                            else:
                                for h in range(HG):
                                    col = slice(h * P, (h + 1) * P)
                                    last = stt(St[:, g, col], St[:, g, col], eg[:, 1, n * HG + h:n * HG + h + 1],
                                               ps[6][:, col], ALU.mult, ALU.add)
                                last.then_inc(sm["s_ok"], 1)
                        dve.wait_ge(o_step, b * NU + n + 1)
                        for h in range(HG):
                            oh = o_sb[:, n % 2, h * P:(h + 1) * P]
                            last = dve.tensor_tensor_reduce(x1[:, h, :], oh, oh, 1.0 / P, cq[:, n * HG + h:n * HG + h + 1],
                                                            ALU.mult, ALU.add, oss[:, n * HG + h:n * HG + h + 1])
                        last.then_inc(sm["o_ok"], 1)
                dve.wait_ge(*after("hp_ps", b, NU, NU - 1))
                dve.wait_ge(sm["x_kept"], b + 1)
                tt(x1[:], xres[:], ps[0][:].rearrange("p (c n) -> p c n", c=CH), ALU.add).then_inc(sm["x1_ok"], 1)

            def norm_rows(st, z, var, rstd, dst, v_sem, rs_sem, done, b):
                for c in range(CH):
                    last = dve.bn_stats(bn[:, c, :], z[:, c, :])
                st.then(last, plain=True)
                for c in range(CH):
                    last = dve.bn_aggr(mv[:, c, :], bn[:, c, :])
                st.then(last)
                ts(var, mv[:, :, 1], 1e-5, None, ALU.add).then_inc(v_sem, 1)
                dve.wait_ge(rs_sem, b + 1)
                for c in range(CH):
                    ts(dst[:, c, :], z[:, c, :], mv[:, c, 0:1], rstd[:, c:c + 1], ALU.subtract, ALU.mult).then_inc(done, 1)

            def post(b):
                st = Steps(dve, dchain["post"], b, POST)
                dve.wait_ge(sm["x1_ok"], b + 1)
                for c in range(CH):
                    last = dve.tensor_tensor_reduce(a1[:, c, :], x1[:, c, :], x1[:, c, :], 1.0 / D, 1e-6, ALU.mult, ALU.add,
                                                    st4[:, 2, c:c + 1])
                last.then_inc(sm["ssx_ok"], 1)
                dve.wait_ge(sm["r1_ok"], b + 1)
                rows_scale(m_sb, x1, st4[:, 3], sm["m_ok"])
                for f in range(FC):
                    dve.wait_ge(*after("fr_ok", b, FC, f))
                    tt(fT[:, f], fT[:, f], fT[:, f], ALU.mult).then_inc(sm["f2_ok"], 1)
                dve.wait_ge(sm["y_ps"], b + 1)
                dve.wait_ge(sm["xx_ok"], b + 1)
                st.then(tt(a1[:], xx[:], ps[0][:].rearrange("p (c n) -> p c n", c=CH), ALU.add))
                norm_rows(st, a1, st4[:, 4], st4[:, 5], a1, sm["v1_ok"], sm["rs1_ok"], sm["a_ok"], b)
                sc = soft[:, 0:CH * HK]
                s3 = sc.rearrange("p (n k) -> p n k", k=NK)
                dve.wait_ge(sm["sc_ps"], b + 1)
                st.then(tt(sc, ps[7][:, 0:CH * HK], const[:, C_CNT:C_CNT + CH * HK], ALU.add))
                st.then(dve.tensor_reduce(rt[:, 0], s3, AX.X, ALU.max))
                tt(s3, s3, bc(rt[:, 0].unsqueeze(2), [P, CH * XH, NK]), ALU.subtract).then_inc(sm["sm_ok"], 1)
                dve.wait_ge(sm["sexp_ok"], b + 1)
                st.then(dve.tensor_reduce(rt[:, 1], s3, AX.X, ALU.add))
                st.then(dve.reciprocal(rt[:, 2], rt[:, 1]))
                tt(s3, s3, bc(rt[:, 2].unsqueeze(2), [P, CH * XH, NK]), ALU.mult).then_inc(sm["p_ok"], 1)
                dve.wait_ge(sm["xo_ps"], b + 1)
                st.then(tt(a1[:], a1[:], ps[7][:].rearrange("p (c n) -> p c n", c=CH), ALU.add))
                norm_rows(st, a1, st4[:, 6], st4[:, 7], x2, sm["v2_ok"], sm["rs2_ok"], sm["x2_ok"], b)
                ce = lambda i: rt[:, i].rearrange("p (c e) -> p c e", c=CH)
                dve.wait_ge(sm["lg_ps"], b + 1)
                lg = ps[7][:, 0:CH * E].rearrange("p (c e) -> p c e", c=CH)
                st.then(dve.tensor_reduce(rt[:, 2, 0:CH], lg, AX.X, ALU.max))
                tt(ce(0), lg, bc(rt[:, 2, 0:CH].unsqueeze(2), [P, CH, E]), ALU.subtract).then_inc(sm["lsub_ok"], 1)
                dve.wait_ge(sm["lexp_ok"], b + 1)
                st.then(dve.tensor_reduce(rt[:, 3, 0:CH], ce(1), AX.X, ALU.add))
                st.then(dve.reciprocal(rt[:, 3, CH:2 * CH], rt[:, 3, 0:CH]))
                st.then(tt(ce(4), ce(1), bc(rt[:, 3, CH:2 * CH].unsqueeze(2), [P, CH, E]), ALU.mult), plain=True)
                for c in range(CH):
                    last = dve.max(top8[:, c, :], ce(4)[:, c, :])
                st.then(last, plain=True)
                for c in range(CH):
                    last = dve.max_index(top8i[:, c, :], top8[:, c, :], ce(4)[:, c, :])
                st.then(last)
                top_f = rt[:, 3, 0:2 * CH].rearrange("p (k c) -> p k c", k=2)
                st.then(dve.tensor_copy(top_f, top8i[:, :, 0:2].rearrange("p c k -> p k c")))
                for k in range(2):
                    last = tt(ce(5 + k), bc(iota8.unsqueeze(1), [P, CH, E]), bc(top_f[:, k].unsqueeze(2), [P, CH, E]),
                              ALU.is_equal)
                st.then(last)
                tt(rt[:, 7], rt[:, 5], rt[:, 6], ALU.add).then_inc(sm["mask_ok"], 1)
                for k in range(2):
                    last = tt(ce(8 + k), ce(4), ce(5 + k), ALU.mult)
                dve.wait_ge(sm["cum_ps"], b + 1)
                st.then(stt(ce(10), ps[6][:, 0:CH * E].rearrange("p (c e) -> p c e", c=CH), -1.0,
                            bc(base[:, :].unsqueeze(1), [P, CH, E]), ALU.add, ALU.add))
                for k in range(2):
                    last = tt(ce(5 + k), ce(10), ce(5 + k), ALU.mult)
                st.then(last)
                st.then(dve.tensor_reduce(rt[:, 0, 0:E], ps[6][:, CH * E:2 * CH * E].rearrange("p (c e) -> p e c", c=CH),
                                          AX.X, ALU.add))
                tt(base[:], base[:], rt[:, 0, 0:E], ALU.add)
                both = lambda i, j: rt[:, i, j * 2 * CH:(j + 1) * 2 * CH]
                dve.tensor_reduce(both(11, 0), rt[:, 5:7].rearrange("p k (c e) -> p (k c) e", e=E), AX.X, ALU.add)
                st.then(dve.tensor_reduce(both(11, 1), rt[:, 8:10].rearrange("p k (c e) -> p (k c) e", e=E), AX.X, ALU.add))
                pos, gate = both(11, 0), both(11, 1)
                ts(both(12, 0), pos, float(CAP), None, ALU.is_lt)
                ts(both(12, 1), pos, float(CAP - 1), None, ALU.min)
                st.then(ts(both(12, 2), rt[:, 3, 0:2 * CH], float(CAP), None, ALU.mult))
                valid = both(12, 0)
                tt(both(13, 0), both(12, 1), both(12, 2), ALU.add)
                ts(both(13, 1), valid, float(-2 * SLOTS), float(2 * SLOTS), ALU.mult, ALU.add)
                st.then(tt(wgt_all[:, b] if isinstance(b, int) else wgt_all[:, bass.ds(b, 1)].rearrange("p o n -> p (o n)"),
                           gate, valid, ALU.mult))
                dve.tensor_copy(slot_all[:, b] if isinstance(b, int) else slot_all[:, bass.ds(b, 1)].rearrange("p o n -> p (o n)"),
                                both(13, 0))
                st.then(tt(both(13, 2), both(13, 0), both(13, 1), ALU.add))
                if not isinstance(b, int) or b > 0:
                    dve.wait_ge(sm["scattered"], b * 2 * CH * 16)
                dve.tensor_copy(scat_i[:, :, :].rearrange("p k c -> p (k c)"), both(13, 2)).then_inc(sm["slots_ok"], 1)
                st.close()

            setup()
            dve.wait_ge(sm["base_ok"], 1)
            phase1(0)
            phase2a(0)
            phase2b(0)
            with dve.Fori(1, B) as b:
                phase1(b)
                phase2a(b)
                post(b - 1)
                phase2b(b)
            post(B - 1)

            def expert(ep, a):
                e = ep * 2 + a
                dve.wait_ge(sm["e_o_ps"], e + 1)
                if not isinstance(ep, int):
                    dve.wait_ge(sm["e_o_st"], (e - 1) * 48)
                dve.tensor_copy(oe[:, a, 0:256], ps[5][:, 0:256])
                dve.tensor_copy(oe[0:64, a, 256:384], ps[5][0:64, 256:384]).then_inc(sm["e_o_ok"], 1)

            expert(0, 0)
            expert(0, 1)
            with dve.Fori(1, E // 2) as ep:
                expert(ep, 0)
                expert(ep, 1)

            st = Steps(dve, dchain["fin"], 0, B * 4)
            for i in range(B):
                a = i % 2
                dve.wait_ge(sm[f"f_rows{a}"], (i // 2 + 1) * 2 * CH * 16)
                dve.wait_ge(sm[f"f_x2_{a}"], (i // 2 + 1) * 16)
                if i >= 2:
                    dve.wait_ge(sm[f"f_out{a}"], i // 2 * 16)
                z = yf[:, a]
                for c in range(CH):
                    last = stt(z[:, c, :], rows[:, a * 2, c, :], wgt_all[:, i, c:c + 1], x2f[:, a, c, :], ALU.mult, ALU.add)
                st.then(last)
                for c in range(CH):
                    last = stt(z[:, c, :], rows[:, a * 2 + 1, c, :], wgt_all[:, i, CH + c:CH + c + 1], z[:, c, :],
                               ALU.mult, ALU.add)
                st.then(last)
                for c in range(CH):
                    last = dve.bn_stats(bn[:, c, :], z[:, c, :])
                st.then(last, plain=True)
                for c in range(CH):
                    last = dve.bn_aggr(mv[:, c, :], bn[:, c, :])
                st.then(last)
                ts(st4[:, 0], mv[:, :, 1], 1e-5, None, ALU.add).then_inc(sm["f_v"], 1)
                dve.wait_ge(sm["f_rs"], i + 1)
                for c in range(CH):
                    last = ts(z[:, c, :], z[:, c, :], mv[:, c, 0:1], st4[:, 1, c:c + 1], ALU.subtract, ALU.mult)
                last.then_inc(sm["f_y"], 1)
            st.close()


_INS = ["x", "ctx_1024", "L0_attn_Wq", "L0_attn_Wk", "L0_attn_Wv", "L0_attn_Wb", "L0_attn_Wa", "L0_attn_A_log",
        "L0_attn_dt_bias", "L0_attn_Wg", "L0_attn_o_norm_w", "L0_attn_Wo", "L0_attn_W_fc", "L0_attn_W_proj",
        "L0_xattn_in_proj_w", "L0_xattn_in_proj_b", "L0_xattn_out_w", "L0_xattn_out_b", "L0_ffn_router_w",
        "L0_ffn_router_b", "L0_ffn_w1", "L0_ffn_b1", "L0_ffn_w2", "L0_ffn_b2"]


def kernel(**inputs):
    import numpy as _np
    import concourse.bacc as _bacc
    from concourse import mybir as _mybir
    from concourse.bass_utils import run_bass_kernel_spmd as _run

    nc = _bacc.Bacc("TRN2", target_bir_lowering=False, num_devices=1)
    f32 = _mybir.dt.float32
    arrays, args = {}, []
    for name in _INS:
        a = _np.ascontiguousarray(inputs[name])
        arrays[f"in_{name}"] = a
        args.append(nc.dram_tensor(f"in_{name}", a.shape, _mybir.dt.from_np(a.dtype), kind="ExternalInput").ap())
    arrays["shape_table"] = shape_constants()
    args.append(nc.dram_tensor("shape_table", (P, C_END), f32, kind="ExternalInput").ap())
    for name, shape in (("n_blocks", (NP, NBLK, BLK, BLK)), ("t_blocks", (NP, NBLK, BLK, BLK)),
                        ("tt_blocks", (NP, NBLK, BLK, BLK)), ("x2_rows", (B, S, D)), ("slots", (SLOTS, D)),
                        ("moe_rows", (SLOTS, D))):
        args.append(nc.dram_tensor(name, shape, f32, kind="Internal").ap())
    args.append(nc.dram_tensor("out_0", (B, S, D), f32, kind="ExternalOutput").ap())
    decoder_kernel(nc, *args)
    r = _run(nc, [arrays], core_ids=[0])
    return r.results[0]["out_0"]
```

```python
from contextlib import ExitStack

import numpy as np

import concourse.bass as bass
from concourse import mybir

F32 = mybir.dt.float32
BF16 = mybir.dt.bfloat16
I32 = mybir.dt.int32
U32 = mybir.dt.uint32
ALU = mybir.AluOpType
ACT = mybir.ActivationFunctionType
AX = mybir.AxisListType

P = 128
B, S, D, H = 4, 512, 128, 8
CH = S // P
HG = 4
GR = H // HG
NU = CH * GR
NP = CH * H
BLK = 32
NBLK = P // BLK
DFF = 512
FC = DFF // P
CTX = 154
KEYS = list(range(11)) + [CTX - 1]
NK = len(KEYS)
XH = 8
XD = D // XH
HK = XH * NK
E = 8
CAP = 320
SLOTS = E * CAP
HID = 512
HC = HID // P
NT = B * CH
SLOT_TILES = [(0, 128), (128, 128), (256, 64)]
NEG = -30000.0
G_FLOOR = -200.0
LOG1P_TERMS = 8
PH1, PH1_Z = 20, 3
INV = 2 * (BLK - 1) + 2
POST = 25

C_ID, C_LE, C_GT, C_NEG = 0, P, 2 * P, 3 * P
C_HM = 4 * P
C_IOTA = C_HM + 2 * XH
C_CNT = C_IOTA + E
C_TOK = C_CNT + CH * HK
C_END = C_TOK + B * CH
TOK, GATE = D, D + 1
ROW = D + 1 + E
NO_TOKEN = 4.0 * B * S
EG = 4


def shape_constants():
    t = np.zeros((P, C_END), np.float32)
    r = np.arange(P)
    t[:, C_ID:C_ID + P] = np.eye(P)
    t[:, C_LE:C_LE + P] = r[:, None] <= r[None, :]
    t[:, C_GT:C_GT + P] = r[:, None] > r[None, :]
    t[:, C_NEG:C_NEG + P] = np.where(r[:, None] > r[None, :], NEG, 0.0)
    hm = (r[:, None] // XD) == np.arange(XH)[None, :]
    t[:, C_HM:C_HM + XH] = hm / np.sqrt(XD)
    t[:, C_HM + XH:C_HM + 2 * XH] = hm
    t[:, C_IOTA:C_IOTA + E] = np.arange(E)
    for tok in range(S):
        rows = [i for i in range(-4, 4) if 0 <= tok + i < S]
        while len(rows) < 8:
            if tok + len(rows) < S:
                rows.append(tok + len(rows))
            else:
                rows.insert(0, tok - (8 - len(rows)))
        hit = [min(p % S, CTX - 1) for p in rows]
        count = [hit.count(k) for k in KEYS]
        row = [np.log(n) if n else -1e30 for n in count]
        c = C_CNT + (tok // P) * HK
        t[tok % P, c:c + HK] = row * XH
    t[:, C_TOK:C_END] = np.arange(NT)[None, :] * P + r[:, None]
    return t


def decoder_kernel(nc, x, ctx_in, Wq, Wk, Wv, Wb, Wa, A_log, dt_bias, Wg, o_norm_w, Wo, W_fc, W_proj,
                   in_w, in_b, out_w, out_b, router_w, router_b, w1, b1, w2, b2, table,
                   n_dram, t_dram, tt_dram, y_dram, slots_dram, out):
    with ExitStack() as ctx:
        def sb(name, shape, dt=F32):
            return ctx.enter_context(nc.sbuf_tensor(name, shape, dt))

        def sem(name):
            return ctx.enter_context(nc.semaphore(name))

        const = sb("const", [P, C_END])
        ident, le, gt = const[:, C_ID:C_ID + P], const[:, C_LE:C_LE + P], const[:, C_GT:C_GT + P]
        iota8 = const[:, C_IOTA:C_IOTA + E]
        ident_h, neg_h = sb("ident_h", [P, P], BF16), sb("neg_h", [P, P], BF16)
        ones = sb("ones", [P, P])
        mhalf = sb("mhalf", [P, 16])
        w_qkvg = sb("w_qkvg", [P, 4, H * P])
        w_ba = sb("w_ba", [P, 2 * H])
        dtb = sb("dtb", [P, H])
        neg_a = sb("neg_a", [P, H])
        w_o = sb("w_o", [P, H, P])
        onw = sb("onw", [P, 1])
        w_fc = sb("w_fc", [P, DFF])
        w_pr = sb("w_pr", [P, FC, P])
        outb = sb("outb", [1, P])
        w_r = sb("w_r", [P, E])
        rb = sb("rb", [1, E])
        xattn_m = sb("xattn_m", [P, B * HK])
        xattn_b = sb("xattn_b", [1, B * HK])
        xattn_vo = sb("xattn_vo", [HK, B * P])

        xin = sb("xin", [P, CH, P])
        xres = sb("xres", [P, CH, P])
        hT = sb("hT", [P, CH * P])
        x1 = sb("x1", [P, CH, P])
        xx = sb("xx", [P, CH, P])
        kn = sb("kn", [P, NU, HG * P])
        kT = sb("kT", [P, NU, HG * P])
        att = sb("att", [P, NU, HG * P])
        Nm = sb("Nm", [P, NP, P])
        Tm = sb("Tm", [P, NP, 2 * BLK])
        TT = sb("TT", [P, NP, P])
        qT = sb("qT", [P, NU, HG * P])
        vv = sb("vv", [P, NU, HG * P])
        St = sb("St", [P, GR, HG * P])
        gates = sb("gates", [P, 16, NP])
        eg = sb("eg", [P, 3, NP])
        neg_eg = sb("neg_eg", [P, NP])
        ekb = sb("ekb", [P, NP])
        beta = sb("beta", [P, NP])
        g_all = sb("g_all", [P, NP])
        kss = sb("kss", [P, NP])
        rk = sb("rk", [P, NP])
        cq = sb("cq", [P, NP])
        oss = sb("oss", [P, NP])
        of = sb("of", [P, NP])
        st4 = sb("st4", [P, 8, CH])
        bn = sb("bn", [P, CH, 6])
        mv = sb("mv", [P, CH, 2])
        blk_t = sb("blk_t", [P, BLK, BLK])
        prod = sb("prod", [P, 17 * 16])
        p_lo = sb("p_lo", [P, NP, BLK])
        work = sb("work", [P, 3, 2, HG * P])
        gate_sb = sb("gate_sb", [P, 2, HG * P])
        k_raw = work[:, 0]
        gm = work[:, 1]
        qsq = work[:, 2]
        u_sb = work[:, 0]
        o_sb = work[:, 1]
        ogT = work[:, 2]
        h_sb = work[:, 1, 0]
        blk_n = St[:, :, :].rearrange("p a b -> p (a b)").rearrange("p (i j) -> p i j", i=BLK)
        blk_tt = gate_sb[:, :, :].rearrange("p a b -> p (a b)").rearrange("p (i j) -> p i j", i=BLK)
        fT = vv[:, 4:8]
        mT = p_lo[:, 16:32, :].rearrange("p q n -> p (q n)")
        a1 = sb("a1", [P, CH, P])
        aT = mT
        pT = mT
        soft = x1[:, :, :].rearrange("p c n -> p (c n)")
        x2_rows = sb("x2_rows", [P, CH, ROW])
        x2 = x2_rows[:, :, 0:D]
        m_sb = x2
        x2T = p_lo[:, 0:16, :].rearrange("p q n -> p (q n)")
        rt = sb("rt", [P, 14, CH * E])
        top8 = sb("top8", [P, CH, 8])
        top8i = sb("top8i", [P, CH, 8], U32)
        base = sb("base", [P, E])
        scat_i = sb("scat_i", [P, 2, CH], I32)
        moe_w1 = kn[:, 0:EG]
        moe_w2 = kn[:, EG:2 * EG].rearrange("p a (c n) -> p a c n", c=HC)
        moe_b1 = sb("moe_b1", [P, EG * HC])
        moe_b2 = sb("moe_b2", [1, E, P])
        xe = qT[:, 0:EG, 0:3 * ROW].rearrange("p a (t d) -> p a t d", t=3)
        xeT = kT[:, 0:2]
        hidT = att[:, 0:8].rearrange("p (a c) n -> p a c n", a=2)
        oe = kT[:, 2:4, 0:3 * P].rearrange("p a (t d) -> p a t d", t=3)
        tok_e = sb("tok_e", [P, EG, 3], I32)
        wgt_e = sb("wgt_e", [P, EG, 3])
        yf = vv[:, 0:B].rearrange("p a (c n) -> p a c n", c=CH)
        empty = qT[:, :, :].rearrange("p a n -> p (a n)")[:, 0:4 * ROW]
        ctx48 = vv[0:B * NK, 0, 0:P]
        bias_rows = vv[0:E * HC + 3, 1, 0:P]
        inw = vv[:, 2, 0:3 * P].rearrange("p (s d) -> p s d", s=3)
        outw = vv[:, 3, 0:P]
        bias_T = sb("bias_T", [P, E * HC + 3])
        b1T, inb = bias_T[:, 0:E * HC], bias_T[:, E * HC:]

        ps = [ctx.enter_context(nc.psum_tensor(f"ps{i}", [P, 512], F32)) for i in range(8)]

        names = """ld_const ld_wk ld_w1 ld_x ld_misc ld_xattn zeroed consts_ok setup_tr setup_cp setup_kv setup_blk setup_m setup_done
        base_ok x_kept h_ready hT_ps hT_ok gates_ps g_ready u_exp eg_ps eg_ok egs_ok o_step k_ps k_act k_sq rk_ok kn_ok kT_ps kT_ok
        gm_ok e_ps dt_exp dt_ok kk_ps n_ok n_stored n_back t_ok t_stored tt_back q_ps q_ok q_sq sq_ps cq_ok v_ps v_ok qk_ps at_ok
        kd_ok l1_ps l1_ok l2_ps l2_ok l3_ps l3_ok l4_ps l4_ok ks_ps r_ok tr_ps u_ok qs_ps qc_ok au_ps o_ok f_ok og_ok ogT_ps ogT_ok
        g_ps gate_ok ktu_ps s_ok hp_ps x1_ok xx_ok ssx_ok r1_ok m_ok mT_ps mT_ok fc_ps fr_ok f2_ok y_ps z_ok v1_ok rs1_ok a_ok aT_ps
        aT_ok sc_ps sm_ok sexp_ok p_ok pT_ps pT_ok xo_ps v2_ok rs2_ok x2_ok y_st x2T_ps x2T_ok lg_ps lsub_ok lexp_ok mask_ok
        cum_ps slots_ok scattered ssh_ok rh_ok
        e_w_ld0 e_w_ld1 e_w_ld2 e_w_ld3 e_x_ld0 e_x_ld1 e_x_ld2 e_x_ld3 e_b_ok e_xT_ps e_xT_ok e_h_ps e_h_ok e_o_ps e_o_ok
        w_e_ok row_added e_added empty_0 emptied f_v f_rs f_y f_out""".split()
        sm = {n: sem(n) for n in names}
        dchain, pchain = {}, {}
        f_x = [sem(f"f_x{i}") for i in range(B)]
        for ph in ("set", "ph1", "inv", "post", "fin"):
            dchain[ph] = sem(f"dve_step_{ph}")

        class Steps:
            def __init__(self, eng, s, b, per):
                self.eng, self.s, self.b, self.per, self.k = eng, s, b, per, 0

            def then(self, ins, plain=False):
                self.k += 1
                ins.then_inc(self.s, 1)
                if plain:
                    wait_apart(self.eng, self.s, self.b * self.per + self.k)
                else:
                    self.eng.wait_ge(self.s, self.b * self.per + self.k)

            def close(self):
                assert self.k == self.per, (self.k, self.per)

        def after(name, b, per, k):
            return sm[name], b * per + k + 1

        def wait_apart(eng, s, value):
            if not isinstance(value, int):
                value = eng.to_reg(value)
                eng.wait_ge(sm["ld_const"], 16)
            eng.wait_ge(s, value)

        def bc(ap, shape):
            return ap.to_broadcast(shape)

        def heads(ap):
            return ap.rearrange("p (h n) -> p h n", h=HG)

        block = ctx.enter_context(nc.Block())

        @block.sync
        def _(sp):
            sp.dma_start(const[:], table).then_inc(sm["ld_const"], 16)
            sp.dma_start(xin[:], x[0].rearrange("(c p) d -> p c d", p=P)).then_inc(sm["ld_x"], 16)
            sp.dma_start(w_ba[:, 0:H], Wb).then_inc(sm["ld_misc"], 16)
            sp.dma_start(w_ba[:, H:2 * H], Wa).then_inc(sm["ld_misc"], 16)
            sp.dma_start(dtb[:], dt_bias.partition_broadcast(P)).then_inc(sm["ld_misc"], 16)
            sp.dma_start(neg_a[:], A_log.partition_broadcast(P)).then_inc(sm["ld_misc"], 16)
            sp.dma_start(w_qkvg[:, 1, :], Wk).then_inc(sm["ld_wk"], 16)
            for i, w in ((0, Wq), (2, Wv), (3, Wg)):
                sp.dma_start(w_qkvg[:, i, :], w).then_inc(sm["ld_w1"], 16)
            sp.dma_start(w_o[:], Wo.rearrange("(h p) n -> p h n", p=P)).then_inc(sm["ld_w1"], 16)
            sp.dma_start(onw[:], o_norm_w.rearrange("(p o) -> p o", o=1)).then_inc(sm["ld_w1"], 16)
            sp.dma_start(w_fc[:], W_fc).then_inc(sm["ld_w1"], 16)
            sp.dma_start(w_pr[:], W_proj.rearrange("(f p) n -> p f n", p=P)).then_inc(sm["ld_w1"], 16)
            sp.dma_start(moe_b2[:], b2.rearrange("(o e) n -> o e n", o=1)).then_inc(sm["ld_w1"], 16)
            sp.wait_ge(sm["zeroed"], 1)
            erows = slots_dram.rearrange("(k p r) d -> k p (r d)", p=P, r=4)
            for k in range(SLOTS // (4 * P)):
                sp.dma_start(erows[k], empty).then_inc(sm["emptied"], 16)

            def exchange(b):
                sp.wait_ge(*after("n_ok", b, NU, NU - 1))
                for r in range(NBLK):
                    sp.dma_start(n_dram[:, r].rearrange("q i j -> i q j"),
                                 Nm[BLK * r:BLK * r + BLK, :, BLK * r:BLK * r + BLK]).then_inc(sm["n_stored"], 16)
                sp.wait_ge(sm["n_stored"], b * 64 + 64)
                sp.dma_start(blk_n, n_dram.rearrange("q r i j -> (q r) i j")).then_inc(sm["n_back"], 16)
                sp.wait_ge(*after("t_ok", b, 1, 0))
                sp.dma_start(t_dram.rearrange("q r i j -> (q r) i j"), blk_t[:]).then_inc(sm["t_stored"], 16)
                sp.dma_start(tt_dram.rearrange("q r i j -> (q r) i j"), blk_tt).then_inc(sm["t_stored"], 16)
                sp.wait_ge(sm["t_stored"], b * 32 + 32)
                if isinstance(b, int):
                    sp.wait_ge(sm["zeroed"], 3)
                for r in range(NBLK):
                    sp.dma_start(Tm[BLK * r:BLK * r + BLK, :, BLK * (r % 2):BLK * (r % 2) + BLK],
                                 t_dram[:, r].rearrange("q i j -> i q j")).then_inc(sm["tt_back"], 16)
                    sp.dma_start(TT[BLK * r:BLK * r + BLK, :, BLK * r:BLK * r + BLK],
                                 tt_dram[:, r].rearrange("q i j -> i q j")).then_inc(sm["tt_back"], 16)

            def next_x(b):
                sp.wait_ge(sm["x_kept"], b)
                sp.wait_ge(sm["h_ready"], b)
                sp.dma_start(xin[:], x[b].rearrange("(c p) d -> p c d", p=P)).then_inc(sm["ld_x"], 16)

            def store_x2(b):
                sp.wait_ge(*after("x2_ok", b, CH, CH - 1))
                y_b = y_dram[b * S:(b + 1) * S] if isinstance(b, int) else y_dram[bass.ds(b * S, S)]
                sp.dma_start(y_b.rearrange("(c p) d -> p c d", p=P), x2).then_inc(sm["y_st"], 16)

            exchange(0)
            with sp.Fori(1, B) as b:
                next_x(b)
                store_x2(b - 1)
                exchange(b)
            store_x2(B - 1)

            sp.sem_inc(sm["e_o_ps"], EG)
            sp.sem_inc(sm["e_xT_ps"], EG)
            sp.sem_inc(sm["e_xT_ok"], 1)
            sp.sem_inc(sm["e_h_ok"], EG * HC)
            sp.sem_inc(sm["e_o_ok"], EG)
            sp.sem_inc(sm["e_added"], EG)

            def load_weights(ep, a):
                e = ep * EG + a
                sp.wait_ge(sm["e_o_ps"], e + 1)
                s = sm[f"e_w_ld{a}"]
                sp.dma_start(moe_w1[:, a], w1[e]).then_inc(s, 16)
                sp.dma_start(moe_w2[:, a], w2[e].rearrange("(c p) n -> p c n", p=P)).then_inc(s, 16)

            def load_rows(ep, a):
                e = ep * EG + a
                s = sm[f"e_x_ld{a}"]
                sp.wait_ge(sm["e_xT_ps"], e + 1)
                sp.wait_ge(sm["e_o_ok"], e + 1)
                sp.dma_start(xe[:, a, 0:2], slots_dram[bass.ds(e * CAP, 2 * P)].rearrange("(t p) d -> p t d", p=P)).then_inc(s, 16)
                sp.dma_start(xe[0:CAP - 2 * P, a, 2], slots_dram[bass.ds(e * CAP + 2 * P, CAP - 2 * P)]).then_inc(s, 16)

            sp.wait_ge(sm["s_ok"], B * (NU - 2))
            sp.wait_ge(sm["o_ok"], B * NU)
            sp.wait_ge(sm["hp_ps"], B * NU)
            for a in range(EG):
                load_weights(0, a)
            sp.wait_ge(sm["scattered"], B * 2 * CH * 16)
            for a in range(EG):
                load_rows(0, a)
            with sp.Fori(1, E // EG) as ep:
                for a in range(EG):
                    load_weights(ep, a)
                    load_rows(ep, a)
            sp.wait_ge(sm["e_added"], EG + E)
            for i in range(B):
                sp.dma_start(yf[:, i], y_dram[i * S:(i + 1) * S].rearrange("(c p) d -> p c d", p=P)).then_inc(f_x[i], 16)
            for i in range(B):
                sp.wait_ge(sm["f_y"], i + 1)
                sp.dma_start(out[i].rearrange("(c p) d -> p c d", p=P), yf[:, i]).then_inc(sm["f_out"], 16)
            sp.wait_ge(sm["f_out"], B * 16)

        @block.gpsimd
        def _(pool):
            pool.memset(ones[:], 1.0).then_inc(sm["consts_ok"], 1)
            pool.memset(mhalf[:], -0.5).then_inc(sm["consts_ok"], 1)
            pool.memset(empty, 0.0).then_inc(sm["empty_0"], 1)
            pool.wait_ge(sm["empty_0"], 1)
            pool.memset(empty[:, TOK:4 * ROW:ROW], NO_TOKEN).then_inc(sm["zeroed"], 1)
            pool.memset(Tm[:], 0.0).then_inc(sm["zeroed"], 1)
            pool.memset(TT[:], 0.0).then_inc(sm["zeroed"], 1)
            pool.memset(base[:], 0.0).then_inc(sm["base_ok"], 1)

            def power(out_ap, in_ap, done, n):
                pool.tensor_tensor(out_ap, in_ap, mhalf[:, 0:n], ALU.pow).then_inc(done, 1)

            def phase1(b):
                first = isinstance(b, int)
                pool.wait_ge(sm["ssh_ok"], b + 1)
                power(st4[:, 1], st4[:, 0], sm["rh_ok"], CH)
                if not first:
                    post_r1(b - 1)
                wait_apart(pool, sm["ld_x"], b * 16 + 16)
                if not first:
                    pool.wait_ge(sm["xx_ok"], b)
                    pool.wait_ge(sm["x1_ok"], b)
                pool.tensor_copy(xres[:], xin[:]).then_inc(sm["x_kept"], 1)
                if not first:
                    post_squares(b - 1)
                for n in range(NU):
                    pool.wait_ge(*after("k_sq", b, NU, n))
                    power(rk[:, n * HG:(n + 1) * HG], kss[:, n * HG:(n + 1) * HG], sm["rk_ok"], HG)
                    if n == 4 and not first:
                        post_rs1(b - 1)
                pool.wait_ge(sm["g_ready"], b + 1)
                for n in range(NU):
                    if n >= 2:
                        pool.wait_ge(*after("e_ps", b, NU, n - 2))
                    pool.tensor_tensor(heads(gm[:, n % 2]), bc(gt.unsqueeze(1), [P, HG, P]),
                                       bc(g_all[:, n * HG:(n + 1) * HG].unsqueeze(2), [P, HG, P]),
                                       ALU.mult).then_inc(sm["gm_ok"], 1)
                    if n >= 1:
                        beta_mult(b, n - 1)
                    if n == 5 and not first:
                        post_rs2(b - 1)
                beta_mult(b, NU - 1)
                for n in range(NU):
                    pool.wait_ge(*after("q_ok", b, NU, n))
                    if n >= 2:
                        pool.wait_ge(*after("sq_ps", b, NU, n - 2))
                    pool.tensor_tensor(qsq[:, n % 2], qT[:, n], qT[:, n], ALU.mult).then_inc(sm["q_sq"], 1)
                    if n == 0:
                        pool.wait_ge(*after("egs_ok", b, 3, 2))
                        pool.wait_ge(*after("kT_ps", b, NU, NU - 1))
                    if n < NU - GR:
                        pool.tensor_tensor(heads(kn[:, n]), heads(kn[:, n]),
                                           bc(ekb[:, n * HG:(n + 1) * HG].unsqueeze(2), [P, HG, P]),
                                           ALU.mult).then_inc(sm["kd_ok"], 1)
                    if n >= 4 and not first:
                        post_scatter(b - 1, n - 4)

            def beta_mult(b, n):
                if n == 0:
                    pool.wait_ge(*after("egs_ok", b, 3, 0))
                pool.wait_ge(*after("dt_exp", b, NU, n))
                pool.tensor_tensor(heads(att[:, n]), heads(att[:, n]),
                                   bc(beta[:, n * HG:(n + 1) * HG].unsqueeze(2), [P, HG, P]),
                                   ALU.mult).then_inc(sm["dt_ok"], 1)

            def phase2b(b):
                for n in range(NU):
                    pool.wait_ge(*after("o_ok", b, NU, n))
                    power(of[:, n * HG:(n + 1) * HG], oss[:, n * HG:(n + 1) * HG], sm["f_ok"], HG)
                pool.wait_ge(sm["x1_ok"], b + 1)
                pool.tensor_tensor(xx[:], xres[:], x1[:], ALU.add).then_inc(sm["xx_ok"], 1)

            def post_r1(b):
                pool.wait_ge(sm["ssx_ok"], b + 1)
                power(st4[:, 3], st4[:, 2], sm["r1_ok"], CH)

            def post_squares(b):
                for f in range(FC):
                    pool.wait_ge(*after("fr_ok", b, FC, f))
                    pool.tensor_tensor(fT[:, f], fT[:, f], fT[:, f], ALU.mult).then_inc(sm["f2_ok"], 1)

            def post_rs1(b):
                pool.wait_ge(sm["v1_ok"], b + 1)
                power(st4[:, 5], st4[:, 4], sm["rs1_ok"], CH)

            def post_rs2(b):
                pool.wait_ge(sm["v2_ok"], b + 1)
                power(st4[:, 7], st4[:, 6], sm["rs2_ok"], CH)

            def post_scatter(b, c):
                if c == 0:
                    wait_apart(pool, sm["slots_ok"], b + 1)
                for k in range(2):
                    pool.indirect_dma_start(
                        slots_dram, bass.IndirectOffsetOnAxis(ap=scat_i[:, k, c:c + 1], axis=0),
                        x2_rows[:, c, :], None, bounds_check=SLOTS - 1, oob_is_err=False,
                    ).then_inc(sm["scattered"], 16)

            phase1(0)
            phase2b(0)
            pool.wait_ge(sm["emptied"], 16 * (SLOTS // (4 * P)))
            with pool.Fori(1, B) as b:
                phase1(b)
                phase2b(b)
            post_r1(B - 1)
            post_squares(B - 1)
            post_rs1(B - 1)
            post_rs2(B - 1)
            for c in range(CH):
                post_scatter(B - 1, c)

            def scatter_rows(ep, a):
                e = ep * EG + a
                wait_apart(pool, sm["e_o_ok"], e + 1 + EG)
                for t, (r0, n) in enumerate(SLOT_TILES):
                    pool.indirect_dma_start(
                        y_dram, bass.IndirectOffsetOnAxis(ap=tok_e[0:n, a, t:t + 1], axis=0),
                        oe[0:n, a % 2, t, :], None, bounds_check=B * S - 1, oob_is_err=False, compute_op=ALU.add,
                    ).then_inc(sm["row_added"], 16)
                pool.wait_ge(sm["row_added"], e * 48 + 48)
                pool.sem_inc(sm["e_added"], 1)

            pool.wait_ge(sm["y_st"], B * 16)
            with pool.Fori(0, E // EG) as ep:
                for a in range(EG):
                    scatter_rows(ep, a)
            for i in range(B):
                pool.wait_ge(sm["f_v"], i + 1)
                power(st4[:, 2 * (i % 2) + 1], st4[:, 2 * (i % 2)], sm["f_rs"], CH)

        @block.tensor
        def _(pe):
            mm = nc.tensor.matmul

            def transpose(out_ap, in_ap, n=P):
                return nc.tensor.transpose(out_ap, in_ap, ident[0:n, 0:n])

            def setup():
                pe.wait_ge(sm["ld_const"], 16)
                pe.wait_ge(sm["ld_xattn"], 16 * (B * 2 + 7))
                transpose(ps[4][:, 0:B * NK], ctx48, B * NK)
                transpose(ps[3][:, 0:E * HC + 3], bias_rows, E * HC + 3)
                transpose(ps[5][:, 0:P], inw[:, 1, :])
                transpose(ps[6][:, 0:P], inw[:, 2, :])
                transpose(ps[7][:, 0:P], outw).then_inc(sm["setup_tr"], 1)
                pe.wait_ge(sm["setup_cp"], 5)
                ctxT, wkT, wvT, woT = (kT[:, i, 0:P] for i in range(4))
                mm(ps[4][:, 0:B * NK], wkT, ctxT[:, 0:B * NK], start=True, stop=True)
                mm(ps[5][:, 0:B * NK], wvT, ctxT[:, 0:B * NK], start=True, stop=True).then_inc(sm["setup_kv"], 1)
                pe.wait_ge(sm["setup_blk"], 2 * B)
                kblk, vblk = kT[:, 4, 0:B * HK], kT[:, 5, 0:B * HK]
                mm(ps[6][:, 0:B * HK], inw[:, 0, :], kblk, start=True, stop=True)
                mm(ps[7][0:1, 0:B * HK], inb[:, 0:1], kblk, start=True, stop=True)
                for b in range(B):
                    last = mm(ps[4][0:HK, b * P:(b + 1) * P], vblk[:, b * HK:(b + 1) * HK], woT, start=True, stop=True)
                last.then_inc(sm["setup_m"], 1)

            def k_proj(b, n):
                c, g = n // GR, n % GR
                if n >= 2:
                    pe.wait_ge(*after("k_act", b, NU, n - 2))
                mm(ps[2 + n % 2][:], hT[:, c * P:(c + 1) * P], w_qkvg[:, 1, g * 512:(g + 1) * 512],
                   start=True, stop=True).then_inc(sm["k_ps"], 1)

            def k_transpose(b, n):
                pe.wait_ge(*after("kn_ok", b, NU, n))
                if n >= 2:
                    pe.wait_ge(*after("kT_ok", b, NU, n - 2))
                for h in range(HG):
                    last = transpose(ps[4 + n % 2][:, h * P:(h + 1) * P], kn[:, n, h * P:(h + 1) * P])
                last.then_inc(sm["kT_ps"], 1)

            def phase1(b):
                first = isinstance(b, int) and b == 0
                if first:
                    pe.wait_ge(sm["ld_const"], 16)
                else:
                    pe.wait_ge(sm["x1_ok"], b)
                pe.wait_ge(sm["h_ready"], b + 1)
                for c in range(CH):
                    last = transpose(ps[0][:, c * P:(c + 1) * P], h_sb[:, c * P:(c + 1) * P])
                last.then_inc(sm["hT_ps"], 1)
                pe.wait_ge(sm["hT_ok"], b + 1)
                if first:
                    pe.wait_ge(sm["ld_misc"], 64)
                for c in range(CH):
                    last = mm(ps[1][:, c * 16:(c + 1) * 16], hT[:, c * P:(c + 1) * P], w_ba[:], start=True, stop=True)
                last.then_inc(sm["gates_ps"], 1)
                if first:
                    pe.wait_ge(sm["ld_wk"], 16)
                else:
                    post_fc(b - 1)
                for n in range(NU + 2):
                    if n < NU:
                        k_proj(b, n)
                    if n >= 2:
                        k_transpose(b, n - 2)
                    if not first:
                        if n == 2:
                            post_y(b - 1)
                        if n == 6:
                            post_aT(b - 1)
                        if n == 7:
                            post_sc(b - 1)
                pe.wait_ge(sm["g_ready"], b + 1)
                if first:
                    pe.wait_ge(sm["consts_ok"], 4)
                for i, tri in enumerate((le, ones[:], gt)):
                    last = mm(ps[1][:, 64 + i * NP:64 + (i + 1) * NP], tri, g_all[:], start=True, stop=True)
                last.then_inc(sm["eg_ps"], 1)
                for n in range(NU + 1):
                    if n < NU:
                        e = ps[6 + n % 2]
                        if n >= 2:
                            pe.wait_ge(*after("dt_exp", b, NU, n - 2))
                        elif not first:
                            pe.wait_ge(sm["aT_ok" if n == 0 else "sm_ok"], b)
                        pe.wait_ge(*after("gm_ok", b, NU, n))
                        for h in range(HG):
                            mm(e[:, h * P:(h + 1) * P], ident_h[:], neg_h[:], start=True, stop=False, skip_group_check=True)
                            last = mm(e[:, h * P:(h + 1) * P], gm[:, n % 2, h * P:(h + 1) * P], le,
                                      start=False, stop=True, skip_group_check=True)
                        last.then_inc(sm["e_ps"], 1)
                    if n >= 1:
                        kk_gram(b, n - 1)
                    if not first:
                        if n == 1:
                            pe.wait_ge(*after("k_act", b, NU, NU - 1))
                            post_pT(b - 1)
                        if n == 3:
                            post_xo(b - 1)

            def kk_gram(b, n):
                pe.wait_ge(*after("kT_ok", b, NU, n))
                if n >= 2:
                    pe.wait_ge(*after("n_ok", b, NU, n - 2))
                if n == 1:
                    pe.wait_ge(sm["eg_ok"], b + 1)
                for h in range(HG):
                    kh = kT[:, n, h * P:(h + 1) * P]
                    last = mm(ps[n % 2][:, h * P:(h + 1) * P], kh, kh, start=True, stop=True)
                last.then_inc(sm["kk_ps"], 1)

            def phase2a(b):
                if isinstance(b, int) and b == 0:
                    pe.wait_ge(sm["ld_w1"], 16 * 8)
                pe.wait_ge(*after("k_act", b, NU, NU - 1))
                pe.wait_ge(*after("n_ok", b, NU, NU - 1))
                first = isinstance(b, int)
                if not first:
                    pe.wait_ge(sm["v2_ok"], b)
                for n in range(NU + 1):
                    if n < NU:
                        c, g = n // GR, n % GR
                        if n >= 1:
                            pe.wait_ge(*after("q_ok", b, NU, n - 1))
                        for h in range(HG):
                            hh = (g * HG + h) * P
                            last = mm(ps[2][:, h * P:(h + 1) * P], w_qkvg[:, 0, hh:hh + P], hT[:, c * P:(c + 1) * P],
                                      start=True, stop=True)
                        last.then_inc(sm["q_ps"], 1)
                        if n >= 1:
                            pe.wait_ge(*after("v_ok", b, NU, n - 1))
                        mm(ps[3][:], hT[:, c * P:(c + 1) * P], w_qkvg[:, 2, g * 512:(g + 1) * 512],
                           start=True, stop=True).then_inc(sm["v_ps"], 1)
                    if n >= 1:
                        m = n - 1
                        pe.wait_ge(*after("q_ok", b, NU, m))
                        if m >= 2:
                            pe.wait_ge(*after("at_ok", b, NU, m - 2))
                        elif m == 0:
                            pe.wait_ge(*after("kT_ok", b, NU, NU - 1))
                        for h in range(HG):
                            last = mm(ps[4 + m % 2][:, h * P:(h + 1) * P], kT[:, m, h * P:(h + 1) * P],
                                      qT[:, m, h * P:(h + 1) * P], start=True, stop=True)
                        last.then_inc(sm["qk_ps"], 1)
                        pe.wait_ge(*after("q_sq", b, NU, m))
                        for h in range(HG):
                            last = mm(ps[1][:, m * HG + h:m * HG + h + 1], qsq[:, m % 2, h * P:(h + 1) * P],
                                      ones[:, 0:1], start=True, stop=True)
                        last.then_inc(sm["sq_ps"], 1)
                    if not first:
                        if n == 0:
                            pe.wait_ge(*after("dt_exp", b, NU, NU - 1))
                            post_x2T(b - 1)
                        if n == 1:
                            post_lg(b - 1)
                        if n == 3:
                            post_cum(b - 1)

            def t_levels(b):
                wait_apart(pe, sm["tt_back"], b * 128 + 128)
                pe.wait_ge(*after("v_ok", b, NU, NU - 1))
                pe.wait_ge(*after("at_ok", b, NU, NU - 1))
                if not isinstance(b, int) or b > 0:
                    pe.wait_ge(sm["slots_ok"], b)
                pe.wait_ge(sm["cq_ok"], b + 1)
                pe.wait_ge(*after("dt_exp", b, NU, NU - 1))
                for half in range(2):
                    for q in range(16 * half, 16 * half + 16):
                        col = (q % 16) * BLK
                        for lo in (0, 64):
                            hi = lo + BLK
                            last = mm(ps[2 + half][hi:hi + BLK, col:col + BLK], Nm[lo:lo + BLK, q, hi:hi + BLK],
                                      Tm[lo:lo + BLK, q, 0:BLK], start=True, stop=True, skip_group_check=True)
                    last.then_inc(sm["l1_ps"], 1)
                for half in range(2):
                    wait_apart(pe, *after("l1_ok", b, 4, 2 * half + 1))
                    for q in range(16 * half, 16 * half + 16):
                        col = (q % 16) * BLK
                        mm(ps[4 + half][BLK:2 * BLK, col:col + BLK], TT[BLK:2 * BLK, q, BLK:2 * BLK],
                           p_lo[BLK:2 * BLK, q, :], start=True, stop=True, skip_group_check=True)
                        for lo in (0, 64):
                            hi = lo + BLK
                            last = mm(ps[6 + half][lo:lo + BLK, col:col + BLK], p_lo[hi:hi + BLK, q, :],
                                      TT[hi:hi + BLK, q, hi:hi + BLK], start=True, stop=True, skip_group_check=True)
                    last.then_inc(sm["l2_ps"], 1)
                banks = [2, 3, 4, 5]
                wait_apart(pe, *after("l2_ok", b, 6, 5))
                for i in range(4):
                    for q in range(8 * i, 8 * i + 8):
                        col = (q % 8) * 64
                        last = mm(ps[banks[i]][64:P, col:col + 64], Nm[0:64, q, 64:P], Tm[0:64, q, :],
                                  start=True, stop=True, skip_group_check=True)
                    last.then_inc(sm["l3_ps"], 1)
                for i in range(4):
                    wait_apart(pe, *after("l3_ok", b, 4, i))
                    p64 = p_lo[64:P].rearrange("p q n -> p (q n)").rearrange("p (q n) -> p q n", n=64)
                    if i >= 2:
                        wait_apart(pe, *after("l4_ok", b, 4, i - 2))
                    for q in range(8 * i, 8 * i + 8):
                        col = (q % 8) * 64
                        last = mm(ps[6 + i % 2][0:64, col:col + 64], p64[:, q % 16, :], TT[64:P, q, 64:P],
                                  start=True, stop=True, skip_group_check=True)
                    last.then_inc(sm["l4_ps"], 1)

            def ks(b, n):
                g = n % GR
                if n == 2:
                    pe.wait_ge(*after("l3_ok", b, 4, 3))
                if n >= 4:
                    pe.wait_ge(*after("r_ok", b, NU - 2, n - 4))
                pe.wait_ge(*after("s_ok", b, NU - 2, n - 2))
                for h in range(HG):
                    last = mm(ps[1 + n % 2][:, h * P:(h + 1) * P], kT[:, n, h * P:(h + 1) * P],
                              St[:, g, h * P:(h + 1) * P], start=True, stop=True)
                last.then_inc(sm["ks_ps"], 1)

            def phase2b(b):
                pe.wait_ge(*after("l4_ok", b, 4, 3))
                if not isinstance(b, int) or b > 0:
                    pe.wait_ge(sm["xx_ok"], b)
                for n in range(NU + 1):
                    c, g = n // GR, n % GR
                    if n < NU:
                        if GR <= n + 1 < NU:
                            ks(b, n + 1)
                        if n >= 2:
                            pe.wait_ge(*after("r_ok", b, NU - 2, n - 2))
                        if n >= 1:
                            pe.wait_ge(*after("u_ok", b, NU, n - 1))
                        for h in range(HG):
                            last = mm(ps[3][:, h * P:(h + 1) * P], TT[:, c * H + g * HG + h, :],
                                      vv[:, n, h * P:(h + 1) * P], start=True, stop=True)
                        last.then_inc(sm["tr_ps"], 1)
                        if n >= 1:
                            pe.wait_ge(*after("o_ok", b, NU, n - 1))
                        if c > 0:
                            for h in range(HG):
                                last = mm(ps[4][:, h * P:(h + 1) * P], qT[:, n, h * P:(h + 1) * P],
                                          St[:, g, h * P:(h + 1) * P], start=True, stop=True)
                            last.then_inc(sm["qs_ps"], 1)
                        if n >= 1:
                            if n >= 2:
                                pe.wait_ge(*after("ogT_ok", b, NU, n - 2))
                            pe.wait_ge(*after("og_ok", b, NU, n - 1))
                            for h in range(HG):
                                last = transpose(ps[7][:, h * P:(h + 1) * P], o_sb[:, (n - 1) % 2, h * P:(h + 1) * P])
                            last.then_inc(sm["ogT_ps"], 1)
                        pe.wait_ge(*after("u_ok", b, NU, n))
                        for h in range(HG):
                            last = mm(ps[5][:, h * P:(h + 1) * P], att[:, n, h * P:(h + 1) * P],
                                      u_sb[:, n % 2, h * P:(h + 1) * P], start=True, stop=True)
                        last.then_inc(sm["au_ps"], 1)
                        if 1 <= n <= NU - 2:
                            pe.wait_ge(*after("s_ok", b, NU - 2, n - 1))
                        elif n == NU - 1:
                            pe.wait_ge(*after("gate_ok", b, NU, n - 1))
                        mm(ps[6][:], hT[:, c * P:(c + 1) * P], w_qkvg[:, 3, g * 512:(g + 1) * 512],
                           start=True, stop=True).then_inc(sm["g_ps"], 1)
                        if n < NU - 2:
                            pe.wait_ge(*after("gate_ok", b, NU, n))
                            pe.wait_ge(*after("kd_ok", b, NU - 2, n))
                            for h in range(HG):
                                last = mm(ps[6][:, h * P:(h + 1) * P], kn[:, n, h * P:(h + 1) * P],
                                          u_sb[:, n % 2, h * P:(h + 1) * P], start=True, stop=True)
                            last.then_inc(sm["ktu_ps"], 1)
                    else:
                        pe.wait_ge(*after("ogT_ok", b, NU, n - 2))
                        pe.wait_ge(*after("og_ok", b, NU, n - 1))
                        for h in range(HG):
                            last = transpose(ps[7][:, h * P:(h + 1) * P], o_sb[:, (n - 1) % 2, h * P:(h + 1) * P])
                        last.then_inc(sm["ogT_ps"], 1)
                    if n >= 1:
                        m = n - 1
                        pe.wait_ge(*after("ogT_ok", b, NU, m))
                        cm, gmm = m // GR, m % GR
                        for h in range(HG):
                            hh = gmm * HG + h
                            last = mm(ps[0][:, cm * P:(cm + 1) * P], ogT[:, m % 2, h * P:(h + 1) * P], w_o[:, hh, :],
                                      start=(hh == 0), stop=(hh == H - 1), skip_group_check=True)
                        last.then_inc(sm["hp_ps"], 1)

            def post_fc(b):
                pe.wait_ge(sm["m_ok"], b + 1)
                for c in range(CH):
                    last = transpose(ps[6][:, c * P:(c + 1) * P], m_sb[:, c, :])
                last.then_inc(sm["mT_ps"], 1)
                pe.wait_ge(sm["mT_ok"], b + 1)
                for f in range(FC):
                    if f >= 2:
                        pe.wait_ge(*after("fr_ok", b, FC, f - 2))
                    mm(ps[6 + (f + 1) % 2][:], w_fc[:, f * P:(f + 1) * P], mT, start=True, stop=True).then_inc(sm["fc_ps"], 1)

            def post_y(b):
                pe.wait_ge(*after("f2_ok", b, FC, FC - 1))
                for c in range(CH):
                    for f in range(FC):
                        last = mm(ps[7][:, c * P:(c + 1) * P], fT[:, f, c * P:(c + 1) * P], w_pr[:, f, :],
                                  start=(f == 0), stop=(f == FC - 1), skip_group_check=True)
                last.then_inc(sm["y_ps"], 1)

            def post_aT(b):
                pe.wait_ge(*after("a_ok", b, CH, CH - 1))
                for c in range(CH):
                    last = transpose(ps[6][:, c * P:(c + 1) * P], a1[:, c, :])
                last.then_inc(sm["aT_ps"], 1)

            def post_sc(b):
                pe.wait_ge(sm["aT_ok"], b + 1)
                off = b * HK
                for c in range(CH):
                    mm(ps[7][:, c * HK:(c + 1) * HK], aT[:, c * P:(c + 1) * P], xattn_m[:, bass.ds(off, HK)],
                       start=True, stop=False, skip_group_check=True)
                    last = mm(ps[7][:, c * HK:(c + 1) * HK], ones[0:1, :], xattn_b[:, bass.ds(off, HK)],
                              start=False, stop=True, skip_group_check=True)
                last.then_inc(sm["sc_ps"], 1)

            def post_pT(b):
                pe.wait_ge(sm["p_ok"], b + 1)
                for c in range(CH):
                    last = transpose(ps[2][0:HK, c * P:(c + 1) * P], soft[:, c * HK:(c + 1) * HK])
                last.then_inc(sm["pT_ps"], 1)

            def post_xo(b):
                pe.wait_ge(sm["pT_ok"], b + 1)
                for c in range(CH):
                    mm(ps[3][:, c * P:(c + 1) * P], pT[0:HK, c * P:(c + 1) * P], xattn_vo[:, bass.ds(b * P, P)],
                       start=True, stop=False, skip_group_check=True)
                    last = mm(ps[3][:, c * P:(c + 1) * P], ones[0:1, :], outb[:], start=False, stop=True,
                              skip_group_check=True)
                last.then_inc(sm["xo_ps"], 1)

            def post_x2T(b):
                pe.wait_ge(*after("x2_ok", b, CH, CH - 1))
                for c in range(CH):
                    last = transpose(ps[6][:, c * P:(c + 1) * P], x2[:, c, :])
                last.then_inc(sm["x2T_ps"], 1)

            def post_lg(b):
                pe.wait_ge(sm["x2T_ok"], b + 1)
                for c in range(CH):
                    mm(ps[7][:, c * E:(c + 1) * E], x2T[:, c * P:(c + 1) * P], w_r[:], start=True, stop=False,
                       skip_group_check=True)
                    last = mm(ps[7][:, c * E:(c + 1) * E], ones[0:1, :], rb[:], start=False, stop=True,
                              skip_group_check=True)
                last.then_inc(sm["lg_ps"], 1)

            def post_cum(b):
                pe.wait_ge(sm["mask_ok"], b + 1)
                mask = rt[:, 7]
                mm(ps[6][:, 0:CH * E], le, mask, start=True, stop=False, skip_group_check=True)
                for s in range(1, CH):
                    mm(ps[6][:, s * E:CH * E], ones[:], mask[:, 0:(CH - s) * E], start=False, stop=(s == CH - 1),
                       skip_group_check=True)
                mm(ps[6][:, CH * E:2 * CH * E], ones[:], mask, start=True, stop=True,
                   skip_group_check=True).then_inc(sm["cum_ps"], 1)

            setup()
            phase1(0)
            phase2a(0)
            t_levels(0)
            phase2b(0)
            with pe.Fori(1, B) as b:
                phase1(b)
                phase2a(b)
                t_levels(b)
                phase2b(b)
            pe.wait_ge(sm["x1_ok"], B)
            for stage in (post_fc, post_y, post_aT, post_sc, post_pT, post_xo, post_x2T, post_lg, post_cum):
                stage(B - 1)

            def expert_rows(ep, a):
                e = ep * EG + a
                pe.wait_ge(sm[f"e_x_ld{a}"], ep * 32 + 32)
                pe.wait_ge(sm["e_xT_ok"], e + 1)
                for t, (r0, n) in enumerate(SLOT_TILES):
                    last = transpose(ps[0][:, r0:r0 + n], xe[0:n, a, t, 0:D], n)
                last.then_inc(sm["e_xT_ps"], 1)

            pe.wait_ge(sm["slots_ok"], B)
            with pe.Fori(0, E // EG) as ep:
                expert_rows(ep, 0)
                for a in range(EG):
                    e = ep * EG + a
                    pe.wait_ge(sm["e_xT_ok"], e + 2)
                    pe.wait_ge(sm[f"e_w_ld{a}"], ep * 32 + 32)
                    for f in range(HC):
                        pe.wait_ge(sm["e_h_ok"], (e + EG - 1) * HC + f + 1)
                        mm(ps[1 + f][:, 0:CAP], moe_w1[:, a, f * P:(f + 1) * P], xeT[:, a % 2, 0:CAP],
                           start=True, stop=True).then_inc(sm["e_h_ps"], 1)
                    if a + 1 < EG:
                        expert_rows(ep, a + 1)
                    pe.wait_ge(sm["e_o_ok"], e + EG - 1)
                    for t, (r0, n) in enumerate(SLOT_TILES):
                        mm(ps[5 + a % 2][:, t * P:(t + 1) * P], ones[0:1, :], moe_b2[:, bass.ds(e, 1), :].rearrange("p o n -> p (o n)"),
                           start=True, stop=False, skip_group_check=True)
                        for f in range(HC):
                            if t == 0:
                                pe.wait_ge(sm["e_h_ok"], (e + EG) * HC + f + 1)
                            last = mm(ps[5 + a % 2][0:n, t * P:(t + 1) * P], hidT[:, a % 2, f, r0:r0 + n],
                                      moe_w2[:, a, f, :], start=False, stop=(f == HC - 1), skip_group_check=True)
                    last.then_inc(sm["e_o_ps"], 1)

        @block.scalar
        def _(act):
            A = nc.scalar.activation

            def copy(out_ap, in_ap, done):
                A(out_ap, in_ap, ACT.Copy).then_inc(done, 1)

            for b in range(B):
                act.dma_start(ctx48[b * NK:b * NK + NK - 1, :], ctx_in[b, 0:NK - 1, :]).then_inc(sm["ld_xattn"], 16)
                act.dma_start(ctx48[b * NK + NK - 1:(b + 1) * NK, :], ctx_in[b, CTX - 1:CTX, :]).then_inc(sm["ld_xattn"], 16)
            act.dma_start(inw, in_w.rearrange("(s e) d -> e s d", e=P)).then_inc(sm["ld_xattn"], 16)
            act.dma_start(bias_rows[E * HC:, :], in_b.rearrange("(s e) -> s e", e=P)).then_inc(sm["ld_xattn"], 16)
            act.dma_start(bias_rows[0:E * HC, :], b1.rearrange("e (c p) -> (e c) p", p=P)).then_inc(sm["ld_xattn"], 16)
            act.dma_start(outw, out_w).then_inc(sm["ld_xattn"], 16)
            act.dma_start(outb[:], out_b.rearrange("(o n) -> o n", o=1)).then_inc(sm["ld_xattn"], 16)
            act.dma_start(w_r[:], router_w).then_inc(sm["ld_xattn"], 16)
            act.dma_start(rb[:], router_b.rearrange("(o n) -> o n", o=1)).then_inc(sm["ld_xattn"], 16)

            def setup():
                act.wait_ge(sm["setup_tr"], 1)
                for i, n in enumerate((B * NK, P, P, P)):
                    copy(kT[:, i, 0:n], ps[4 + i][:, 0:n], sm["setup_cp"])
                copy(bias_T[:], ps[3][:, 0:E * HC + 3], sm["setup_cp"])
                act.wait_ge(sm["setup_m"], 1)
                copy(xattn_m[:], ps[6][:, 0:B * HK], sm["setup_done"])
                copy(xattn_b[:], ps[7][0:1, 0:B * HK], sm["setup_done"])
                copy(xattn_vo[:], ps[4][0:HK, :], sm["setup_done"])

            def phase1(b):
                first = isinstance(b, int)
                act.wait_ge(sm["hT_ps"], b + 1)
                copy(hT[:], ps[0][:], sm["hT_ok"])
                if not first:
                    post_mT(b - 1)
                act.wait_ge(dchain["ph1"], b * PH1 + 1)
                A(gates[:, 1].rearrange("p (c h) -> p c h", c=CH),
                  ps[1][:, 0:64].rearrange("p (c n) -> p c n", c=CH)[:, :, 0:H], ACT.Exp, scale=-1.0).then_inc(sm["u_exp"], 1)
                act.wait_ge(dchain["ph1"], b * PH1 + PH1_Z)
                A(gates[:, 4], gates[:, 3], ACT.Exp).then_inc(sm["u_exp"], 1)
                if not first:
                    post_relu(b - 1)
                for n in range(NU):
                    act.wait_ge(*after("k_ps", b, NU, n))
                    if n >= 2:
                        act.wait_ge(*after("kn_ok", b, NU, n - 2))
                    A(k_raw[:, n % 2], ps[2 + n % 2][:], ACT.Silu).then_inc(sm["k_act"], 1)
                    if n >= 2:
                        kT_copy(b, n - 2)
                    if n == 6 and not first:
                        post_aT(b - 1)
                kT_copy(b, NU - 2)
                kT_copy(b, NU - 1)
                act.wait_ge(sm["eg_ps"], b + 1)
                A(eg[:, :, :].rearrange("p a n -> p (a n)"), ps[1][:, 64:64 + 3 * NP], ACT.Exp).then_inc(sm["eg_ok"], 1)
                if not first:
                    post_sexp(b - 1)
                for n in range(NU):
                    act.wait_ge(*after("e_ps", b, NU, n))
                    A(att[:, n], ps[6 + n % 2][:], ACT.Exp).then_inc(sm["dt_exp"], 1)
                    if n == 1 and not first:
                        post_pT(b - 1)

            def kT_copy(b, n):
                act.wait_ge(*after("kT_ps", b, NU, n))
                copy(kT[:, n], ps[4 + n % 2][:], sm["kT_ok"])

            def phase2a(b):
                if isinstance(b, int):
                    act.wait_ge(sm["emptied"], 16 * (SLOTS // (4 * P)))
                for n in range(NU):
                    act.wait_ge(*after("q_ps", b, NU, n))
                    A(qT[:, n], ps[2][:], ACT.Silu).then_inc(sm["q_ok"], 1)
                    act.wait_ge(*after("v_ps", b, NU, n))
                    A(vv[:, n], ps[3][:], ACT.Silu).then_inc(sm["v_ok"], 1)
                    if n == 0 and not isinstance(b, int):
                        post_x2T(b - 1)
                    if n == 2 and not isinstance(b, int):
                        post_lexp(b - 1)

            def t_levels(b):
                for half in range(2):
                    act.wait_ge(*after("l1_ps", b, 2, half))
                    for hi in (32, 96):
                        copy(p_lo[hi:hi + BLK, 16 * half:16 * half + 16, :],
                             ps[2 + half][hi:hi + BLK, :].rearrange("p (q n) -> p q n", n=BLK), sm["l1_ok"])
                for half in range(2):
                    act.wait_ge(*after("l2_ps", b, 2, half))
                    qs = slice(16 * half, 16 * half + 16)
                    A(Tm[BLK:2 * BLK, qs, 0:BLK], ps[4 + half][BLK:2 * BLK, :].rearrange("p (q n) -> p q n", n=BLK),
                      ACT.Copy, scale=-1.0).then_inc(sm["l2_ok"], 1)
                    for lo in (0, 64):
                        hi = lo + BLK
                        A(TT[lo:lo + BLK, qs, hi:hi + BLK], ps[6 + half][lo:lo + BLK, :].rearrange("p (q n) -> p q n", n=BLK),
                          ACT.Copy, scale=-1.0).then_inc(sm["l2_ok"], 1)
                p64 = p_lo[64:P].rearrange("p q n -> p (q n)").rearrange("p (q n) -> p q n", n=64)
                for i in range(4):
                    act.wait_ge(*after("l3_ps", b, 4, i))
                    if i >= 2:
                        act.wait_ge(*after("l4_ps", b, 4, i - 2))
                    copy(p64[:, 8 * (i % 2):8 * (i % 2) + 8, :], ps[2 + i][64:P, :].rearrange("p (q n) -> p q n", n=64), sm["l3_ok"])
                    if i >= 1:
                        l4_copy(b, i - 1)
                l4_copy(b, 3)

            def l4_copy(b, i):
                act.wait_ge(*after("l4_ps", b, 4, i))
                A(TT[0:64, 8 * i:8 * i + 8, 64:P], ps[6 + i % 2][0:64, :].rearrange("p (q n) -> p q n", n=64),
                  ACT.Copy, scale=-1.0).then_inc(sm["l4_ok"], 1)

            def phase2b(b):
                for n in range(NU + 1):
                    if n < NU:
                        act.wait_ge(*after("tr_ps", b, NU, n))
                        if n >= 2:
                            act.wait_ge(*after("au_ps", b, NU, n - 2))
                        copy(u_sb[:, n % 2], ps[3][:], sm["u_ok"])
                        if n >= GR:
                            act.wait_ge(*after("qs_ps", b, NU - 2, n - 2))
                            act.wait_ge(*after("ogT_ps", b, NU, n - 2))
                            copy(o_sb[:, n % 2], ps[4][:], sm["qc_ok"])
                    if n >= 1:
                        act.wait_ge(*after("ogT_ps", b, NU, n - 1))
                        if n >= 3:
                            act.wait_ge(*after("hp_ps", b, NU, n - 3))
                        copy(ogT[:, (n - 1) % 2], ps[7][:], sm["ogT_ok"])
                    if n < NU:
                        act.wait_ge(*after("g_ps", b, NU, n))
                        if n >= 2:
                            act.wait_ge(*after("og_ok", b, NU, n - 2))
                        A(gate_sb[:, n % 2], ps[6][:], ACT.Silu).then_inc(sm["gate_ok"], 1)

            def post_mT(b):
                act.wait_ge(sm["mT_ps"], b + 1)
                copy(mT, ps[6][:], sm["mT_ok"])

            def post_relu(b):
                for f in range(FC):
                    act.wait_ge(*after("fc_ps", b, FC, f))
                    A(fT[:, f], ps[6 + (f + 1) % 2][:], ACT.Relu).then_inc(sm["fr_ok"], 1)

            def post_aT(b):
                act.wait_ge(sm["aT_ps"], b + 1)
                copy(aT, ps[6][:], sm["aT_ok"])

            def post_sexp(b):
                act.wait_ge(sm["sm_ok"], b + 1)
                A(soft[:, 0:CH * HK], soft[:, 0:CH * HK], ACT.Exp).then_inc(sm["sexp_ok"], 1)

            def post_pT(b):
                act.wait_ge(sm["pT_ps"], b + 1)
                copy(pT[0:HK, :], ps[2][0:HK, :], sm["pT_ok"])

            def post_x2T(b):
                act.wait_ge(sm["x2T_ps"], b + 1)
                copy(x2T, ps[6][:], sm["x2T_ok"])

            def post_lexp(b):
                act.wait_ge(sm["lsub_ok"], b + 1)
                A(rt[:, 1], rt[:, 0], ACT.Exp).then_inc(sm["lexp_ok"], 1)

            setup()
            act.wait_ge(sm["ld_misc"], 64)
            A(neg_a[:], neg_a[:], ACT.Exp).then_inc(sm["u_exp"], 1)
            phase1(0)
            phase2a(0)
            t_levels(0)
            phase2b(0)
            with act.Fori(1, B) as b:
                phase1(b)
                phase2a(b)
                t_levels(b)
                phase2b(b)
            for stage in (post_mT, post_relu, post_aT, post_sexp, post_pT, post_x2T, post_lexp):
                stage(B - 1)

            act.wait_ge(sm["e_h_ok"], EG * HC)
            with act.Fori(0, E // EG) as ep:
                act.wait_ge(sm["e_h_ok"], (ep + 1) * EG * HC)
                A(moe_b1[:], b1T[:, bass.ds(ep * (EG * HC), EG * HC)], ACT.Copy).then_inc(sm["e_b_ok"], 1)
                for a in range(EG):
                    e = ep * EG + a
                    act.wait_ge(sm["e_xT_ps"], e + 1 + EG)
                    act.wait_ge(sm["e_o_ps"], e - 1 + EG)
                    copy(xeT[:, a % 2, 0:CAP], ps[0][:, 0:CAP], sm["e_xT_ok"])
                    if a == 0:
                        act.wait_ge(sm["e_b_ok"], ep + 1)
                    for f in range(HC):
                        act.wait_ge(*after("e_h_ps", e, HC, f))
                        A(hidT[:, a % 2, f, 0:CAP], ps[1 + f][:, 0:CAP], ACT.Gelu,
                          bias=moe_b1[:, a * HC + f:a * HC + f + 1]).then_inc(sm["e_h_ok"], 1)

        @block.vector
        def _(dve):
            tt, ts, stt = dve.tensor_tensor, dve.tensor_scalar, dve.scalar_tensor_tensor
            o_step = sm["o_step"]

            def setup():
                st = Steps(dve, dchain["set"], 0, 2)
                dve.wait_ge(sm["ld_const"], 16)
                dve.tensor_copy(ident_h[:], ident).then_inc(sm["consts_ok"], 1)
                dve.tensor_copy(neg_h[:], const[:, C_NEG:C_NEG + P]).then_inc(sm["consts_ok"], 1)
                dve.wait_ge(sm["setup_kv"], 1)
                dve.wait_ge(sm["ld_xattn"], 16 * (B * 2 + 7))
                k48, v48 = kT[:, 6, 0:B * NK], kT[:, 7, 0:B * NK]
                st.then(ts(k48, ps[4][:, 0:B * NK], inb[:, 1:2], None, ALU.add))
                st.then(ts(v48, ps[5][:, 0:B * NK], inb[:, 2:3], None, ALU.add))
                st.close()
                for i, src in enumerate((k48, v48)):
                    hm = const[:, C_HM + i * XH:C_HM + (i + 1) * XH]
                    for b in range(B):
                        tt(kT[:, 4 + i, b * HK:(b + 1) * HK].rearrange("p (h k) -> p h k", h=XH),
                           bc(src[:, b * NK:(b + 1) * NK].unsqueeze(1), [P, XH, NK]), bc(hm.unsqueeze(2), [P, XH, NK]),
                           ALU.mult).then_inc(sm["setup_blk"], 1)
                dve.wait_ge(sm["ld_w1"], 16 * 8)
                ts(w_o[:], w_o[:], onw[:, 0:1], None, ALU.mult).then_inc(sm["setup_done"], 1)

            def rows_scale(dst, src, r, done):
                for c in range(CH):
                    last = ts(dst[:, c, :], src[:, c, :], r[:, c:c + 1], None, ALU.mult)
                last.then_inc(done, 1)

            def phase1(b, post_st=None):
                st = Steps(dve, dchain["ph1"], b, PH1)
                dve.wait_ge(sm["ld_x"], b * 16 + 16)
                for c in range(CH):
                    last = dve.tensor_tensor_reduce(h_sb[:, c * P:(c + 1) * P], xin[:, c, :], xin[:, c, :], 1.0 / D, 1e-6, ALU.mult, ALU.add,
                                                    st4[:, 0, c:c + 1])
                last.then_inc(sm["ssh_ok"], 1)
                if post_st:
                    post_ssx(b - 1)
                dve.wait_ge(sm["rh_ok"], b + 1)
                rows_scale(h_sb.rearrange("p (c n) -> p c n", c=CH), xin, st4[:, 1], sm["h_ready"])
                if post_st:
                    post_m(b - 1)
                gg = lambda i: gates[:, i]
                dve.wait_ge(sm["gates_ps"], b + 1)
                if isinstance(b, int):
                    dve.wait_ge(sm["ld_misc"], 64)
                st.then(tt(gg(0).rearrange("p (c h) -> p c h", c=CH),
                           ps[1][:, 0:64].rearrange("p (c n) -> p c n", c=CH)[:, :, H:2 * H],
                           bc(dtb[:, :].unsqueeze(1), [P, CH, H]), ALU.add))
                st.then(ts(gg(2), gg(0), -1.0, None, ALU.mult))
                st.then(tt(gg(3), gg(0), gg(2), ALU.min))
                dve.wait_ge(sm["u_exp"], b * 2 + 3)
                st.then(ts(gg(5), gg(4), 2.0, None, ALU.add))
                st.then(dve.reciprocal(gg(6), gg(5)))
                st.then(tt(gg(7), gg(4), gg(6), ALU.mult))
                st.then(tt(gg(8), gg(7), gg(7), ALU.mult))
                st.then(ts(gg(9), gg(8), 1.0 / (2 * LOG1P_TERMS + 1), None, ALU.mult))
                for k in range(LOG1P_TERMS - 1, 0, -1):
                    st.then(stt(gg(9), gg(9), 1.0 / (2 * k + 1), gg(8), ALU.add, ALU.mult))
                st.then(stt(gg(10), gg(9), 1.0, gg(7), ALU.add, ALU.mult))
                st.then(ts(gg(11), gg(0), 0.0, None, ALU.max))
                st.then(stt(gg(12), gg(10), 2.0, gg(11), ALU.mult, ALU.add))
                st.then(stt(gg(13).rearrange("p (c h) -> p c h", c=CH), gg(12).rearrange("p (c h) -> p c h", c=CH), -1.0,
                            bc(neg_a[:, :].unsqueeze(1), [P, CH, H]), ALU.mult, ALU.mult))
                ts(g_all[:], gg(13), G_FLOOR, None, ALU.max).then_inc(sm["g_ready"], 1)
                st.then(ts(gg(14), gg(1), 1.0, None, ALU.add))
                dve.reciprocal(beta[:], gg(14)).then_inc(sm["egs_ok"], 1)
                st.close()
                for n in range(NU + 1):
                    if n < NU:
                        dve.wait_ge(*after("k_act", b, NU, n))
                        for h in range(HG):
                            kh = k_raw[:, n % 2, h * P:(h + 1) * P]
                            last = dve.tensor_tensor_reduce(kn[:, n, h * P:(h + 1) * P], kh, kh, 1.0, 1e-6, ALU.mult, ALU.add,
                                                            kss[:, n * HG + h:n * HG + h + 1])
                        last.then_inc(sm["k_sq"], 1)
                    if n >= 1:
                        m = n - 1
                        dve.wait_ge(*after("rk_ok", b, NU, m))
                        tt(heads(kn[:, m]), heads(k_raw[:, m % 2]),
                           bc(rk[:, m * HG:(m + 1) * HG].unsqueeze(2), [P, HG, P]), ALU.mult).then_inc(sm["kn_ok"], 1)
                    if post_st and n == 4:
                        post_a_stats(b - 1, post_st)
                    if post_st and n == 5:
                        post_a(b - 1)
                if post_st:
                    post_scores(b - 1, post_st)
                dve.wait_ge(sm["eg_ok"], b + 1)
                dve.wait_ge(*after("egs_ok", b, 3, 0))
                ts(neg_eg[:], eg[:, 0], -1.0, None, ALU.mult).then_inc(sm["egs_ok"], 1)
                tt(ekb[:], eg[:, 2], beta[:], ALU.mult).then_inc(sm["egs_ok"], 1)
                if post_st:
                    post_probs(b - 1, post_st)
                for n in range(NU):
                    dve.wait_ge(*after("dt_ok", b, NU, n))
                    dve.wait_ge(*after("kk_ps", b, NU, n))
                    tt(Nm[:, n * HG:(n + 1) * HG, :], heads(ps[n % 2][:]), heads(att[:, n]), ALU.mult).then_inc(sm["n_ok"], 1)
                    if post_st and n == 3:
                        post_x2_stats(b - 1, post_st)
                    if post_st and n == 5:
                        post_x2(b - 1)

            def eliminate(st, j):
                ni, ncol = BLK - 1 - j, j + 1
                pr = prod[:, 0:ni * ncol].rearrange("p (i c) -> p i c", i=ni)
                st.then(tt(pr, bc(blk_n[:, j, j + 1:].unsqueeze(2), [P, ni, ncol]),
                           bc(blk_t[:, j, 0:ncol].unsqueeze(1), [P, ni, ncol]), ALU.mult))
                st.then(tt(blk_t[:, j + 1:, 0:ncol], blk_t[:, j + 1:, 0:ncol], pr, ALU.subtract))

            def phase2a(b, post_st=None):
                st = Steps(dve, dchain["inv"], b, INV)
                if not isinstance(b, int):
                    dve.wait_ge(sm["t_stored"], b * 32)
                flat = blk_t[:, :, :].rearrange("p i c -> p (i c)")
                st.then(dve.memset(flat, 0.0))
                st.then(dve.memset(flat[:, 0:BLK * BLK:BLK + 1], 1.0))
                for n in range(NU):
                    dve.wait_ge(*after("qk_ps", b, NU, n))
                    tt(att[:, n], ps[4 + n % 2][:], att[:, n], ALU.mult).then_inc(sm["at_ok"], 1)
                    if post_st and n == 0:
                        post_logits(b - 1, post_st)
                    if post_st and n == 1:
                        post_choice(b - 1, post_st)
                    if post_st and n == 3:
                        post_slots(b - 1, post_st)
                    if n == 2:
                        dve.wait_ge(sm["n_back"], b * 16 + 16)
                    if n >= 2:
                        for j in range(5 * (n - 2) + (n - 2 > 0), min(BLK - 1, 5 * (n - 1) + 1)):
                            eliminate(st, j)
                st.close()
                dve.tensor_copy(blk_tt, blk_t[:, :, :].rearrange("p i c -> p c i")).then_inc(sm["t_ok"], 1)
                dve.wait_ge(*after("sq_ps", b, NU, NU - 1))
                ts(cq[:], ps[1][:, 0:NP], 1e-6, 1e-6 * P, ALU.add, ALU.mult).then_inc(sm["cq_ok"], 1)

            def rhs(b, n):
                dve.wait_ge(*after("ks_ps", b, NU - 2, n - 2))
                for h in range(HG):
                    col = slice(h * P, (h + 1) * P)
                    last = stt(vv[:, n, col], ps[1 + n % 2][:, col], neg_eg[:, n * HG + h:n * HG + h + 1], vv[:, n, col],
                               ALU.mult, ALU.add)
                last.then_inc(sm["r_ok"], 1)

            def gate_out(b, n):
                dve.wait_ge(*after("f_ok", b, NU, n))
                dve.wait_ge(*after("gate_ok", b, NU, n))
                for h in range(HG):
                    col = slice(h * P, (h + 1) * P)
                    last = stt(o_sb[:, n % 2, col], o_sb[:, n % 2, col], of[:, n * HG + h:n * HG + h + 1],
                               gate_sb[:, n % 2, col], ALU.mult, ALU.mult)
                last.then_inc(sm["og_ok"], 1)

            def phase2b(b):
                dve.wait_ge(*after("egs_ok", b, 3, 2))
                if not isinstance(b, int):
                    dve.wait_ge(sm["y_st"], b * 16)
                    dve.wait_ge(sm["scattered"], b * 2 * CH * 16)
                for n in range(NU + 1):
                    c, g = n // GR, n % GR
                    if GR <= n + 1 < NU:
                        rhs(b, n + 1)
                    if n >= 1:
                        gate_out(b, n - 1)
                    if n < NU:
                        dve.wait_ge(*after("au_ps", b, NU, n))
                        if n >= 2:
                            dve.wait_ge(*after("ogT_ps", b, NU, n - 2))
                        if c == 0:
                            dve.tensor_copy(o_sb[:, n % 2], ps[5][:]).then_inc(o_step, 1)
                        else:
                            dve.wait_ge(*after("qc_ok", b, NU - 2, n - 2))
                            for h in range(HG):
                                col = slice(h * P, (h + 1) * P)
                                last = stt(o_sb[:, n % 2, col], o_sb[:, n % 2, col], eg[:, 0, n * HG + h:n * HG + h + 1],
                                           ps[5][:, col], ALU.mult, ALU.add)
                            last.then_inc(o_step, 1)
                        if n < NU - 2:
                            dve.wait_ge(*after("ktu_ps", b, NU - 2, n))
                            if c == 0:
                                dve.tensor_copy(St[:, g], ps[6][:]).then_inc(sm["s_ok"], 1)
                            else:
                                for h in range(HG):
                                    col = slice(h * P, (h + 1) * P)
                                    last = stt(St[:, g, col], St[:, g, col], eg[:, 1, n * HG + h:n * HG + h + 1],
                                               ps[6][:, col], ALU.mult, ALU.add)
                                last.then_inc(sm["s_ok"], 1)
                        dve.wait_ge(o_step, b * NU + n + 1)
                        for h in range(HG):
                            oh = o_sb[:, n % 2, h * P:(h + 1) * P]
                            last = dve.tensor_tensor_reduce(x1[:, h, :], oh, oh, 1.0 / P, cq[:, n * HG + h:n * HG + h + 1],
                                                            ALU.mult, ALU.add, oss[:, n * HG + h:n * HG + h + 1])
                        last.then_inc(sm["o_ok"], 1)
                dve.wait_ge(*after("hp_ps", b, NU, NU - 1))
                dve.wait_ge(sm["x_kept"], b + 1)
                tt(x1[:], xres[:], ps[0][:].rearrange("p (c n) -> p c n", c=CH), ALU.add).then_inc(sm["x1_ok"], 1)

            def norm_stats(st, z, var, v_sem):
                for c in range(CH):
                    last = dve.bn_stats(bn[:, c, :], z[:, c, :])
                st.then(last, plain=True)
                for c in range(CH):
                    last = dve.bn_aggr(mv[:, c, :], bn[:, c, :])
                st.then(last)
                ts(var, mv[:, :, 1], 1e-5, None, ALU.add).then_inc(v_sem, 1)

            def norm_apply(z, rstd, dst, rs_sem, done, b):
                dve.wait_ge(rs_sem, b + 1)
                for c in range(CH):
                    ts(dst[:, c, :], z[:, c, :], mv[:, c, 0:1], rstd[:, c:c + 1], ALU.subtract, ALU.mult).then_inc(done, 1)

            def post_ssx(b):
                dve.wait_ge(sm["x1_ok"], b + 1)
                for c in range(CH):
                    last = dve.tensor_tensor_reduce(a1[:, c, :], x1[:, c, :], x1[:, c, :], 1.0 / D, 1e-6, ALU.mult, ALU.add,
                                                    st4[:, 2, c:c + 1])
                last.then_inc(sm["ssx_ok"], 1)

            def post_m(b):
                dve.wait_ge(sm["r1_ok"], b + 1)
                rows_scale(m_sb, x1, st4[:, 3], sm["m_ok"])

            def post_a_stats(b, st):
                dve.wait_ge(sm["y_ps"], b + 1)
                dve.wait_ge(sm["xx_ok"], b + 1)
                st.then(tt(a1[:], xx[:], ps[7][:].rearrange("p (c n) -> p c n", c=CH), ALU.add))
                norm_stats(st, a1, st4[:, 4], sm["v1_ok"])

            def post_a(b):
                norm_apply(a1, st4[:, 5], a1, sm["rs1_ok"], sm["a_ok"], b)

            def post_scores(b, st):
                sc = soft[:, 0:CH * HK]
                s3 = sc.rearrange("p (n k) -> p n k", k=NK)
                dve.wait_ge(sm["sc_ps"], b + 1)
                st.then(tt(sc, ps[7][:, 0:CH * HK], const[:, C_CNT:C_CNT + CH * HK], ALU.add))
                st.then(dve.tensor_reduce(rt[:, 0], s3, AX.X, ALU.max))
                tt(s3, s3, bc(rt[:, 0].unsqueeze(2), [P, CH * XH, NK]), ALU.subtract).then_inc(sm["sm_ok"], 1)

            def post_probs(b, st):
                s3 = soft[:, 0:CH * HK].rearrange("p (n k) -> p n k", k=NK)
                dve.wait_ge(sm["sexp_ok"], b + 1)
                st.then(dve.tensor_reduce(rt[:, 1], s3, AX.X, ALU.add))
                st.then(dve.reciprocal(rt[:, 2], rt[:, 1]))
                tt(s3, s3, bc(rt[:, 2].unsqueeze(2), [P, CH * XH, NK]), ALU.mult).then_inc(sm["p_ok"], 1)

            def post_x2_stats(b, st):
                dve.wait_ge(sm["xo_ps"], b + 1)
                st.then(tt(a1[:], a1[:], ps[3][:].rearrange("p (c n) -> p c n", c=CH), ALU.add))
                norm_stats(st, a1, st4[:, 6], sm["v2_ok"])

            def post_x2(b):
                norm_apply(a1, st4[:, 7], x2, sm["rs2_ok"], sm["x2_ok"], b)

            ce = lambda i: rt[:, i].rearrange("p (c e) -> p c e", c=CH)

            def post_logits(b, st):
                dve.wait_ge(sm["lg_ps"], b + 1)
                lg = ps[7][:, 0:CH * E].rearrange("p (c e) -> p c e", c=CH)
                st.then(dve.tensor_reduce(rt[:, 2, 0:CH], lg, AX.X, ALU.max))
                tt(ce(0), lg, bc(rt[:, 2, 0:CH].unsqueeze(2), [P, CH, E]), ALU.subtract).then_inc(sm["lsub_ok"], 1)

            def post_choice(b, st):
                dve.wait_ge(sm["lexp_ok"], b + 1)
                st.then(dve.tensor_reduce(rt[:, 3, 0:CH], ce(1), AX.X, ALU.add))
                st.then(dve.reciprocal(rt[:, 3, CH:2 * CH], rt[:, 3, 0:CH]))
                st.then(tt(ce(4), ce(1), bc(rt[:, 3, CH:2 * CH].unsqueeze(2), [P, CH, E]), ALU.mult), plain=True)
                for c in range(CH):
                    last = dve.max(top8[:, c, :], ce(4)[:, c, :])
                st.then(last, plain=True)
                for c in range(CH):
                    last = dve.max_index(top8i[:, c, :], top8[:, c, :], ce(4)[:, c, :])
                st.then(last)
                top_f = rt[:, 3, 0:2 * CH].rearrange("p (k c) -> p k c", k=2)
                st.then(dve.tensor_copy(top_f, top8i[:, :, 0:2].rearrange("p c k -> p k c")))
                for k in range(2):
                    last = tt(ce(5 + k), bc(iota8.unsqueeze(1), [P, CH, E]), bc(top_f[:, k].unsqueeze(2), [P, CH, E]),
                              ALU.is_equal)
                st.then(last)
                tt(rt[:, 7], rt[:, 5], rt[:, 6], ALU.add).then_inc(sm["mask_ok"], 1)

            def post_slots(b, st):
                dve.wait_ge(sm["cum_ps"], b + 1)
                st.then(stt(ce(10), ps[6][:, 0:CH * E].rearrange("p (c e) -> p c e", c=CH), -1.0,
                            bc(base[:, :].unsqueeze(1), [P, CH, E]), ALU.add, ALU.add))
                for k in range(2):
                    last = tt(ce(5 + k), ce(10), ce(5 + k), ALU.mult)
                st.then(last)
                st.then(dve.tensor_reduce(rt[:, 0, 0:E], ps[6][:, CH * E:2 * CH * E].rearrange("p (c e) -> p e c", c=CH),
                                          AX.X, ALU.add))
                tt(base[:], base[:], rt[:, 0, 0:E], ALU.add)
                both = lambda i, j: rt[:, i, j * 2 * CH:(j + 1) * 2 * CH]
                st.then(dve.tensor_reduce(both(11, 0), rt[:, 5:7].rearrange("p k (c e) -> p (k c) e", e=E), AX.X, ALU.add))
                pos = both(11, 0)
                ts(both(12, 0), pos, float(CAP), None, ALU.is_lt)
                st.then(ts(both(12, 2), rt[:, 3, 0:2 * CH], float(CAP), None, ALU.mult))
                valid = both(12, 0)
                tt(both(13, 0), pos, both(12, 2), ALU.add)
                st.then(ts(both(13, 1), valid, float(-2 * SLOTS), float(2 * SLOTS), ALU.mult, ALU.add))
                st.then(tt(both(13, 2), both(13, 0), both(13, 1), ALU.add))
                dve.tensor_copy(x2_rows[:, :, GATE:], ce(4))
                dve.tensor_copy(x2_rows[:, :, TOK:TOK + 1], const[:, bass.ds(C_TOK + b * CH, CH)].unsqueeze(2))
                if not isinstance(b, int) or b > 0:
                    dve.wait_ge(sm["scattered"], b * 2 * CH * 16)
                dve.tensor_copy(scat_i[:, :, :].rearrange("p k c -> p (k c)"), both(13, 2)).then_inc(sm["slots_ok"], 1)
                st.close()

            setup()
            dve.wait_ge(sm["base_ok"], 1)
            phase1(0)
            phase2a(0)
            phase2b(0)
            with dve.Fori(1, B) as b:
                post_st = Steps(dve, dchain["post"], b - 1, POST)
                phase1(b, post_st)
                phase2a(b, post_st)
                phase2b(b)
            post_st = Steps(dve, dchain["post"], B - 1, POST)
            post_ssx(B - 1)
            post_m(B - 1)
            post_a_stats(B - 1, post_st)
            post_a(B - 1)
            post_scores(B - 1, post_st)
            post_probs(B - 1, post_st)
            post_x2_stats(B - 1, post_st)
            post_x2(B - 1)
            post_logits(B - 1, post_st)
            post_choice(B - 1, post_st)
            post_slots(B - 1, post_st)

            with dve.Fori(0, E // EG) as ep:
                for a in range(EG):
                    e = ep * EG + a
                    dve.wait_ge(sm[f"e_x_ld{a}"], ep * 32 + 32)
                    dve.wait_ge(sm["e_added"], e + 1)
                    for t, (r0, n) in enumerate(SLOT_TILES):
                        dve.tensor_copy(tok_e[0:n, a, t:t + 1], xe[0:n, a, t, TOK:TOK + 1])
                        last = dve.tensor_copy(wgt_e[0:n, a, t:t + 1], xe[0:n, a, t, bass.ds(e + GATE, 1)])
                    last.then_inc(sm["w_e_ok"], 1)
                    dve.wait_ge(sm["w_e_ok"], e + 1)
                    dve.wait_ge(sm["e_o_ps"], e + 1 + EG)
                    dve.wait_ge(sm["e_added"], e - 1 + EG)
                    for t, (r0, n) in enumerate(SLOT_TILES):
                        last = ts(oe[0:n, a % 2, t, :], ps[5 + a % 2][0:n, t * P:(t + 1) * P], wgt_e[0:n, a, t:t + 1],
                                  None, ALU.mult)
                    last.then_inc(sm["e_o_ok"], 1)

            st = Steps(dve, dchain["fin"], 0, B * 2)
            for i in range(B):
                z, var, rstd = yf[:, i], st4[:, 2 * (i % 2)], st4[:, 2 * (i % 2) + 1]
                dve.wait_ge(f_x[i], 16)
                for c in range(CH):
                    last = dve.bn_stats(bn[:, c, :], z[:, c, :])
                st.then(last, plain=True)
                for c in range(CH):
                    last = dve.bn_aggr(mv[:, c, :], bn[:, c, :])
                st.then(last)
                ts(var, mv[:, :, 1], 1e-5, None, ALU.add).then_inc(sm["f_v"], 1)
                dve.wait_ge(sm["f_rs"], i + 1)
                for c in range(CH):
                    last = ts(z[:, c, :], z[:, c, :], mv[:, c, 0:1], rstd[:, c:c + 1], ALU.subtract, ALU.mult)
                last.then_inc(sm["f_y"], 1)
            st.close()


_INS = ["x", "ctx_1024", "L0_attn_Wq", "L0_attn_Wk", "L0_attn_Wv", "L0_attn_Wb", "L0_attn_Wa", "L0_attn_A_log",
        "L0_attn_dt_bias", "L0_attn_Wg", "L0_attn_o_norm_w", "L0_attn_Wo", "L0_attn_W_fc", "L0_attn_W_proj",
        "L0_xattn_in_proj_w", "L0_xattn_in_proj_b", "L0_xattn_out_w", "L0_xattn_out_b", "L0_ffn_router_w",
        "L0_ffn_router_b", "L0_ffn_w1", "L0_ffn_b1", "L0_ffn_w2", "L0_ffn_b2"]


def kernel(**inputs):
    import numpy as _np
    import concourse.bacc as _bacc
    from concourse import mybir as _mybir
    from concourse.bass_utils import run_bass_kernel_spmd as _run

    nc = _bacc.Bacc("TRN2", target_bir_lowering=False, num_devices=1)
    f32 = _mybir.dt.float32
    arrays, args = {}, []
    for name in _INS:
        a = _np.ascontiguousarray(inputs[name])
        arrays[f"in_{name}"] = a
        args.append(nc.dram_tensor(f"in_{name}", a.shape, _mybir.dt.from_np(a.dtype), kind="ExternalInput").ap())
    arrays["shape_table"] = shape_constants()
    args.append(nc.dram_tensor("shape_table", (P, C_END), f32, kind="ExternalInput").ap())
    for name, shape in (("n_blocks", (NP, NBLK, BLK, BLK)), ("t_blocks", (NP, NBLK, BLK, BLK)),
                        ("tt_blocks", (NP, NBLK, BLK, BLK)), ("y_rows", (B * S, D)), ("slots", (SLOTS, ROW))):
        args.append(nc.dram_tensor(name, shape, f32, kind="Internal").ap())
    args.append(nc.dram_tensor("out_0", (B, S, D), f32, kind="ExternalOutput").ap())
    decoder_kernel(nc, *args)
    r = _run(nc, [arrays], core_ids=[0])
    return r.results[0]["out_0"]
```

```python
from contextlib import ExitStack

import numpy as np

import concourse.bass as bass
from concourse import mybir

F32 = mybir.dt.float32
BF16 = mybir.dt.bfloat16
I32 = mybir.dt.int32
U32 = mybir.dt.uint32
ALU = mybir.AluOpType
ACT = mybir.ActivationFunctionType
AX = mybir.AxisListType

P = 128
B, S, D, H = 4, 512, 128, 8
CH = S // P
HG = 4
GR = H // HG
NU = CH * GR
NP = CH * H
BLK = 32
NBLK = P // BLK
DFF = 512
FC = DFF // P
CTX = 154
KEYS = list(range(11)) + [CTX - 1]
NK = len(KEYS)
XH = 8
XD = D // XH
HK = XH * NK
E = 8
CAP = 320
SLOTS = E * CAP
HID = 512
HC = HID // P
NT = B * CH
SLOT_TILES = [(0, 128), (128, 128), (256, 64)]
NEG = -30000.0
G_FLOOR = -200.0
LOG1P_TERMS = 8
PH1, PH1_Z = 20, 3
INV = 2 + 4 * (BLK - 2) + 1
HALF_PROD = 17 * 8
POST = 25

C_ID, C_LE, C_GT, C_NEG = 0, P, 2 * P, 3 * P
C_HM = 4 * P
C_IOTA = C_HM + 2 * XH
C_CNT = C_IOTA + E
C_TOK = C_CNT + CH * HK
C_END = C_TOK + B * CH
TOK, GATE = D, D + 1
ROW = D + 1 + E
NO_TOKEN = 4.0 * B * S
EG = 4


def shape_constants():
    t = np.zeros((P, C_END), np.float32)
    r = np.arange(P)
    t[:, C_ID:C_ID + P] = np.eye(P)
    t[:, C_LE:C_LE + P] = r[:, None] <= r[None, :]
    t[:, C_GT:C_GT + P] = r[:, None] > r[None, :]
    t[:, C_NEG:C_NEG + P] = np.where(r[:, None] > r[None, :], NEG, 0.0)
    hm = (r[:, None] // XD) == np.arange(XH)[None, :]
    t[:, C_HM:C_HM + XH] = hm / np.sqrt(XD)
    t[:, C_HM + XH:C_HM + 2 * XH] = hm
    t[:, C_IOTA:C_IOTA + E] = np.arange(E)
    for tok in range(S):
        rows = [i for i in range(-4, 4) if 0 <= tok + i < S]
        while len(rows) < 8:
            if tok + len(rows) < S:
                rows.append(tok + len(rows))
            else:
                rows.insert(0, tok - (8 - len(rows)))
        hit = [min(p % S, CTX - 1) for p in rows]
        count = [hit.count(k) for k in KEYS]
        row = [np.log(n) if n else -1e30 for n in count]
        c = C_CNT + (tok // P) * HK
        t[tok % P, c:c + HK] = row * XH
    t[:, C_TOK:C_END] = np.arange(NT)[None, :] * P + r[:, None]
    return t


def decoder_kernel(nc, x, ctx_in, Wq, Wk, Wv, Wb, Wa, A_log, dt_bias, Wg, o_norm_w, Wo, W_fc, W_proj,
                   in_w, in_b, out_w, out_b, router_w, router_b, w1, b1, w2, b2, table,
                   n_dram, t_dram, tt_dram, y_dram, slots_dram, out):
    with ExitStack() as ctx:
        def sb(name, shape, dt=F32):
            return ctx.enter_context(nc.sbuf_tensor(name, shape, dt))

        def sem(name):
            return ctx.enter_context(nc.semaphore(name))

        const = sb("const", [P, C_END])
        ident, le, gt = const[:, C_ID:C_ID + P], const[:, C_LE:C_LE + P], const[:, C_GT:C_GT + P]
        iota8 = const[:, C_IOTA:C_IOTA + E]
        ident_h, neg_h = sb("ident_h", [P, P], BF16), sb("neg_h", [P, P], BF16)
        ones = sb("ones", [P, P])
        mhalf = sb("mhalf", [P, 16])
        w_qkvg = sb("w_qkvg", [P, 4, H * P])
        w_ba = sb("w_ba", [P, 2 * H])
        dtb = sb("dtb", [P, H])
        neg_a = sb("neg_a", [P, H])
        w_o = sb("w_o", [P, H, P])
        onw = sb("onw", [P, 1])
        w_fc = sb("w_fc", [P, DFF])
        w_pr = sb("w_pr", [P, FC, P])
        outb = sb("outb", [1, P])
        w_r = sb("w_r", [P, E])
        rb = sb("rb", [1, E])
        xattn_m = sb("xattn_m", [P, B * HK])
        xattn_b = sb("xattn_b", [1, B * HK])
        xattn_vo = sb("xattn_vo", [HK, B * P])

        xin = sb("xin", [P, CH, P])
        xres = sb("xres", [P, CH, P])
        hT = sb("hT", [P, CH * P])
        x1 = sb("x1", [P, CH, P])
        xx = sb("xx", [P, CH, P])
        kn = sb("kn", [P, NU, HG * P])
        kT = sb("kT", [P, NU, HG * P])
        att = sb("att", [P, NU, HG * P])
        Nm = sb("Nm", [P, NP, P])
        Tm = sb("Tm", [P, NP, 2 * BLK])
        TT = sb("TT", [P, NP, P])
        qT = sb("qT", [P, NU, HG * P])
        vv = sb("vv", [P, NU, HG * P])
        St = sb("St", [P, GR, HG * P])
        gates = sb("gates", [P, 16, NP])
        eg = sb("eg", [P, 3, NP])
        neg_eg = sb("neg_eg", [P, NP])
        ekb = sb("ekb", [P, NP])
        beta = sb("beta", [P, NP])
        g_all = sb("g_all", [P, NP])
        kss = sb("kss", [P, NP])
        rk = sb("rk", [P, NP])
        cq = sb("cq", [P, NP])
        oss = sb("oss", [P, NP])
        of = sb("of", [P, NP])
        st4 = sb("st4", [P, 8, CH])
        bn = sb("bn", [P, CH, 6])
        mv = sb("mv", [P, CH, 2])
        blk_t = sb("blk_t", [P, BLK, BLK])
        prod = sb("prod", [P, 2 * HALF_PROD])
        p_lo = sb("p_lo", [P, NP, BLK])
        work = sb("work", [P, 3, 2, HG * P])
        gate_sb = sb("gate_sb", [P, 2, HG * P])
        k_raw = work[:, 0:2].rearrange("p a b n -> p (a b) n")
        gm = work[:, 2]
        qsq = work[:, 2]
        Tc = work[:, 0].rearrange("p a n -> p (a n)").rearrange("p (q n) -> p q n", n=BLK)
        TTc = work[:, 1].rearrange("p a n -> p (a n)").rearrange("p (q n) -> p q n", n=BLK)
        u_sb = work[:, 0]
        o_sb = work[:, 1]
        ogT = work[:, 2]
        h_sb = p_lo[:, 0:16, :].rearrange("p q n -> p (q n)")
        blk_n = St[:, :, :].rearrange("p a b -> p (a b)").rearrange("p (i j) -> p i j", i=BLK)
        blk_tt = gate_sb[:, :, :].rearrange("p a b -> p (a b)").rearrange("p (i j) -> p i j", i=BLK)
        fT = vv[:, 4:8]
        mT = p_lo[:, 16:32, :].rearrange("p q n -> p (q n)")
        a1 = sb("a1", [P, CH, P])
        aT = mT
        pT = mT
        soft = x1[:, :, :].rearrange("p c n -> p (c n)")
        x2_rows = sb("x2_rows", [P, CH, ROW])
        x2 = x2_rows[:, :, 0:D]
        m_sb = x2
        x2T = p_lo[:, 0:16, :].rearrange("p q n -> p (q n)")
        rt = sb("rt", [P, 14, CH * E])
        top8 = sb("top8", [P, CH, 8])
        top8i = sb("top8i", [P, CH, 8], U32)
        base = sb("base", [P, E])
        scat_i = sb("scat_i", [P, 2, CH], I32)
        moe_w1 = kn[:, 0:EG]
        moe_w2 = kn[:, EG:2 * EG].rearrange("p a (c n) -> p a c n", c=HC)
        moe_b1 = sb("moe_b1", [P, EG * HC])
        moe_b2 = sb("moe_b2", [1, E, P])
        xe = qT[:, 0:EG, 0:3 * ROW].rearrange("p a (t d) -> p a t d", t=3)
        xeT = kT[:, 0:2]
        hidT = att[:, 0:8].rearrange("p (a c) n -> p a c n", a=2)
        oe = kT[:, 2:4, 0:3 * P].rearrange("p a (t d) -> p a t d", t=3)
        tok_e = sb("tok_e", [P, EG, 3], I32)
        wgt_e = sb("wgt_e", [P, EG, 3])
        mvf = rt[:, 0:2, 0:2 * CH].rearrange("p a (c t) -> p a c t", t=2)
        yf = vv[:, 0:B].rearrange("p a (c n) -> p a c n", c=CH)
        empty = qT[:, :, :].rearrange("p a n -> p (a n)")[:, 0:4 * ROW]
        ctx48 = vv[0:B * NK, 0, 0:P]
        bias_rows = vv[0:E * HC + 3, 1, 0:P]
        inw = vv[:, 2, 0:3 * P].rearrange("p (s d) -> p s d", s=3)
        outw = vv[:, 3, 0:P]
        bias_T = sb("bias_T", [P, E * HC + 3])
        b1T, inb = bias_T[:, 0:E * HC], bias_T[:, E * HC:]

        ps = [ctx.enter_context(nc.psum_tensor(f"ps{i}", [P, 512], F32)) for i in range(8)]

        names = """ld_const ld_wk ld_w1 ld_x ld_misc ld_xattn zeroed consts_ok setup_tr setup_cp setup_kv setup_blk setup_m setup_done
        base_ok x_kept h_ready hT_ps hT_ok gates_ps g_ready u_exp eg_ps eg_ok egs_ok o_step k_ps k_act k_sq rk_ok kn_ok kT_ps kT_ok
        gm_ok e_ps dt_exp  kk_ps n_ok n_stored n_back t_ok t_stored tt_stored t_back tt_back td_ok q_ps q_ok q_sq sq_ps cq_ok v_ps v_ok qk_ps at_ok
        kd_ok l1_ps l1_ok l2_ps l2_ok l3_ps l3_ok l4_ps l4_ok ks_ps r_ok tr_ps u_ok qs_ps qc_ok au_ps o_ok f_ok og_ok ogT_ps ogT_ok
        g_ps gate_ok ktu_ps s_ok hp_ps x1_ok xx_ok ssx_ok r1_ok m_ok mT_ps mT_ok fc_ps fr_ok f2_ok y_ps  v1_ok rs1_ok a_ok aT_ps
        aT_ok sc_ps sm_ok sexp_ok p_ok pT_ps pT_ok xo_ps v2_ok rs2_ok x2_ok y_st x2T_ps x2T_ok lg_ps lsub_ok lexp_ok mask_ok
        cum_ps slots_ok scattered ssh_ok rh_ok
        e_w_ld0 e_w_ld1 e_w_ld2 e_w_ld3 e_x_ld0 e_x_ld1 e_x_ld2 e_x_ld3 e_b_ok e_xT_ps e_xT_ok e_h_ps e_h_ok e_o_ps e_o_ok
        w_e_ok row_added e_added empty_0 emptied f_v f_rs f_y f_out""".split()
        sm = {n: sem(n) for n in names}
        dchain, pchain = {}, {}
        f_x = [sem(f"f_x{i}") for i in range(B)]
        for ph in ("set", "ph1", "inv", "post", "fin"):
            dchain[ph] = sem(f"dve_step_{ph}")

        class Steps:
            def __init__(self, eng, s, b, per):
                self.eng, self.s, self.b, self.per, self.k = eng, s, b, per, 0

            def then(self, ins, plain=False):
                self.k += 1
                ins.then_inc(self.s, 1)
                if plain:
                    wait_apart(self.eng, self.s, self.b * self.per + self.k)
                else:
                    self.eng.wait_ge(self.s, self.b * self.per + self.k)

            def step(self, ins):
                self.k += 1
                ins.then_inc(self.s, 1)
                return self.value()

            def value(self):
                return self.b * self.per + self.k

            def close(self):
                assert self.k == self.per, (self.k, self.per)

        def after(name, b, per, k):
            return sm[name], b * per + k + 1

        def wait_apart(eng, s, value):
            if not isinstance(value, int):
                value = eng.to_reg(value)
                eng.wait_ge(sm["ld_const"], 16)
            eng.wait_ge(s, value)

        def bc(ap, shape):
            return ap.to_broadcast(shape)

        def heads(ap):
            return ap.rearrange("p (h n) -> p h n", h=HG)

        block = ctx.enter_context(nc.Block())

        @block.sync
        def _(sp):
            sp.dma_start(const[:], table).then_inc(sm["ld_const"], 16)
            sp.dma_start(xin[:], x[0].rearrange("(c p) d -> p c d", p=P)).then_inc(sm["ld_x"], 16)
            sp.dma_start(w_ba[:, 0:H], Wb).then_inc(sm["ld_misc"], 16)
            sp.dma_start(w_ba[:, H:2 * H], Wa).then_inc(sm["ld_misc"], 16)
            sp.dma_start(dtb[:], dt_bias.partition_broadcast(P)).then_inc(sm["ld_misc"], 16)
            sp.dma_start(neg_a[:], A_log.partition_broadcast(P)).then_inc(sm["ld_misc"], 16)
            sp.dma_start(w_qkvg[:, 1, :], Wk).then_inc(sm["ld_wk"], 16)
            for i, w in ((0, Wq), (2, Wv), (3, Wg)):
                sp.dma_start(w_qkvg[:, i, :], w).then_inc(sm["ld_w1"], 16)
            sp.dma_start(w_o[:], Wo.rearrange("(h p) n -> p h n", p=P)).then_inc(sm["ld_w1"], 16)
            sp.dma_start(onw[:], o_norm_w.rearrange("(p o) -> p o", o=1)).then_inc(sm["ld_w1"], 16)
            sp.dma_start(w_fc[:], W_fc).then_inc(sm["ld_w1"], 16)
            sp.dma_start(w_pr[:], W_proj.rearrange("(f p) n -> p f n", p=P)).then_inc(sm["ld_w1"], 16)
            sp.dma_start(moe_b2[:], b2.rearrange("(o e) n -> o e n", o=1)).then_inc(sm["ld_w1"], 16)
            sp.wait_ge(sm["zeroed"], 1)
            erows = slots_dram.rearrange("(k p r) d -> k p (r d)", p=P, r=4)
            for k in range(SLOTS // (4 * P)):
                sp.dma_start(erows[k], empty).then_inc(sm["emptied"], 16)

            for b in range(B):
                sp.dma_start(ctx48[b * NK:b * NK + NK - 1, :], ctx_in[b, 0:NK - 1, :]).then_inc(sm["ld_xattn"], 16)
                sp.dma_start(ctx48[b * NK + NK - 1:(b + 1) * NK, :], ctx_in[b, CTX - 1:CTX, :]).then_inc(sm["ld_xattn"], 16)
            sp.dma_start(inw, in_w.rearrange("(s e) d -> e s d", e=P)).then_inc(sm["ld_xattn"], 16)
            sp.dma_start(bias_rows[E * HC:, :], in_b.rearrange("(s e) -> s e", e=P)).then_inc(sm["ld_xattn"], 16)
            sp.dma_start(bias_rows[0:E * HC, :], b1.rearrange("e (c p) -> (e c) p", p=P)).then_inc(sm["ld_xattn"], 16)
            sp.dma_start(outw, out_w).then_inc(sm["ld_xattn"], 16)
            sp.dma_start(outb[:], out_b.rearrange("(o n) -> o n", o=1)).then_inc(sm["ld_xattn"], 16)
            sp.dma_start(w_r[:], router_w).then_inc(sm["ld_xattn"], 16)
            sp.dma_start(rb[:], router_b.rearrange("(o n) -> o n", o=1)).then_inc(sm["ld_xattn"], 16)

            def exchange_n(b):
                sp.wait_ge(*after("n_ok", b, NU, NU - 1))
                for r in range(NBLK):
                    sp.dma_start(n_dram[:, r].rearrange("q i j -> i q j"),
                                 Nm[BLK * r:BLK * r + BLK, :, BLK * r:BLK * r + BLK]).then_inc(sm["n_stored"], 16)
                sp.wait_ge(sm["n_stored"], b * 64 + 64)
                sp.dma_start(blk_n, n_dram.rearrange("q r i j -> (q r) i j")).then_inc(sm["n_back"], 16)

            def exchange_t(b):
                sp.wait_ge(*after("t_ok", b, 2, 0))
                sp.dma_start(t_dram.rearrange("q r i j -> (q r) i j"), blk_t[:]).then_inc(sm["t_stored"], 16)
                sp.wait_ge(*after("t_ok", b, 2, 1))
                sp.dma_start(tt_dram.rearrange("q r i j -> (q r) i j"), blk_tt).then_inc(sm["tt_stored"], 16)
                sp.wait_ge(sm["t_stored"], b * 16 + 16)
                sp.dma_start(Tc, t_dram.rearrange("q r i j -> (r i) q j")).then_inc(sm["t_back"], 16)
                sp.wait_ge(sm["tt_stored"], b * 16 + 16)
                sp.dma_start(TTc, tt_dram.rearrange("q r i j -> (r i) q j")).then_inc(sm["tt_back"], 16)

            def next_x(b):
                sp.wait_ge(sm["x_kept"], b)
                sp.wait_ge(sm["h_ready"], b)
                sp.dma_start(xin[:], x[b].rearrange("(c p) d -> p c d", p=P)).then_inc(sm["ld_x"], 16)

            def store_x2(b):
                sp.wait_ge(*after("x2_ok", b, CH, CH - 1))
                y_b = y_dram[b * S:(b + 1) * S] if isinstance(b, int) else y_dram[bass.ds(b * S, S)]
                sp.dma_start(y_b.rearrange("(c p) d -> p c d", p=P), x2).then_inc(sm["y_st"], 16)

            exchange_n(0)
            exchange_t(0)
            with sp.Fori(1, B) as b:
                next_x(b)
                exchange_n(b)
                exchange_t(b)
                store_x2(b - 1)
            store_x2(B - 1)

            sp.sem_inc(sm["e_o_ps"], EG)
            sp.sem_inc(sm["e_xT_ps"], EG)
            sp.sem_inc(sm["e_xT_ok"], 1)
            sp.sem_inc(sm["e_h_ok"], EG * HC)
            sp.sem_inc(sm["e_o_ok"], EG)
            sp.sem_inc(sm["e_added"], EG)

            def load_weights(ep, a):
                e = ep * EG + a
                sp.wait_ge(sm["e_o_ps"], e + 1)
                s = sm[f"e_w_ld{a}"]
                sp.dma_start(moe_w1[:, a], w1[e]).then_inc(s, 16)
                sp.dma_start(moe_w2[:, a], w2[e].rearrange("(c p) n -> p c n", p=P)).then_inc(s, 16)

            def load_rows(ep, a):
                e = ep * EG + a
                s = sm[f"e_x_ld{a}"]
                sp.wait_ge(sm["e_xT_ps"], e + 1)
                sp.wait_ge(sm["e_o_ok"], e + 1)
                sp.dma_start(xe[:, a, 0:2], slots_dram[bass.ds(e * CAP, 2 * P)].rearrange("(t p) d -> p t d", p=P)).then_inc(s, 16)
                sp.dma_start(xe[0:CAP - 2 * P, a, 2], slots_dram[bass.ds(e * CAP + 2 * P, CAP - 2 * P)]).then_inc(s, 16)

            sp.wait_ge(sm["s_ok"], B * (NU - 2))
            sp.wait_ge(sm["o_ok"], B * NU)
            sp.wait_ge(sm["hp_ps"], B * NU)
            for a in range(EG):
                load_weights(0, a)
            sp.wait_ge(sm["scattered"], B * 2 * CH * 16)
            for a in range(EG):
                load_rows(0, a)
            with sp.Fori(1, E // EG) as ep:
                for a in range(EG):
                    load_weights(ep, a)
                    load_rows(ep, a)
            sp.wait_ge(sm["e_added"], EG + E)
            for i in range(B):
                sp.dma_start(yf[:, i], y_dram[i * S:(i + 1) * S].rearrange("(c p) d -> p c d", p=P)).then_inc(f_x[i], 16)
            for i in range(B):
                sp.wait_ge(sm["f_y"], i + 1)
                sp.dma_start(out[i].rearrange("(c p) d -> p c d", p=P), yf[:, i]).then_inc(sm["f_out"], 16)
            sp.wait_ge(sm["f_out"], B * 16)

        @block.gpsimd
        def _(pool):
            pool.memset(ones[:], 1.0).then_inc(sm["consts_ok"], 1)
            pool.memset(mhalf[:], -0.5).then_inc(sm["consts_ok"], 1)
            pool.memset(empty, 0.0).then_inc(sm["empty_0"], 1)
            pool.wait_ge(sm["empty_0"], 1)
            pool.memset(empty[:, TOK:4 * ROW:ROW], NO_TOKEN).then_inc(sm["zeroed"], 1)
            pool.memset(Tm[:], 0.0).then_inc(sm["zeroed"], 1)
            pool.memset(TT[:], 0.0).then_inc(sm["zeroed"], 1)
            pool.memset(base[:], 0.0).then_inc(sm["base_ok"], 1)

            def power(out_ap, in_ap, done, n):
                pool.tensor_tensor(out_ap, in_ap, mhalf[:, 0:n], ALU.pow).then_inc(done, 1)

            def head_r(b):
                pool.wait_ge(sm["ssh_ok"], b + 1)
                power(st4[:, 1], st4[:, 0], sm["rh_ok"], CH)

            def phase1(b):
                first = isinstance(b, int)
                for n in range(NU):
                    pool.wait_ge(*after("k_sq", b, NU, n))
                    power(rk[:, n * HG:(n + 1) * HG], kss[:, n * HG:(n + 1) * HG], sm["rk_ok"], HG)
                    if n == 1 and not first:
                        post_r1(b - 1)
                    if n == 2 and not first:
                        pool.wait_ge(sm["x1_ok"], b)
                        pool.tensor_tensor(xx[:], xres[:], x1[:], ALU.add).then_inc(sm["xx_ok"], 1)
                    if n == 3:
                        wait_apart(pool, sm["ld_x"], b * 16 + 16)
                        if not first:
                            pool.wait_ge(sm["xx_ok"], b)
                        pool.tensor_copy(xres[:], xin[:]).then_inc(sm["x_kept"], 1)
                pool.wait_ge(sm["g_ready"], b + 1)
                for n in range(NU):
                    if n >= 2:
                        pool.wait_ge(*after("e_ps", b, NU, n - 2))
                    pool.tensor_tensor(heads(gm[:, n % 2]), bc(gt.unsqueeze(1), [P, HG, P]),
                                       bc(g_all[:, n * HG:(n + 1) * HG].unsqueeze(2), [P, HG, P]),
                                       ALU.mult).then_inc(sm["gm_ok"], 1)
                    if n == 4 and not first:
                        post_rs1(b - 1)
                for n in range(NU):
                    if n == 1 and not first:
                        post_rs2(b - 1)
                    pool.wait_ge(*after("q_ok", b, NU, n))
                    if n >= 2:
                        pool.wait_ge(*after("sq_ps", b, NU, n - 2))
                    pool.tensor_tensor(qsq[:, n % 2], qT[:, n], qT[:, n], ALU.mult).then_inc(sm["q_sq"], 1)
                    if n == 0:
                        pool.wait_ge(*after("egs_ok", b, 3, 2))
                        pool.wait_ge(*after("kT_ps", b, NU, NU - 1))
                    if n < NU - GR:
                        pool.tensor_tensor(heads(kn[:, n]), heads(kn[:, n]),
                                           bc(ekb[:, n * HG:(n + 1) * HG].unsqueeze(2), [P, HG, P]),
                                           ALU.mult).then_inc(sm["kd_ok"], 1)
                if not first:
                    for c in range(CH):
                        post_scatter(b - 1, c)

            def phase2b(b, nxt=None):
                for n in range(NU):
                    pool.wait_ge(*after("o_ok", b, NU, n))
                    power(of[:, n * HG:(n + 1) * HG], oss[:, n * HG:(n + 1) * HG], sm["f_ok"], HG)
                    if nxt is not None and n == NU - 2:
                        head_r(nxt)

            def post_r1(b):
                pool.wait_ge(sm["ssx_ok"], b + 1)
                power(st4[:, 3], st4[:, 2], sm["r1_ok"], CH)

            def post_rs1(b):
                pool.wait_ge(sm["v1_ok"], b + 1)
                power(st4[:, 5], st4[:, 4], sm["rs1_ok"], CH)

            def post_rs2(b):
                pool.wait_ge(sm["v2_ok"], b + 1)
                power(st4[:, 7], st4[:, 6], sm["rs2_ok"], CH)

            def post_scatter(b, c):
                if c == 0:
                    wait_apart(pool, sm["slots_ok"], b + 1)
                for k in range(2):
                    pool.indirect_dma_start(
                        slots_dram, bass.IndirectOffsetOnAxis(ap=scat_i[:, k, c:c + 1], axis=0),
                        x2_rows[:, c, :], None, bounds_check=SLOTS - 1, oob_is_err=False,
                    ).then_inc(sm["scattered"], 16)

            head_r(0)
            phase1(0)
            pool.wait_ge(sm["emptied"], 16 * (SLOTS // (4 * P)))
            with pool.Fori(1, B) as b:
                phase2b(b - 1, b)
                phase1(b)
            phase2b(B - 1)
            post_r1(B - 1)
            pool.wait_ge(sm["x1_ok"], B)
            pool.tensor_tensor(xx[:], xres[:], x1[:], ALU.add).then_inc(sm["xx_ok"], 1)
            post_rs1(B - 1)
            post_rs2(B - 1)
            for c in range(CH):
                post_scatter(B - 1, c)

            def scatter_rows(ep, a):
                e = ep * EG + a
                wait_apart(pool, sm["e_o_ok"], e + 1 + EG)
                for t, (r0, n) in enumerate(SLOT_TILES):
                    pool.indirect_dma_start(
                        y_dram, bass.IndirectOffsetOnAxis(ap=tok_e[0:n, a, t:t + 1], axis=0),
                        oe[0:n, a % 2, t, :], None, bounds_check=B * S - 1, oob_is_err=False, compute_op=ALU.add,
                    ).then_inc(sm["row_added"], 16)
                pool.wait_ge(sm["row_added"], e * 48 + 48)
                pool.sem_inc(sm["e_added"], 1)

            pool.wait_ge(sm["y_st"], B * 16)
            with pool.Fori(0, E // EG) as ep:
                for a in range(EG):
                    scatter_rows(ep, a)
            for i in range(B):
                pool.wait_ge(sm["f_v"], i + 1)
                power(st4[:, 2 * (i % 2) + 1], st4[:, 2 * (i % 2)], sm["f_rs"], CH)

        @block.tensor
        def _(pe):
            mm = nc.tensor.matmul

            def transpose(out_ap, in_ap, n=P):
                return nc.tensor.transpose(out_ap, in_ap, ident[0:n, 0:n])

            def setup():
                pe.wait_ge(*after("kT_ok", 0, NU, NU - 1))
                pe.wait_ge(*after("n_ok", 0, NU, NU - 1))
                pe.wait_ge(*after("k_act", 0, NU, NU - 1))
                pe.wait_ge(sm["ld_xattn"], 16 * (B * 2 + 7))
                transpose(ps[4][:, 0:B * NK], ctx48, B * NK)
                transpose(ps[3][:, 0:E * HC + 3], bias_rows, E * HC + 3)
                transpose(ps[5][:, 0:P], inw[:, 1, :])
                transpose(ps[6][:, 0:P], inw[:, 2, :])
                transpose(ps[7][:, 0:P], outw).then_inc(sm["setup_tr"], 1)
                pe.wait_ge(sm["setup_cp"], 5)
                ctxT, wkT, wvT, woT = (qT[:, i, 0:P] for i in range(4))
                mm(ps[4][:, 0:B * NK], wkT, ctxT[:, 0:B * NK], start=True, stop=True)
                mm(ps[5][:, 0:B * NK], wvT, ctxT[:, 0:B * NK], start=True, stop=True).then_inc(sm["setup_kv"], 1)
                pe.wait_ge(sm["setup_blk"], 2 * B + 1)
                kblk, vblk = qT[:, 4, 0:B * HK], qT[:, 5, 0:B * HK]
                mm(ps[6][:, 0:B * HK], inw[:, 0, :], kblk, start=True, stop=True)
                mm(ps[7][0:1, 0:B * HK], inb[:, 0:1], kblk, start=True, stop=True)
                for b in range(B):
                    mm(ps[4][0:HK, b * P:(b + 1) * P], vblk[:, b * HK:(b + 1) * HK], woT, start=True, stop=False,
                       skip_group_check=True)
                    last = mm(ps[4][0:HK, b * P:(b + 1) * P], ones[0:1, 0:HK], outb[:], start=False, stop=True,
                              skip_group_check=True)
                last.then_inc(sm["setup_m"], 1)
                pe.wait_ge(sm["setup_done"], 4)

            def k_proj(b, n):
                c, g = n // GR, n % GR
                if n >= 2:
                    pe.wait_ge(*after("k_act", b, NU, n - 2))
                mm(ps[2 + n % 2][:], hT[:, c * P:(c + 1) * P], w_qkvg[:, 1, g * 512:(g + 1) * 512],
                   start=True, stop=True).then_inc(sm["k_ps"], 1)

            def k_transpose(b, n):
                pe.wait_ge(*after("kn_ok", b, NU, n))
                if n >= 2:
                    pe.wait_ge(*after("kT_ok", b, NU, n - 2))
                for h in range(HG):
                    last = transpose(ps[4 + n % 2][:, h * P:(h + 1) * P], kn[:, n, h * P:(h + 1) * P])
                last.then_inc(sm["kT_ps"], 1)

            def head_hT(b):
                pe.wait_ge(sm["h_ready"], b + 1)
                for c in range(CH):
                    last = transpose(ps[6][:, c * P:(c + 1) * P], h_sb[:, c * P:(c + 1) * P])
                last.then_inc(sm["hT_ps"], 1)

            def head_gates(b):
                pe.wait_ge(sm["hT_ok"], b + 1)
                for c in range(CH):
                    last = mm(ps[1][:, c * 16:(c + 1) * 16], hT[:, c * P:(c + 1) * P], w_ba[:], start=True, stop=True)
                last.then_inc(sm["gates_ps"], 1)

            def phase1(b):
                first = isinstance(b, int) and b == 0
                for n in range(2, NU + 3):
                    if n < NU:
                        k_proj(b, n)
                    if n == 3 and not first:
                        pe.wait_ge(sm["x1_ok"], b)
                        post_mT(b - 1)
                    if n >= 3:
                        k_transpose(b, n - 3)
                    if not first:
                        if 3 <= n < 3 + FC:
                            post_fc(b - 1, n - 3)
                        if n >= NU:
                            pe.wait_ge(*after("k_act", b, NU, NU - 1))
                            post_y(b - 1, range(2 * (n - NU), min(CH, 2 * (n - NU) + 2)))
                pe.wait_ge(sm["g_ready"], b + 1)
                if first:
                    pe.wait_ge(sm["consts_ok"], 4)
                for i, tri in enumerate((le, ones[:], gt)):
                    last = mm(ps[1][:, 64 + i * NP:64 + (i + 1) * NP], tri, g_all[:], start=True, stop=True)
                last.then_inc(sm["eg_ps"], 1)
                for n in range(NU + 1):
                    if n < NU:
                        e = ps[6 + n % 2]
                        if n >= 2:
                            pe.wait_ge(*after("dt_exp", b, NU, n - 2))
                        elif not first:
                            pe.wait_ge(sm["f2_ok"], b * FC)
                        pe.wait_ge(*after("gm_ok", b, NU, n))
                        for h in range(HG):
                            mm(e[:, h * P:(h + 1) * P], ident_h[:], neg_h[:], start=True, stop=False, skip_group_check=True)
                            last = mm(e[:, h * P:(h + 1) * P], gm[:, n % 2, h * P:(h + 1) * P], le,
                                      start=False, stop=True, skip_group_check=True)
                        last.then_inc(sm["e_ps"], 1)
                    if n >= 1:
                        kk_gram(b, n - 1)
                    if not first:
                        if n == 6:
                            post_aT(b - 1)
                        if n == 7:
                            post_sc(b - 1)

            def kk_gram(b, n):
                pe.wait_ge(*after("kT_ok", b, NU, n))
                if n >= 2:
                    pe.wait_ge(*after("n_ok", b, NU, n - 2))
                if n == 1:
                    pe.wait_ge(sm["eg_ok"], b + 1)
                for h in range(HG):
                    kh = kT[:, n, h * P:(h + 1) * P]
                    last = mm(ps[n % 2][:, h * P:(h + 1) * P], kh, kh, start=True, stop=True)
                last.then_inc(sm["kk_ps"], 1)

            def phase2a(b):
                if isinstance(b, int) and b == 0:
                    pe.wait_ge(sm["ld_w1"], 16 * 8)
                pe.wait_ge(*after("k_act", b, NU, NU - 1))
                pe.wait_ge(*after("n_ok", b, NU, NU - 1))
                first = isinstance(b, int)
                if not first:
                    pe.wait_ge(sm["sm_ok"], b)
                    pe.wait_ge(*after("dt_exp", b, NU, NU - 1))
                    post_pT(b - 1)
                    post_xo(b - 1)
                for n in range(NU + 1):
                    if n < NU:
                        c, g = n // GR, n % GR
                        if n >= 1:
                            pe.wait_ge(*after("q_ok", b, NU, n - 1))
                        for h in range(HG):
                            hh = (g * HG + h) * P
                            last = mm(ps[2][:, h * P:(h + 1) * P], w_qkvg[:, 0, hh:hh + P], hT[:, c * P:(c + 1) * P],
                                      start=True, stop=True)
                        last.then_inc(sm["q_ps"], 1)
                        if n >= 1:
                            pe.wait_ge(*after("v_ok", b, NU, n - 1))
                        mm(ps[3][:], hT[:, c * P:(c + 1) * P], w_qkvg[:, 2, g * 512:(g + 1) * 512],
                           start=True, stop=True).then_inc(sm["v_ps"], 1)
                    if n >= 1:
                        m = n - 1
                        pe.wait_ge(*after("q_sq", b, NU, m))
                        for h in range(HG):
                            last = mm(ps[1][:, m * HG + h:m * HG + h + 1], qsq[:, m % 2, h * P:(h + 1) * P],
                                      ones[:, 0:1], start=True, stop=True)
                        last.then_inc(sm["sq_ps"], 1)
                        if m < 4:
                            qk_gram(b, m)
                if not first:
                    pe.wait_ge(*after("v_ok", b, NU, NU - 1))
                for m in range(4, NU):
                    qk_gram(b, m)
                    if m == 5 and not first:
                        post_x2T(b - 1)
                if not first:
                    post_lg(b - 1)

            def qk_gram(b, m):
                pe.wait_ge(*after("q_ok", b, NU, m))
                if m >= 4:
                    pe.wait_ge(*after("at_ok", b, NU, m - 4))
                elif m == 0:
                    pe.wait_ge(*after("kT_ok", b, NU, NU - 1))
                    pe.wait_ge(*after("dt_exp", b, NU, NU - 1))
                for h in range(HG):
                    last = mm(ps[4 + m % 4][:, h * P:(h + 1) * P], kT[:, m, h * P:(h + 1) * P],
                              qT[:, m, h * P:(h + 1) * P], start=True, stop=True)
                last.then_inc(sm["qk_ps"], 1)

            def t_levels(b):
                wait_apart(pe, sm["t_back"], b * 16 + 16)
                pe.wait_ge(*after("v_ok", b, NU, NU - 1))
                pe.wait_ge(*after("at_ok", b, NU, NU - 1))
                pe.wait_ge(*after("dt_exp", b, NU, NU - 1))
                for half in range(2):
                    for q in range(16 * half, 16 * half + 16):
                        col = (q % 16) * BLK
                        for lo in (0, 64):
                            hi = lo + BLK
                            last = mm(ps[2 + half][hi:hi + BLK, col:col + BLK], Nm[lo:lo + BLK, q, hi:hi + BLK],
                                      Tc[lo:lo + BLK, q, :], start=True, stop=True, skip_group_check=True)
                    last.then_inc(sm["l1_ps"], 1)
                for half in range(2):
                    wait_apart(pe, *after("l1_ok", b, 4, 2 * half + 1))
                    if half == 0:
                        pe.wait_ge(sm["tt_back"], b * 16 + 16)
                    for q in range(16 * half, 16 * half + 16):
                        col = (q % 16) * BLK
                        mm(ps[4 + half][BLK:2 * BLK, col:col + BLK], TTc[BLK:2 * BLK, q, :],
                           p_lo[BLK:2 * BLK, q, :], start=True, stop=True, skip_group_check=True)
                        for lo in (0, 64):
                            hi = lo + BLK
                            last = mm(ps[6 + half][lo:lo + BLK, col:col + BLK], p_lo[hi:hi + BLK, q, :],
                                      TTc[hi:hi + BLK, q, :], start=True, stop=True, skip_group_check=True)
                    last.then_inc(sm["l2_ps"], 1)
                if not isinstance(b, int):
                    post_cum(b - 1)
                banks = [2, 3, 4, 5]
                wait_apart(pe, sm["td_ok"], b + 1)
                wait_apart(pe, *after("l2_ok", b, 6, 5))
                for i in range(4):
                    for q in range(8 * i, 8 * i + 8):
                        col = (q % 8) * 64
                        last = mm(ps[banks[i]][64:P, col:col + 64], Nm[0:64, q, 64:P], Tm[0:64, q, :],
                                  start=True, stop=True, skip_group_check=True)
                    last.then_inc(sm["l3_ps"], 1)
                for i in range(4):
                    wait_apart(pe, *after("l3_ok", b, 4, i))
                    p64 = p_lo[64:P].rearrange("p q n -> p (q n)").rearrange("p (q n) -> p q n", n=64)
                    if i >= 2:
                        wait_apart(pe, *after("l4_ok", b, 4, i - 2))
                    for q in range(8 * i, 8 * i + 8):
                        col = (q % 8) * 64
                        last = mm(ps[6 + i % 2][0:64, col:col + 64], p64[:, q % 16, :], TT[64:P, q, 64:P],
                                  start=True, stop=True, skip_group_check=True)
                    last.then_inc(sm["l4_ps"], 1)

            def unit_mm(bank, n, lhs, rhs, done):
                for h in range(HG):
                    last = mm(ps[bank][:, h * P:(h + 1) * P], lhs(h), rhs(h), start=True, stop=True)
                last.then_inc(done, 1)

            def out_transpose(b, n):
                if n >= 1:
                    pe.wait_ge(*after("ogT_ok", b, NU, n - 1))
                pe.wait_ge(*after("og_ok", b, NU, n))
                for h in range(HG):
                    last = transpose(ps[7][:, h * P:(h + 1) * P], o_sb[:, n % 2, h * P:(h + 1) * P])
                last.then_inc(sm["ogT_ps"], 1)

            def out_proj(b, n):
                pe.wait_ge(*after("ogT_ok", b, NU, n))
                c, g = n // GR, n % GR
                for h in range(HG):
                    hh = g * HG + h
                    last = mm(ps[0][:, c * P:(c + 1) * P], ogT[:, n % 2, h * P:(h + 1) * P], w_o[:, hh, :],
                              start=(hh == 0), stop=(hh == H - 1), skip_group_check=True)
                last.then_inc(sm["hp_ps"], 1)

            def phase2b(b, nxt=None):
                pe.wait_ge(*after("l4_ok", b, 4, 3))
                pe.wait_ge(sm["cq_ok"], b + 1)
                for n in range(NU):
                    c, g = n // GR, n % GR
                    hs = lambda h: slice(h * P, (h + 1) * P)
                    if n >= GR:
                        pe.wait_ge(*after("r_ok", b, NU - GR, n - GR))
                    if n >= 1:
                        pe.wait_ge(*after("u_ok", b, NU, n - 1))
                    unit_mm(3, n, lambda h: TT[:, c * H + g * HG + h, :], lambda h: vv[:, n, hs(h)], sm["tr_ps"])
                    if c > 0:
                        if n > GR:
                            pe.wait_ge(*after("qc_ok", b, NU - GR, n - GR - 1))
                        unit_mm(4, n, lambda h: qT[:, n, hs(h)], lambda h: St[:, g, hs(h)], sm["qs_ps"])
                    if GR <= n + 1 < NU:
                        if n >= GR:
                            pe.wait_ge(*after("r_ok", b, NU - GR, n - GR))
                        pe.wait_ge(*after("s_ok", b, NU - GR, n + 1 - GR))
                        unit_mm(1, n, lambda h: kT[:, n + 1, hs(h)], lambda h: St[:, (n + 1) % GR, hs(h)], sm["ks_ps"])
                    pe.wait_ge(*after("u_ok", b, NU, n))
                    if n >= 1:
                        pe.wait_ge(sm["o_step"], b * NU + n)
                    unit_mm(5, n, lambda h: att[:, n, hs(h)], lambda h: u_sb[:, n % 2, hs(h)], sm["au_ps"])
                    if n < NU - GR:
                        if n >= 1:
                            pe.wait_ge(*after("s_ok", b, NU - GR, n - 1))
                        pe.wait_ge(*after("kd_ok", b, NU - GR, n))
                        unit_mm(6, n, lambda h: kn[:, n, hs(h)], lambda h: u_sb[:, n % 2, hs(h)], sm["ktu_ps"])
                    if n >= 1:
                        out_transpose(b, n - 1)
                    if n >= 1:
                        pe.wait_ge(*after("gate_ok", b, NU, n - 1))
                    mm(ps[2][:], hT[:, c * P:(c + 1) * P], w_qkvg[:, 3, g * 512:(g + 1) * 512],
                       start=True, stop=True).then_inc(sm["g_ps"], 1)
                    if n >= 1:
                        out_proj(b, n - 1)
                if nxt is not None:
                    head_hT(nxt)
                    head_gates(nxt)
                    pe.wait_ge(*after("gate_ok", b, NU, NU - 1))
                    pe.wait_ge(*after("u_ok", b, NU, NU - 1))
                    k_proj(nxt, 0)
                    k_proj(nxt, 1)
                out_transpose(b, NU - 1)
                out_proj(b, NU - 1)

            def post_mT(b):
                pe.wait_ge(sm["m_ok"], b + 1)
                for c in range(CH):
                    last = transpose(ps[6][:, c * P:(c + 1) * P], m_sb[:, c, :])
                last.then_inc(sm["mT_ps"], 1)

            def post_fc(b, f):
                if f == 0:
                    pe.wait_ge(sm["mT_ok"], b + 1)
                if f >= 2:
                    pe.wait_ge(*after("fr_ok", b, FC, f - 2))
                mm(ps[6 + (f + 1) % 2][:], w_fc[:, f * P:(f + 1) * P], mT, start=True, stop=True).then_inc(sm["fc_ps"], 1)

            def post_y(b, tiles=range(CH)):
                pe.wait_ge(*after("f2_ok", b, FC, FC - 1))
                for c in tiles:
                    for f in range(FC):
                        last = mm(ps[2][:, c * P:(c + 1) * P], fT[:, f, c * P:(c + 1) * P], w_pr[:, f, :],
                                  start=(f == 0), stop=(f == FC - 1), skip_group_check=True)
                    if c == CH - 1:
                        last.then_inc(sm["y_ps"], 1)

            def post_aT(b):
                pe.wait_ge(*after("a_ok", b, CH, CH - 1))
                for c in range(CH):
                    last = transpose(ps[2][:, c * P:(c + 1) * P], a1[:, c, :])
                last.then_inc(sm["aT_ps"], 1)

            def post_sc(b):
                pe.wait_ge(sm["aT_ok"], b + 1)
                off = b * HK
                for c in range(CH):
                    mm(ps[3][:, c * HK:(c + 1) * HK], aT[:, c * P:(c + 1) * P], xattn_m[:, bass.ds(off, HK)],
                       start=True, stop=False, skip_group_check=True)
                    last = mm(ps[3][:, c * HK:(c + 1) * HK], ones[0:1, :], xattn_b[:, bass.ds(off, HK)],
                              start=False, stop=True, skip_group_check=True)
                last.then_inc(sm["sc_ps"], 1)

            def post_pT(b):
                pe.wait_ge(sm["p_ok"], b + 1)
                for c in range(CH):
                    last = transpose(ps[6][0:HK, c * P:(c + 1) * P], soft[:, c * HK:(c + 1) * HK])
                last.then_inc(sm["pT_ps"], 1)

            def post_xo(b):
                pe.wait_ge(sm["pT_ok"], b + 1)
                for c in range(CH):
                    last = mm(ps[0][:, c * P:(c + 1) * P], pT[0:HK, c * P:(c + 1) * P], xattn_vo[:, bass.ds(b * P, P)],
                              start=True, stop=True)
                last.then_inc(sm["xo_ps"], 1)

            def post_x2T(b):
                pe.wait_ge(*after("x2_ok", b, CH, CH - 1))
                for c in range(CH):
                    last = transpose(ps[3][:, c * P:(c + 1) * P], x2[:, c, :])
                last.then_inc(sm["x2T_ps"], 1)

            def post_lg(b):
                pe.wait_ge(sm["x2T_ok"], b + 1)
                for c in range(CH):
                    mm(ps[0][:, c * E:(c + 1) * E], x2T[:, c * P:(c + 1) * P], w_r[:], start=True, stop=False,
                       skip_group_check=True)
                    last = mm(ps[0][:, c * E:(c + 1) * E], ones[0:1, :], rb[:], start=False, stop=True,
                              skip_group_check=True)
                last.then_inc(sm["lg_ps"], 1)

            def post_cum(b):
                pe.wait_ge(sm["mask_ok"], b + 1)
                mask = rt[:, 7]
                mm(ps[0][:, 64:64 + CH * E], le, mask, start=True, stop=False, skip_group_check=True)
                for s in range(1, CH):
                    mm(ps[0][:, 64 + s * E:64 + CH * E], ones[:], mask[:, 0:(CH - s) * E], start=False, stop=(s == CH - 1),
                       skip_group_check=True)
                mm(ps[0][:, 64 + CH * E:64 + 2 * CH * E], ones[:], mask, start=True, stop=True,
                   skip_group_check=True).then_inc(sm["cum_ps"], 1)

            pe.wait_ge(sm["ld_const"], 16)
            head_hT(0)
            pe.wait_ge(sm["ld_misc"], 64)
            head_gates(0)
            pe.wait_ge(sm["ld_wk"], 16)
            k_proj(0, 0)
            k_proj(0, 1)
            phase1(0)
            setup()
            phase2a(0)
            t_levels(0)
            with pe.Fori(1, B) as b:
                phase2b(b - 1, b)
                phase1(b)
                phase2a(b)
                t_levels(b)
                pe.wait_ge(sm["slots_ok"], b)
            phase2b(B - 1)
            pe.wait_ge(sm["x1_ok"], B)
            post_mT(B - 1)
            for f in range(FC):
                post_fc(B - 1, f)
            for stage in (post_y, post_aT, post_sc, post_pT, post_xo, post_x2T, post_lg, post_cum):
                stage(B - 1)

            def expert_rows(ep, a):
                e = ep * EG + a
                pe.wait_ge(sm[f"e_x_ld{a}"], ep * 32 + 32)
                pe.wait_ge(sm["e_xT_ok"], e + 1)
                for t, (r0, n) in enumerate(SLOT_TILES):
                    last = transpose(ps[0][:, r0:r0 + n], xe[0:n, a, t, 0:D], n)
                last.then_inc(sm["e_xT_ps"], 1)

            pe.wait_ge(sm["slots_ok"], B)
            with pe.Fori(0, E // EG) as ep:
                expert_rows(ep, 0)
                for a in range(EG):
                    e = ep * EG + a
                    pe.wait_ge(sm["e_xT_ok"], e + 2)
                    pe.wait_ge(sm[f"e_w_ld{a}"], ep * 32 + 32)
                    for f in range(HC):
                        pe.wait_ge(sm["e_h_ok"], (e + EG - 1) * HC + f + 1)
                        mm(ps[1 + f][:, 0:CAP], moe_w1[:, a, f * P:(f + 1) * P], xeT[:, a % 2, 0:CAP],
                           start=True, stop=True).then_inc(sm["e_h_ps"], 1)
                    if a + 1 < EG:
                        expert_rows(ep, a + 1)
                    pe.wait_ge(sm["e_o_ok"], e + EG - 1)
                    for t, (r0, n) in enumerate(SLOT_TILES):
                        mm(ps[5 + a % 2][:, t * P:(t + 1) * P], ones[0:1, :], moe_b2[:, bass.ds(e, 1), :].rearrange("p o n -> p (o n)"),
                           start=True, stop=False, skip_group_check=True)
                        for f in range(HC):
                            if t == 0:
                                pe.wait_ge(sm["e_h_ok"], (e + EG) * HC + f + 1)
                            last = mm(ps[5 + a % 2][0:n, t * P:(t + 1) * P], hidT[:, a % 2, f, r0:r0 + n],
                                      moe_w2[:, a, f, :], start=False, stop=(f == HC - 1), skip_group_check=True)
                    last.then_inc(sm["e_o_ps"], 1)

        @block.scalar
        def _(act):
            A = nc.scalar.activation

            def copy(out_ap, in_ap, done):
                A(out_ap, in_ap, ACT.Copy).then_inc(done, 1)

            def setup():
                act.wait_ge(sm["emptied"], 16 * (SLOTS // (4 * P)))
                act.wait_ge(sm["setup_tr"], 1)
                for i, n in enumerate((B * NK, P, P, P)):
                    copy(qT[:, i, 0:n], ps[4 + i][:, 0:n], sm["setup_cp"])
                copy(bias_T[:], ps[3][:, 0:E * HC + 3], sm["setup_cp"])
                act.wait_ge(sm["setup_m"], 1)
                copy(xattn_m[:], ps[6][:, 0:B * HK], sm["setup_done"])
                copy(xattn_b[:], ps[7][0:1, 0:B * HK], sm["setup_done"])
                copy(xattn_vo[:], ps[4][0:HK, :], sm["setup_done"])

            def head_hT(b):
                act.wait_ge(sm["hT_ps"], b + 1)
                copy(hT[:], ps[6][:], sm["hT_ok"])

            def k_silu(b, n):
                act.wait_ge(*after("k_ps", b, NU, n))
                if n >= 4:
                    act.wait_ge(*after("kn_ok", b, NU, n - 4))
                A(k_raw[:, n % 4], ps[2 + n % 2][:], ACT.Silu).then_inc(sm["k_act"], 1)

            def gate_exps(b):
                act.wait_ge(dchain["ph1"], b * PH1 + 1)
                A(gates[:, 1].rearrange("p (c h) -> p c h", c=CH),
                  ps[1][:, 0:64].rearrange("p (c n) -> p c n", c=CH)[:, :, 0:H], ACT.Exp, scale=-1.0).then_inc(sm["u_exp"], 1)
                act.wait_ge(dchain["ph1"], b * PH1 + PH1_Z)
                A(gates[:, 4], gates[:, 3], ACT.Exp).then_inc(sm["u_exp"], 1)

            def phase1(b):
                first = isinstance(b, int)
                gate_exps(b)
                for n in range(2, NU + 3):
                    if n < NU:
                        k_silu(b, n)
                    if n == 3 and not first:
                        post_mT(b - 1)
                    if n >= 3:
                        kT_copy(b, n - 3)
                    if 3 <= n < 3 + FC and not first:
                        post_relu2(b - 1, n - 3)
                act.wait_ge(sm["eg_ps"], b + 1)
                A(eg[:, :, :].rearrange("p a n -> p (a n)"), ps[1][:, 64:64 + 3 * NP], ACT.Exp).then_inc(sm["eg_ok"], 1)
                for n in range(NU):
                    act.wait_ge(*after("e_ps", b, NU, n))
                    A(att[:, n], ps[6 + n % 2][:], ACT.Exp).then_inc(sm["dt_exp"], 1)
                    if n == 6 and not first:
                        post_aT(b - 1)
                if not first:
                    post_sexp(b - 1)

            def kT_copy(b, n):
                act.wait_ge(*after("kT_ps", b, NU, n))
                copy(kT[:, n], ps[4 + n % 2][:], sm["kT_ok"])

            def phase2a(b):
                if not isinstance(b, int):
                    post_pT(b - 1)
                for n in range(NU):
                    act.wait_ge(*after("q_ps", b, NU, n))
                    A(qT[:, n], ps[2][:], ACT.Silu).then_inc(sm["q_ok"], 1)
                    act.wait_ge(*after("v_ps", b, NU, n))
                    A(vv[:, n], ps[3][:], ACT.Silu).then_inc(sm["v_ok"], 1)
                if not isinstance(b, int):
                    post_x2T(b - 1)
                    post_lexp(b - 1)

            def t_levels(b):
                for half in range(2):
                    act.wait_ge(*after("l1_ps", b, 2, half))
                    for hi in (32, 96):
                        copy(p_lo[hi:hi + BLK, 16 * half:16 * half + 16, :],
                             ps[2 + half][hi:hi + BLK, :].rearrange("p (q n) -> p q n", n=BLK), sm["l1_ok"])
                for half in range(2):
                    act.wait_ge(*after("l2_ps", b, 2, half))
                    qs = slice(16 * half, 16 * half + 16)
                    A(Tm[BLK:2 * BLK, qs, 0:BLK], ps[4 + half][BLK:2 * BLK, :].rearrange("p (q n) -> p q n", n=BLK),
                      ACT.Copy, scale=-1.0).then_inc(sm["l2_ok"], 1)
                    for lo in (0, 64):
                        hi = lo + BLK
                        A(TT[lo:lo + BLK, qs, hi:hi + BLK], ps[6 + half][lo:lo + BLK, :].rearrange("p (q n) -> p q n", n=BLK),
                          ACT.Copy, scale=-1.0).then_inc(sm["l2_ok"], 1)
                p64 = p_lo[64:P].rearrange("p q n -> p (q n)").rearrange("p (q n) -> p q n", n=64)
                for i in range(4):
                    act.wait_ge(*after("l3_ps", b, 4, i))
                    if i >= 2:
                        act.wait_ge(*after("l4_ps", b, 4, i - 2))
                    copy(p64[:, 8 * (i % 2):8 * (i % 2) + 8, :], ps[2 + i][64:P, :].rearrange("p (q n) -> p q n", n=64), sm["l3_ok"])
                    if i >= 1:
                        l4_copy(b, i - 1)
                l4_copy(b, 3)

            def l4_copy(b, i):
                act.wait_ge(*after("l4_ps", b, 4, i))
                A(TT[0:64, 8 * i:8 * i + 8, 64:P], ps[6 + i % 2][0:64, :].rearrange("p (q n) -> p q n", n=64),
                  ACT.Copy, scale=-1.0).then_inc(sm["l4_ok"], 1)

            def phase2b(b, nxt=None):
                for n in range(NU + 1):
                    if n == NU and nxt is not None:
                        head_hT(nxt)
                        k_silu(nxt, 0)
                        k_silu(nxt, 1)
                    if n < NU:
                        act.wait_ge(*after("tr_ps", b, NU, n))
                        if n >= 2:
                            act.wait_ge(*after("au_ps", b, NU, n - 2))
                        copy(u_sb[:, n % 2], ps[3][:], sm["u_ok"])
                        if n >= GR:
                            act.wait_ge(*after("qs_ps", b, NU - 2, n - 2))
                            act.wait_ge(*after("ogT_ps", b, NU, n - 2))
                            copy(o_sb[:, n % 2], ps[4][:], sm["qc_ok"])
                    if n >= 1:
                        act.wait_ge(*after("ogT_ps", b, NU, n - 1))
                        if n >= 3:
                            act.wait_ge(*after("hp_ps", b, NU, n - 3))
                        copy(ogT[:, (n - 1) % 2], ps[7][:], sm["ogT_ok"])
                    if n < NU:
                        act.wait_ge(*after("g_ps", b, NU, n))
                        if n >= 2:
                            act.wait_ge(*after("og_ok", b, NU, n - 2))
                        A(gate_sb[:, n % 2], ps[2][:], ACT.Silu).then_inc(sm["gate_ok"], 1)

            def post_mT(b):
                act.wait_ge(sm["mT_ps"], b + 1)
                copy(mT, ps[6][:], sm["mT_ok"])

            def post_relu2(b, f):
                act.wait_ge(*after("fc_ps", b, FC, f))
                A(fT[:, f], ps[6 + (f + 1) % 2][:], ACT.Relu).then_inc(sm["fr_ok"], 1)
                act.wait_ge(*after("fr_ok", b, FC, f))
                A(fT[:, f], fT[:, f], ACT.Square).then_inc(sm["f2_ok"], 1)

            def post_aT(b):
                act.wait_ge(sm["aT_ps"], b + 1)
                copy(aT, ps[2][:], sm["aT_ok"])

            def post_sexp(b):
                act.wait_ge(sm["sm_ok"], b + 1)
                A(soft[:, 0:CH * HK], soft[:, 0:CH * HK], ACT.Exp).then_inc(sm["sexp_ok"], 1)

            def post_pT(b):
                act.wait_ge(sm["pT_ps"], b + 1)
                copy(pT[0:HK, :], ps[6][0:HK, :], sm["pT_ok"])

            def post_x2T(b):
                act.wait_ge(sm["x2T_ps"], b + 1)
                copy(x2T, ps[3][:], sm["x2T_ok"])

            def post_lexp(b):
                act.wait_ge(sm["lsub_ok"], b + 1)
                A(rt[:, 1], rt[:, 0], ACT.Exp).then_inc(sm["lexp_ok"], 1)

            act.wait_ge(sm["ld_misc"], 64)
            A(neg_a[:], neg_a[:], ACT.Exp).then_inc(sm["u_exp"], 1)
            head_hT(0)
            k_silu(0, 0)
            k_silu(0, 1)
            phase1(0)
            setup()
            phase2a(0)
            t_levels(0)
            with act.Fori(1, B) as b:
                phase2b(b - 1, b)
                phase1(b)
                phase2a(b)
                t_levels(b)
            phase2b(B - 1)
            post_mT(B - 1)
            for f in range(FC):
                post_relu2(B - 1, f)
            for stage in (post_aT, post_sexp, post_pT, post_x2T, post_lexp):
                stage(B - 1)

            act.wait_ge(sm["e_h_ok"], EG * HC)
            with act.Fori(0, E // EG) as ep:
                act.wait_ge(sm["e_h_ok"], (ep + 1) * EG * HC)
                A(moe_b1[:], b1T[:, bass.ds(ep * (EG * HC), EG * HC)], ACT.Copy).then_inc(sm["e_b_ok"], 1)
                for a in range(EG):
                    e = ep * EG + a
                    act.wait_ge(sm["e_xT_ps"], e + 1 + EG)
                    act.wait_ge(sm["e_o_ps"], e - 1 + EG)
                    copy(xeT[:, a % 2, 0:CAP], ps[0][:, 0:CAP], sm["e_xT_ok"])
                    if a == 0:
                        act.wait_ge(sm["e_b_ok"], ep + 1)
                    for f in range(HC):
                        act.wait_ge(*after("e_h_ps", e, HC, f))
                        A(hidT[:, a % 2, f, 0:CAP], ps[1 + f][:, 0:CAP], ACT.Gelu,
                          bias=moe_b1[:, a * HC + f:a * HC + f + 1]).then_inc(sm["e_h_ok"], 1)

        @block.vector
        def _(dve):
            tt, ts, stt = dve.tensor_tensor, dve.tensor_scalar, dve.scalar_tensor_tensor
            o_step = sm["o_step"]

            def setup():
                st = Steps(dve, dchain["set"], 0, 2)
                dve.wait_ge(sm["setup_kv"], 1)
                dve.wait_ge(sm["ld_xattn"], 16 * (B * 2 + 7))
                k48, v48 = qT[:, 6, 0:B * NK], qT[:, 7, 0:B * NK]
                st.then(ts(k48, ps[4][:, 0:B * NK], inb[:, 1:2], None, ALU.add))
                st.then(ts(v48, ps[5][:, 0:B * NK], inb[:, 2:3], None, ALU.add))
                st.close()
                for i, src in enumerate((k48, v48)):
                    hm = const[:, C_HM + i * XH:C_HM + (i + 1) * XH]
                    for b in range(B):
                        tt(qT[:, 4 + i, b * HK:(b + 1) * HK].rearrange("p (h k) -> p h k", h=XH),
                           bc(src[:, b * NK:(b + 1) * NK].unsqueeze(1), [P, XH, NK]), bc(hm.unsqueeze(2), [P, XH, NK]),
                           ALU.mult).then_inc(sm["setup_blk"], 1)
                ts(outb[:], outb[:], 1.0 / XH, None, ALU.mult).then_inc(sm["setup_blk"], 1)
                dve.wait_ge(sm["ld_w1"], 16 * 8)
                ts(w_o[:], w_o[:], onw[:, 0:1], None, ALU.mult).then_inc(sm["setup_done"], 1)

            def rows_scale(dst, src, r, done):
                for c in range(CH):
                    last = ts(dst[:, c, :], src[:, c, :], r[:, c:c + 1], None, ALU.mult)
                last.then_inc(done, 1)

            def k_squares(b, n):
                dve.wait_ge(*after("k_act", b, NU, n))
                for h in range(HG):
                    kh = k_raw[:, n % 4, h * P:(h + 1) * P]
                    last = dve.tensor_tensor_reduce(kn[:, n, h * P:(h + 1) * P], kh, kh, 1.0, 1e-6, ALU.mult, ALU.add,
                                                    kss[:, n * HG + h:n * HG + h + 1])
                last.then_inc(sm["k_sq"], 1)

            def head_ss(b):
                dve.wait_ge(sm["ld_x"], b * 16 + 16)
                for c in range(CH):
                    last = dve.tensor_tensor_reduce(h_sb[:, c * P:(c + 1) * P], xin[:, c, :], xin[:, c, :], 1.0 / D, 1e-6, ALU.mult, ALU.add,
                                                    st4[:, 0, c:c + 1])
                last.then_inc(sm["ssh_ok"], 1)

            def head_h(b):
                dve.wait_ge(sm["rh_ok"], b + 1)
                rows_scale(h_sb.rearrange("p (c n) -> p c n", c=CH), xin, st4[:, 1], sm["h_ready"])

            def gate_steps(b, st, part):
                gg = lambda i: gates[:, i]
                if part == 0:
                    dve.wait_ge(sm["gates_ps"], b + 1)
                    if isinstance(b, int):
                        dve.wait_ge(sm["ld_misc"], 64)
                    st.then(tt(gg(0).rearrange("p (c h) -> p c h", c=CH),
                               ps[1][:, 0:64].rearrange("p (c n) -> p c n", c=CH)[:, :, H:2 * H],
                               bc(dtb[:, :].unsqueeze(1), [P, CH, H]), ALU.add))
                    st.then(ts(gg(2), gg(0), -1.0, None, ALU.mult))
                    st.then(tt(gg(3), gg(0), gg(2), ALU.min))
                elif part == 1:
                    dve.wait_ge(sm["u_exp"], b * 2 + 3)
                    st.then(ts(gg(5), gg(4), 2.0, None, ALU.add))
                    st.then(dve.reciprocal(gg(6), gg(5)))
                    st.then(tt(gg(7), gg(4), gg(6), ALU.mult))
                elif part == 2:
                    st.then(tt(gg(8), gg(7), gg(7), ALU.mult))
                    st.then(ts(gg(9), gg(8), 1.0 / (2 * LOG1P_TERMS + 1), None, ALU.mult))
                elif part <= 5:
                    for k in range(LOG1P_TERMS - 1, 0, -1):
                        if 3 + (LOG1P_TERMS - 1 - k) // 3 == part:
                            st.then(stt(gg(9), gg(9), 1.0 / (2 * k + 1), gg(8), ALU.add, ALU.mult))
                elif part == 6:
                    st.then(stt(gg(10), gg(9), 1.0, gg(7), ALU.add, ALU.mult))
                    st.then(ts(gg(11), gg(0), 0.0, None, ALU.max))
                    st.then(stt(gg(12), gg(10), 2.0, gg(11), ALU.mult, ALU.add))
                else:
                    st.then(stt(gg(13).rearrange("p (c h) -> p c h", c=CH), gg(12).rearrange("p (c h) -> p c h", c=CH), -1.0,
                                bc(neg_a[:, :].unsqueeze(1), [P, CH, H]), ALU.mult, ALU.mult))
                    ts(g_all[:], gg(13), G_FLOOR, None, ALU.max).then_inc(sm["g_ready"], 1)
                    st.then(ts(gg(14), gg(1), 1.0, None, ALU.add))
                    dve.reciprocal(beta[:], gg(14)).then_inc(sm["egs_ok"], 1)
                    st.close()

            def phase1(b, st, post_st=None):
                if post_st:
                    post_ssx(b - 1)
                for n in range(NU + 2):
                    if 2 <= n < NU:
                        k_squares(b, n)
                    if post_st and n == 2:
                        post_m(b - 1)
                    if n >= 2:
                        m = n - 2
                        dve.wait_ge(*after("rk_ok", b, NU, m))
                        tt(heads(kn[:, m]), heads(k_raw[:, m % 4]),
                           bc(rk[:, m * HG:(m + 1) * HG].unsqueeze(2), [P, HG, P]), ALU.mult).then_inc(sm["kn_ok"], 1)
                    if 1 <= n < NU:
                        gate_steps(b, st, n)
                dve.wait_ge(sm["eg_ok"], b + 1)
                dve.wait_ge(*after("egs_ok", b, 3, 0))
                ts(neg_eg[:], eg[:, 0], -1.0, None, ALU.mult).then_inc(sm["egs_ok"], 1)
                tt(ekb[:], eg[:, 2], beta[:], ALU.mult).then_inc(sm["egs_ok"], 1)
                for n in range(NU):
                    dve.wait_ge(*after("dt_exp", b, NU, n))
                    dve.wait_ge(*after("kk_ps", b, NU, n))
                    for h in range(HG):
                        q, col = n * HG + h, slice(h * P, (h + 1) * P)
                        last = stt(Nm[:, q, :], ps[n % 2][:, col], beta[:, q:q + 1], att[:, n, col], ALU.mult, ALU.mult)
                    last.then_inc(sm["n_ok"], 1)
                    if post_st and n == 1:
                        post_a_stats(b - 1, post_st)
                    if post_st and n == 3:
                        post_a(b - 1)
                if post_st:
                    post_scores(b - 1, post_st)
                    post_probs(b - 1, post_st)

            def eliminate(st):
                upper = lower = st.value()
                for j in range(BLK - 1):
                    ni, ncol = BLK - 1 - j, j + 1
                    halves = [(j + 1, (ni + 1) // 2, 0), (j + 1 + (ni + 1) // 2, ni // 2, HALF_PROD)]
                    products, counts = [], []
                    for i0, n, at in halves:
                        if n:
                            pr = prod[:, at:at + n * ncol].rearrange("p (i c) -> p i c", i=n)
                            dve.wait_ge(st.s, upper if at == 0 else lower)
                            counts.append(st.step(tt(pr, bc(blk_n[:, j, i0:i0 + n].unsqueeze(2), [P, n, ncol]),
                                                     bc(blk_t[:, j, 0:ncol].unsqueeze(1), [P, n, ncol]), ALU.mult)))
                            products.append(pr)
                    for (i0, n, at), pr, count in zip(halves, products, counts):
                        dve.wait_ge(st.s, count)
                        rows_t = blk_t[:, i0:i0 + n, 0:ncol]
                        last = tt(rows_t, rows_t, pr, ALU.subtract)
                        if j == BLK - 2:
                            last.then_inc(sm["t_ok"], 1)
                        elif at == 0:
                            upper = st.step(last)
                        else:
                            lower = st.step(last)
                dve.wait_ge(*after("t_ok", st.b, 2, 0))

            def phase2a(b, post_st=None):
                st = Steps(dve, dchain["inv"], b, INV)
                if not isinstance(b, int):
                    dve.wait_ge(sm["t_stored"], b * 16)
                flat = blk_t[:, :, :].rearrange("p i c -> p (i c)")
                st.then(dve.memset(flat, 0.0))
                st.then(dve.memset(flat[:, 0:BLK * BLK:BLK + 1], 1.0))
                if post_st:
                    post_x2_stats(b - 1, post_st)
                dve.wait_ge(sm["n_back"], b * 16 + 16)
                eliminate(st)
                st.close()
                dve.tensor_copy(blk_tt, blk_t[:, :, :].rearrange("p i c -> p c i")).then_inc(sm["t_ok"], 1)
                for n in range(NU):
                    att_mult(b, n)
                    if post_st and n == 3:
                        post_x2(b - 1)
                if post_st:
                    post_logits(b - 1, post_st)
                    post_choice(b - 1, post_st)
                if not post_st:
                    dve.wait_ge(sm["zeroed"], 3)
                dve.wait_ge(sm["t_back"], b * 16 + 16)
                for r in range(2):
                    dve.tensor_copy(Tm[BLK * r:BLK * r + BLK, :, BLK * r:BLK * r + BLK], Tc[BLK * r:BLK * r + BLK, :, :])
                dve.wait_ge(sm["tt_back"], b * 16 + 16)
                for r in range(NBLK):
                    last = dve.tensor_copy(TT[BLK * r:BLK * r + BLK, :, BLK * r:BLK * r + BLK], TTc[BLK * r:BLK * r + BLK, :, :])
                last.then_inc(sm["td_ok"], 1)
                if post_st:
                    post_slots(b - 1, post_st)
                dve.wait_ge(*after("sq_ps", b, NU, NU - 1))
                ts(cq[:], ps[1][:, 0:NP], 1e-6, 1e-6 * P, ALU.add, ALU.mult).then_inc(sm["cq_ok"], 1)

            def att_mult(b, n):
                dve.wait_ge(*after("qk_ps", b, NU, n))
                for h in range(HG):
                    q, col = n * HG + h, slice(h * P, (h + 1) * P)
                    last = stt(att[:, n, col], ps[4 + n % 4][:, col], beta[:, q:q + 1], att[:, n, col], ALU.mult, ALU.mult)
                last.then_inc(sm["at_ok"], 1)

            def rhs(b, n):
                dve.wait_ge(*after("ks_ps", b, NU - 2, n - 2))
                for h in range(HG):
                    col = slice(h * P, (h + 1) * P)
                    last = stt(vv[:, n, col], ps[1][:, col], neg_eg[:, n * HG + h:n * HG + h + 1], vv[:, n, col],
                               ALU.mult, ALU.add)
                last.then_inc(sm["r_ok"], 1)

            def gate_out(b, n):
                dve.wait_ge(*after("f_ok", b, NU, n))
                dve.wait_ge(*after("gate_ok", b, NU, n))
                for h in range(HG):
                    col = slice(h * P, (h + 1) * P)
                    last = stt(o_sb[:, n % 2, col], o_sb[:, n % 2, col], of[:, n * HG + h:n * HG + h + 1],
                               gate_sb[:, n % 2, col], ALU.mult, ALU.mult)
                last.then_inc(sm["og_ok"], 1)

            def phase2b(b, nxt=None, nxt_st=None):
                dve.wait_ge(*after("egs_ok", b, 3, 2))
                for n in range(NU + 1):
                    c, g = n // GR, n % GR
                    if n >= 1:
                        gate_out(b, n - 1)
                    if GR <= n + 1 < NU:
                        rhs(b, n + 1)
                    if nxt is not None and n == NU - 1:
                        head_h(nxt)
                    if n < NU:
                        dve.wait_ge(*after("au_ps", b, NU, n))
                        if n >= 2:
                            dve.wait_ge(*after("ogT_ps", b, NU, n - 2))
                        if c == 0:
                            dve.tensor_copy(o_sb[:, n % 2], ps[5][:]).then_inc(o_step, 1)
                        else:
                            dve.wait_ge(*after("qc_ok", b, NU - 2, n - 2))
                            for h in range(HG):
                                col = slice(h * P, (h + 1) * P)
                                last = stt(o_sb[:, n % 2, col], o_sb[:, n % 2, col], eg[:, 0, n * HG + h:n * HG + h + 1],
                                           ps[5][:, col], ALU.mult, ALU.add)
                            last.then_inc(o_step, 1)
                        if n < NU - 2:
                            dve.wait_ge(*after("ktu_ps", b, NU - 2, n))
                            if c == 0:
                                dve.tensor_copy(St[:, g], ps[6][:]).then_inc(sm["s_ok"], 1)
                            else:
                                for h in range(HG):
                                    col = slice(h * P, (h + 1) * P)
                                    last = stt(St[:, g, col], St[:, g, col], eg[:, 1, n * HG + h:n * HG + h + 1],
                                               ps[6][:, col], ALU.mult, ALU.add)
                                last.then_inc(sm["s_ok"], 1)
                        dve.wait_ge(o_step, b * NU + n + 1)
                        for h in range(HG):
                            oh = o_sb[:, n % 2, h * P:(h + 1) * P]
                            last = dve.tensor_tensor_reduce(x1[:, h, :], oh, oh, 1.0 / P, cq[:, n * HG + h:n * HG + h + 1],
                                                            ALU.mult, ALU.add, oss[:, n * HG + h:n * HG + h + 1])
                        last.then_inc(sm["o_ok"], 1)
                        if nxt is not None and n == NU - 2:
                            head_ss(nxt)
                if nxt is not None:
                    k_squares(nxt, 0)
                    k_squares(nxt, 1)
                    gate_steps(nxt, nxt_st, 0)
                dve.wait_ge(*after("hp_ps", b, NU, NU - 1))
                dve.wait_ge(sm["x_kept"], b + 1)
                tt(x1[:], xres[:], ps[0][:].rearrange("p (c n) -> p c n", c=CH), ALU.add).then_inc(sm["x1_ok"], 1)

            def norm_stats(st, z, var, v_sem):
                for c in range(CH):
                    last = dve.bn_stats(bn[:, c, :], z[:, c, :])
                st.then(last, plain=True)
                for c in range(CH):
                    last = dve.bn_aggr(mv[:, c, :], bn[:, c, :])
                st.then(last)
                ts(var, mv[:, :, 1], 1e-5, None, ALU.add).then_inc(v_sem, 1)

            def norm_apply(z, rstd, dst, rs_sem, done, b):
                dve.wait_ge(rs_sem, b + 1)
                for c in range(CH):
                    ts(dst[:, c, :], z[:, c, :], mv[:, c, 0:1], rstd[:, c:c + 1], ALU.subtract, ALU.mult).then_inc(done, 1)

            def post_ssx(b):
                dve.wait_ge(sm["x1_ok"], b + 1)
                for c in range(CH):
                    last = dve.tensor_tensor_reduce(a1[:, c, :], x1[:, c, :], x1[:, c, :], 1.0 / D, 1e-6, ALU.mult, ALU.add,
                                                    st4[:, 2, c:c + 1])
                last.then_inc(sm["ssx_ok"], 1)

            def post_m(b):
                dve.wait_ge(sm["r1_ok"], b + 1)
                rows_scale(m_sb, x1, st4[:, 3], sm["m_ok"])

            def post_a_stats(b, st):
                dve.wait_ge(sm["y_ps"], b + 1)
                dve.wait_ge(sm["xx_ok"], b + 1)
                st.then(tt(a1[:], xx[:], ps[2][:].rearrange("p (c n) -> p c n", c=CH), ALU.add))
                norm_stats(st, a1, st4[:, 4], sm["v1_ok"])

            def post_a(b):
                norm_apply(a1, st4[:, 5], a1, sm["rs1_ok"], sm["a_ok"], b)

            def post_scores(b, st):
                sc = soft[:, 0:CH * HK]
                s3 = sc.rearrange("p (n k) -> p n k", k=NK)
                dve.wait_ge(sm["sc_ps"], b + 1)
                st.then(tt(sc, ps[3][:, 0:CH * HK], const[:, C_CNT:C_CNT + CH * HK], ALU.add))
                st.then(dve.tensor_reduce(rt[:, 0], s3, AX.X, ALU.max))
                tt(s3, s3, bc(rt[:, 0].unsqueeze(2), [P, CH * XH, NK]), ALU.subtract).then_inc(sm["sm_ok"], 1)

            def post_probs(b, st):
                s3 = soft[:, 0:CH * HK].rearrange("p (n k) -> p n k", k=NK)
                dve.wait_ge(sm["sexp_ok"], b + 1)
                st.then(dve.tensor_reduce(rt[:, 1], s3, AX.X, ALU.add))
                st.then(dve.reciprocal(rt[:, 2], rt[:, 1]))
                tt(s3, s3, bc(rt[:, 2].unsqueeze(2), [P, CH * XH, NK]), ALU.mult).then_inc(sm["p_ok"], 1)

            def post_x2_stats(b, st):
                dve.wait_ge(sm["xo_ps"], b + 1)
                st.then(tt(a1[:], a1[:], ps[0][:].rearrange("p (c n) -> p c n", c=CH), ALU.add))
                norm_stats(st, a1, st4[:, 6], sm["v2_ok"])

            def post_x2(b):
                norm_apply(a1, st4[:, 7], x2, sm["rs2_ok"], sm["x2_ok"], b)

            ce = lambda i: rt[:, i].rearrange("p (c e) -> p c e", c=CH)

            def post_logits(b, st):
                dve.wait_ge(sm["lg_ps"], b + 1)
                lg = ps[0][:, 0:CH * E].rearrange("p (c e) -> p c e", c=CH)
                st.then(dve.tensor_reduce(rt[:, 2, 0:CH], lg, AX.X, ALU.max))
                tt(ce(0), lg, bc(rt[:, 2, 0:CH].unsqueeze(2), [P, CH, E]), ALU.subtract).then_inc(sm["lsub_ok"], 1)

            def post_choice(b, st):
                dve.wait_ge(sm["lexp_ok"], b + 1)
                st.then(dve.tensor_reduce(rt[:, 3, 0:CH], ce(1), AX.X, ALU.add))
                st.then(dve.reciprocal(rt[:, 3, CH:2 * CH], rt[:, 3, 0:CH]))
                st.then(tt(ce(4), ce(1), bc(rt[:, 3, CH:2 * CH].unsqueeze(2), [P, CH, E]), ALU.mult), plain=True)
                for c in range(CH):
                    last = dve.max(top8[:, c, :], ce(4)[:, c, :])
                st.then(last, plain=True)
                for c in range(CH):
                    last = dve.max_index(top8i[:, c, :], top8[:, c, :], ce(4)[:, c, :])
                st.then(last)
                top_f = rt[:, 3, 0:2 * CH].rearrange("p (k c) -> p k c", k=2)
                st.then(dve.tensor_copy(top_f, top8i[:, :, 0:2].rearrange("p c k -> p k c")))
                for k in range(2):
                    last = tt(ce(5 + k), bc(iota8.unsqueeze(1), [P, CH, E]), bc(top_f[:, k].unsqueeze(2), [P, CH, E]),
                              ALU.is_equal)
                st.then(last)
                tt(rt[:, 7], rt[:, 5], rt[:, 6], ALU.add).then_inc(sm["mask_ok"], 1)

            def post_slots(b, st):
                dve.wait_ge(sm["cum_ps"], b + 1)
                st.then(stt(ce(10), ps[0][:, 64:64 + CH * E].rearrange("p (c e) -> p c e", c=CH), -1.0,
                            bc(base[:, :].unsqueeze(1), [P, CH, E]), ALU.add, ALU.add))
                for k in range(2):
                    last = tt(ce(5 + k), ce(10), ce(5 + k), ALU.mult)
                st.then(last)
                st.then(dve.tensor_reduce(rt[:, 0, 0:E], ps[0][:, 64 + CH * E:64 + 2 * CH * E].rearrange("p (c e) -> p e c", c=CH),
                                          AX.X, ALU.add))
                tt(base[:], base[:], rt[:, 0, 0:E], ALU.add)
                both = lambda i, j: rt[:, i, j * 2 * CH:(j + 1) * 2 * CH]
                st.then(dve.tensor_reduce(both(11, 0), rt[:, 5:7].rearrange("p k (c e) -> p (k c) e", e=E), AX.X, ALU.add))
                pos = both(11, 0)
                ts(both(12, 0), pos, float(CAP), None, ALU.is_lt)
                st.then(ts(both(12, 2), rt[:, 3, 0:2 * CH], float(CAP), None, ALU.mult))
                valid = both(12, 0)
                tt(both(13, 0), pos, both(12, 2), ALU.add)
                st.then(ts(both(13, 1), valid, float(-2 * SLOTS), float(2 * SLOTS), ALU.mult, ALU.add))
                st.then(tt(both(13, 2), both(13, 0), both(13, 1), ALU.add))
                dve.tensor_copy(x2_rows[:, :, GATE:], ce(4))
                dve.tensor_copy(x2_rows[:, :, TOK:TOK + 1], const[:, bass.ds(C_TOK + b * CH, CH)].unsqueeze(2))
                dve.tensor_copy(scat_i[:, :, :].rearrange("p k c -> p (k c)"), both(13, 2)).then_inc(sm["slots_ok"], 1)
                st.close()

            dve.wait_ge(sm["ld_const"], 16)
            dve.tensor_copy(ident_h[:], ident).then_inc(sm["consts_ok"], 1)
            dve.tensor_copy(neg_h[:], const[:, C_NEG:C_NEG + P]).then_inc(sm["consts_ok"], 1)
            dve.wait_ge(sm["base_ok"], 1)
            head_ss(0)
            head_h(0)
            ph1_st = Steps(dve, dchain["ph1"], 0, PH1)
            k_squares(0, 0)
            k_squares(0, 1)
            gate_steps(0, ph1_st, 0)
            phase1(0, ph1_st)
            setup()
            phase2a(0)
            with dve.Fori(1, B) as b:
                post_st = Steps(dve, dchain["post"], b - 1, POST)
                ph1_st = Steps(dve, dchain["ph1"], b, PH1)
                phase2b(b - 1, b, ph1_st)
                phase1(b, ph1_st, post_st)
                phase2a(b, post_st)
                dve.wait_ge(sm["y_st"], b * 16)
                dve.wait_ge(sm["scattered"], b * 2 * CH * 16)
            phase2b(B - 1)
            post_st = Steps(dve, dchain["post"], B - 1, POST)
            post_ssx(B - 1)
            post_m(B - 1)
            post_a_stats(B - 1, post_st)
            post_a(B - 1)
            post_scores(B - 1, post_st)
            post_probs(B - 1, post_st)
            post_x2_stats(B - 1, post_st)
            post_x2(B - 1)
            post_logits(B - 1, post_st)
            post_choice(B - 1, post_st)
            post_slots(B - 1, post_st)

            with dve.Fori(0, E // EG) as ep:
                for a in range(EG):
                    e = ep * EG + a
                    dve.wait_ge(sm[f"e_x_ld{a}"], ep * 32 + 32)
                    dve.wait_ge(sm["e_added"], e + 1)
                    for t, (r0, n) in enumerate(SLOT_TILES):
                        dve.tensor_copy(tok_e[0:n, a, t:t + 1], xe[0:n, a, t, TOK:TOK + 1])
                        last = dve.tensor_copy(wgt_e[0:n, a, t:t + 1], xe[0:n, a, t, bass.ds(e + GATE, 1)])
                    last.then_inc(sm["w_e_ok"], 1)
                    dve.wait_ge(sm["w_e_ok"], e + 1)
                    dve.wait_ge(sm["e_o_ps"], e + 1 + EG)
                    dve.wait_ge(sm["e_added"], e - 1 + EG)
                    for t, (r0, n) in enumerate(SLOT_TILES):
                        last = ts(oe[0:n, a % 2, t, :], ps[5 + a % 2][0:n, t * P:(t + 1) * P], wgt_e[0:n, a, t:t + 1],
                                  None, ALU.mult)
                    last.then_inc(sm["e_o_ok"], 1)

            st = Steps(dve, dchain["fin"], 0, B * 2)
            for i in range(B + 1):
                if i < B:
                    a = i % 2
                    dve.wait_ge(f_x[i], 16)
                    for c in range(CH):
                        last = dve.bn_stats(bn[:, c, :], yf[:, i, c, :])
                    st.then(last, plain=True)
                    for c in range(CH):
                        last = dve.bn_aggr(mvf[:, a, c, :], bn[:, c, :])
                    st.then(last)
                    ts(st4[:, 2 * a], mvf[:, a, :, 1], 1e-5, None, ALU.add).then_inc(sm["f_v"], 1)
                if i >= 1:
                    a = (i - 1) % 2
                    dve.wait_ge(sm["f_rs"], i)
                    for c in range(CH):
                        last = ts(yf[:, i - 1, c, :], yf[:, i - 1, c, :], mvf[:, a, c, 0:1], st4[:, 2 * a + 1, c:c + 1],
                                  ALU.subtract, ALU.mult)
                    last.then_inc(sm["f_y"], 1)
            st.close()


_INS = ["x", "ctx_1024", "L0_attn_Wq", "L0_attn_Wk", "L0_attn_Wv", "L0_attn_Wb", "L0_attn_Wa", "L0_attn_A_log",
        "L0_attn_dt_bias", "L0_attn_Wg", "L0_attn_o_norm_w", "L0_attn_Wo", "L0_attn_W_fc", "L0_attn_W_proj",
        "L0_xattn_in_proj_w", "L0_xattn_in_proj_b", "L0_xattn_out_w", "L0_xattn_out_b", "L0_ffn_router_w",
        "L0_ffn_router_b", "L0_ffn_w1", "L0_ffn_b1", "L0_ffn_w2", "L0_ffn_b2"]


def kernel(**inputs):
    import numpy as _np
    import concourse.bacc as _bacc
    from concourse import mybir as _mybir
    from concourse.bass_utils import run_bass_kernel_spmd as _run

    nc = _bacc.Bacc("TRN2", target_bir_lowering=False, num_devices=1)
    f32 = _mybir.dt.float32
    arrays, args = {}, []
    for name in _INS:
        a = _np.ascontiguousarray(inputs[name])
        arrays[f"in_{name}"] = a
        args.append(nc.dram_tensor(f"in_{name}", a.shape, _mybir.dt.from_np(a.dtype), kind="ExternalInput").ap())
    arrays["shape_table"] = shape_constants()
    args.append(nc.dram_tensor("shape_table", (P, C_END), f32, kind="ExternalInput").ap())
    for name, shape in (("n_blocks", (NP, NBLK, BLK, BLK)), ("t_blocks", (NP, NBLK, BLK, BLK)),
                        ("tt_blocks", (NP, NBLK, BLK, BLK)), ("y_rows", (B * S, D)), ("slots", (SLOTS, ROW))):
        args.append(nc.dram_tensor(name, shape, f32, kind="Internal").ap())
    args.append(nc.dram_tensor("out_0", (B, S, D), f32, kind="ExternalOutput").ap())
    decoder_kernel(nc, *args)
    r = _run(nc, [arrays], core_ids=[0])
    return r.results[0]["out_0"]
```
